# Optimizing a Trainium2 kernel written in Bass

```python
import numpy as np
import jax
import jax.numpy as jnp

def _softmax(x, axis=-1):
    return jax.nn.softmax(x, axis=axis)

def _gelu(x):
    return jax.nn.gelu(x, approximate=True)

def _silu(x):
    return jax.nn.silu(x)

def _sigmoid(x):
    return jax.nn.sigmoid(x)

def _layernorm(x, axis=-1, eps=1e-05):
    m = jnp.mean(x, axis=axis, keepdims=True)
    v = jnp.var(x, axis=axis, keepdims=True)
    return (x - m) / jnp.sqrt(v + eps)

def _scatter_add(tgt, idx, src, axis=0):
    return tgt.at[idx].add(src)

def _segment_sum(src, seg, n):
    return jax.ops.segment_sum(src, seg, n)
kernel_name = 'mk_macaron_d2_jaxref_r8_182807'

def setup_inputs(seed: int=0):
    np.random.seed(seed)
    _w = jnp.asarray

    def _L0_attn_setup():
        import jax, jax.numpy as jnp
        from jax import lax
        import numpy as np
        B, S, D = (4, 256, 128)
        D_INNER, D_STATE, D_CONV = (256, 16, 4)

        def silu(v):
            return v * jax.nn.sigmoid(v)
        key = jax.random.key(seed)
        ks = jax.random.split(key, 7)
        return {'x': jax.random.normal(ks[0], (B, S, D), jnp.float32), 'w_in': jax.random.normal(ks[1], (D, 2 * D_INNER), jnp.float32) * 0.02, 'conv_w': jax.random.normal(ks[2], (D_INNER, 1, D_CONV), jnp.float32) * 0.1, 'conv_b': jax.random.normal(ks[3], (D_INNER,), jnp.float32) * 0.01, 'w_B': jax.random.normal(ks[4], (D_INNER, D_STATE), jnp.float32) * 0.02, 'w_C': jax.random.normal(ks[5], (D_STATE, D_INNER), jnp.float32) * 0.02, 'w_out': jax.random.normal(ks[6], (D_INNER, D), jnp.float32) * 0.02}
    _L0_attn_in = _L0_attn_setup()

    def _L0_ffn_setup():
        import jax, jax.numpy as jnp
        import numpy as np
        B, S, D, E, H, DO = (4, 256, 128, 8, 512, 128)
        TOP_K = 2
        LN_EPS = 1e-05
        key = jax.random.key(seed)
        ks = jax.random.split(key, 9)
        s = 0.02
        return {'x': jax.random.normal(ks[0], (B, S, D), dtype=jnp.float32), 'W1': jax.random.normal(ks[1], (E, D, H), dtype=jnp.float32) * s, 'b1': jnp.zeros((E, H), dtype=jnp.float32), 'W2': jax.random.normal(ks[2], (E, H, DO), dtype=jnp.float32) * s, 'b2': jnp.zeros((E, DO), dtype=jnp.float32), 'gate_W': jax.random.normal(ks[3], (D, E), dtype=jnp.float32) * s, 'shared_W': jax.random.normal(ks[4], (D, DO), dtype=jnp.float32) * s, 'shared_b': jnp.zeros((DO,), dtype=jnp.float32), 'gamma': jnp.ones((DO,), dtype=jnp.float32), 'beta': jnp.zeros((DO,), dtype=jnp.float32)}
    _L0_ffn_in = _L0_ffn_setup()

    def _L1_attn_setup():
        import jax, jax.numpy as jnp
        import numpy as np
        N_HEAD = 8
        HEAD = 64
        RATIO = 2
        DEG = 2
        N_EMBD = 128
        QKV = (RATIO + 2) * N_HEAD * HEAD

        def _rope(t):
            B, T, h, d = t.shape
            div = 2.0 * np.pi / float(T) ** (np.arange(0, d, 2, dtype=np.float32) / d)
            ang = jnp.arange(T, dtype=jnp.float32)[:, None] * jnp.asarray(div)[None, :]
            sin = jnp.repeat(jnp.sin(ang), 2, axis=-1)[None, :, None, :]
            cos = jnp.repeat(jnp.cos(ang), 2, axis=-1)[None, :, None, :]
            x1 = t[..., ::2]
            x2 = t[..., 1::2]
            rot = jnp.stack((-x2, x1), axis=-1).reshape(t.shape)
            return t * cos + rot * sin
        key = jax.random.key(seed)
        k1, k2, k3 = jax.random.split(key, 3)
        B, T = (1, 256)
        x = jax.random.normal(k1, (B, T, N_EMBD), dtype=jnp.float32)
        w_attn = jax.random.normal(k2, (N_EMBD, QKV + N_HEAD), dtype=jnp.float32) * N_EMBD ** (-0.5)
        w_proj = jax.random.normal(k3, (RATIO * N_HEAD * HEAD, N_EMBD), dtype=jnp.float32) * (RATIO * N_HEAD * HEAD) ** (-0.5)
        ln_w = jnp.ones((HEAD,), dtype=jnp.float32)
        return {'x': x, 'w_attn': w_attn, 'w_proj': w_proj, 'ln_w': ln_w}
    _L1_attn_in = _L1_attn_setup()

    def _L1_ffn_setup():
        import math
        import jax, jax.numpy as jnp
        import numpy as np
        NUM_EXPERTS = 8
        CAPACITY_FACTOR = 1.5
        key = jax.random.key(seed)
        ks = jax.random.split(key, 4)
        B, T, D, F, E = (4, 256, 128, 512, NUM_EXPERTS)
        scale = 0.02
        return {'x': jax.random.normal(ks[0], (B, T, D), dtype=jnp.float32), 'router_w': jax.random.normal(ks[1], (E, D), dtype=jnp.float32) * scale, 'w1': jax.random.normal(ks[2], (E, D, F), dtype=jnp.float32) * scale, 'b1': jnp.zeros((E, F), dtype=jnp.float32), 'w2': jax.random.normal(ks[3], (E, F, D), dtype=jnp.float32) * scale, 'b2': jnp.zeros((E, D), dtype=jnp.float32)}
    _L1_ffn_in = _L1_ffn_setup()
    _d = {'L0_attn_x': _L0_attn_in['x'], 'L0_attn_w_in': _L0_attn_in['w_in'], 'L0_attn_conv_w': _L0_attn_in['conv_w'], 'L0_attn_conv_b': _L0_attn_in['conv_b'], 'L0_attn_w_B': _L0_attn_in['w_B'], 'L0_attn_w_C': _L0_attn_in['w_C'], 'L0_attn_w_out': _L0_attn_in['w_out'], 'L0_ffn_W1': _L0_ffn_in['W1'], 'L0_ffn_b1': _L0_ffn_in['b1'], 'L0_ffn_W2': _L0_ffn_in['W2'], 'L0_ffn_b2': _L0_ffn_in['b2'], 'L0_ffn_gate_W': _L0_ffn_in['gate_W'], 'L0_ffn_shared_W': _L0_ffn_in['shared_W'], 'L0_ffn_shared_b': _L0_ffn_in['shared_b'], 'L0_ffn_gamma': _L0_ffn_in['gamma'], 'L0_ffn_beta': _L0_ffn_in['beta'], 'L1_attn_w_attn': _L1_attn_in['w_attn'], 'L1_attn_w_proj': _L1_attn_in['w_proj'], 'L1_attn_ln_w': _L1_attn_in['ln_w'], 'L1_ffn_router_w': _L1_ffn_in['router_w'], 'L1_ffn_w1': _L1_ffn_in['w1'], 'L1_ffn_b1': _L1_ffn_in['b1'], 'L1_ffn_w2': _L1_ffn_in['w2'], 'L1_ffn_b2': _L1_ffn_in['b2']}
    _x0 = _d['L0_attn_x']
    _d['L0_attn_x'] = jax.random.normal(jax.random.fold_in(jax.random.key(seed), 1), (8, 512, 128), dtype=_x0.dtype)
    del _x0
    return _d

def reference(L0_attn_x, L0_attn_w_in, L0_attn_conv_w, L0_attn_conv_b, L0_attn_w_B, L0_attn_w_C, L0_attn_w_out, L0_ffn_W1, L0_ffn_b1, L0_ffn_W2, L0_ffn_b2, L0_ffn_gate_W, L0_ffn_shared_W, L0_ffn_shared_b, L0_ffn_gamma, L0_ffn_beta, L1_attn_w_attn, L1_attn_w_proj, L1_attn_ln_w, L1_ffn_router_w, L1_ffn_w1, L1_ffn_b1, L1_ffn_w2, L1_ffn_b2):

    def _L0_attn_ref(x, w_in, conv_w, conv_b, w_B, w_C, w_out):
        import jax, jax.numpy as jnp
        from jax import lax
        import numpy as np
        B, S, D = (4, 256, 128)
        D_INNER, D_STATE, D_CONV = (256, 16, 4)

        def silu(v):
            return v * jax.nn.sigmoid(v)
        d_inner = conv_w.shape[0]
        d_conv = conv_w.shape[2]
        xz = x @ w_in
        xp, z = jnp.split(xz, 2, axis=-1)
        xc = lax.conv_general_dilated(xp.transpose(0, 2, 1), conv_w, window_strides=(1,), padding=[(d_conv - 1, 0)], dimension_numbers=('NCH', 'OIH', 'NCH'), feature_group_count=d_inner)
        xc = (xc + conv_b[None, :, None]).transpose(0, 2, 1)
        xc = silu(xc)
        h0 = jnp.zeros((xc.shape[0], w_B.shape[1]), xc.dtype)

        def step(h, xt):
            h = h * 0.9 + 0.1 * (xt @ w_B)
            return (h, h @ w_C)
        _, ys = lax.scan(step, h0, xc.transpose(1, 0, 2))
        y = ys.transpose(1, 0, 2) * silu(z)
        return y @ w_out

    def _L0_ffn_ref(x, W1, b1, W2, b2, gate_W, shared_W, shared_b, gamma, beta):
        import jax, jax.numpy as jnp
        import numpy as np
        B, S, D, E, H, DO = (4, 256, 128, 8, 512, 128)
        TOP_K = 2
        LN_EPS = 1e-05
        d = x.shape[-1]
        flat = x.reshape(-1, d)
        n_exp = gate_W.shape[-1]
        probs = jax.nn.softmax(flat @ gate_W, axis=-1)
        topk_w, topk_idx = jax.lax.top_k(probs, TOP_K)
        topk_w = topk_w / topk_w.sum(axis=-1, keepdims=True)
        combine = (jax.nn.one_hot(topk_idx, n_exp, dtype=flat.dtype) * topk_w[..., None]).sum(axis=1)
        out = 0.5 * jax.nn.gelu(flat @ shared_W + shared_b, approximate=False)
        for e in range(n_exp):
            h = jax.nn.gelu(flat @ W1[e] + b1[e], approximate=False)
            out = out + combine[:, e:e + 1] * (h @ W2[e] + b2[e])
        mean = out.mean(axis=-1, keepdims=True)
        var = ((out - mean) ** 2).mean(axis=-1, keepdims=True)
        out = (out - mean) * jax.lax.rsqrt(var + LN_EPS) * gamma + beta
        return out.reshape(*x.shape[:-1], out.shape[-1])

    def _L1_attn_ref(x, w_attn, w_proj, ln_w):
        import jax, jax.numpy as jnp
        import numpy as np
        N_HEAD = 8
        HEAD = 64
        RATIO = 2
        DEG = 2
        N_EMBD = 128
        QKV = (RATIO + 2) * N_HEAD * HEAD

        def _rope(t):
            B, T, h, d = t.shape
            div = 2.0 * np.pi / float(T) ** (np.arange(0, d, 2, dtype=np.float32) / d)
            ang = jnp.arange(T, dtype=jnp.float32)[:, None] * jnp.asarray(div)[None, :]
            sin = jnp.repeat(jnp.sin(ang), 2, axis=-1)[None, :, None, :]
            cos = jnp.repeat(jnp.cos(ang), 2, axis=-1)[None, :, None, :]
            x1 = t[..., ::2]
            x2 = t[..., 1::2]
            rot = jnp.stack((-x2, x1), axis=-1).reshape(t.shape)
            return t * cos + rot * sin
        B, T, C = x.shape
        h, d, r = (N_HEAD, HEAD, RATIO)
        hq = r * h
        qkvg = x @ w_attn
        q = qkvg[..., :hq * d].reshape(B, T, hq, d)
        k = qkvg[..., hq * d:(hq + h) * d].reshape(B, T, h, d)
        v = qkvg[..., (hq + h) * d:QKV].reshape(B, T, h, d)
        log_g = jax.nn.log_sigmoid(6.906768 + qkvg[..., QKV:])
        q = _rope(q)
        k = _rope(k)
        k = jnp.repeat(k, r, axis=2)
        v = jnp.repeat(v, r, axis=2)
        log_G = jnp.repeat(jnp.cumsum(log_g, axis=1), r, axis=2).transpose(0, 2, 1)
        scale = 1.0 / d ** 0.5
        s = jnp.einsum('bthd,bshd->bhts', q, k) * scale
        logits = DEG * jnp.log(jnp.abs(s) + 1e-30) + log_G[:, :, :, None] - log_G[:, :, None, :]
        mask = jnp.tril(jnp.ones((T, T), dtype=bool))
        logits = jnp.where(mask, logits, -jnp.inf)
        m = jax.lax.stop_gradient(jnp.max(logits, axis=-1, keepdims=True))
        a = jnp.exp(logits - m)
        if DEG % 2 == 1:
            a = a * jnp.sign(s)
        a = jnp.where(mask, a, 0.0)
        num = jnp.einsum('bhts,bshd->bthd', a, v)
        den = jnp.sum(a, axis=-1).transpose(0, 2, 1)
        y = num / (den[..., None] + 1e-06)
        mu = jnp.mean(y, axis=-1, keepdims=True)
        var = jnp.mean((y - mu) ** 2, axis=-1, keepdims=True)
        y = (y - mu) / jnp.sqrt(var + 1e-09) * ln_w
        return y.reshape(B, T, hq * d) @ w_proj

    def _L1_ffn_ref(x, router_w, w1, b1, w2, b2):
        import math
        import jax, jax.numpy as jnp
        import numpy as np
        NUM_EXPERTS = 8
        CAPACITY_FACTOR = 1.5
        B, T, D = x.shape
        E = router_w.shape[0]
        N = B * T
        C = max(math.ceil(CAPACITY_FACTOR * N / E), 1)
        x_flat = x.reshape(N, D)
        logits = x_flat @ router_w.T
        probs = jax.nn.softmax(logits, axis=-1)
        chosen_e = jnp.argmax(probs, axis=-1)
        chosen_p = jnp.max(probs, axis=-1)
        onehot = jax.nn.one_hot(chosen_e, E, dtype=jnp.float32)
        pos = jnp.take_along_axis(jnp.cumsum(onehot, axis=0), chosen_e[:, None], axis=1)[:, 0] - 1.0
        pos = pos.astype(jnp.int32)
        kept = pos < C
        pos_c = jnp.clip(pos, 0, C - 1)
        buf = jnp.zeros((E, C, D), dtype=x.dtype).at[chosen_e, pos_c].add(x_flat * kept[:, None].astype(x.dtype))
        h = jax.nn.gelu(jnp.einsum('ecd,edf->ecf', buf, w1) + b1[:, None, :], approximate=False)
        eo = jnp.einsum('ecf,efd->ecd', h, w2) + b2[:, None, :]
        y = eo[chosen_e, pos_c] * (chosen_p * kept.astype(x.dtype))[:, None]
        return y.reshape(B, T, D)
    x = L0_attn_x
    x = x + 0.5 * _L0_ffn_ref(_layernorm(x, axis=-1), L0_ffn_W1, L0_ffn_b1, L0_ffn_W2, L0_ffn_b2, L0_ffn_gate_W, L0_ffn_shared_W, L0_ffn_shared_b, L0_ffn_gamma, L0_ffn_beta)
    x = x + _L0_attn_ref(_layernorm(x, axis=-1), L0_attn_w_in, L0_attn_conv_w, L0_attn_conv_b, L0_attn_w_B, L0_attn_w_C, L0_attn_w_out)
    x = x + 0.5 * _L0_ffn_ref(_layernorm(x, axis=-1), L0_ffn_W1, L0_ffn_b1, L0_ffn_W2, L0_ffn_b2, L0_ffn_gate_W, L0_ffn_shared_W, L0_ffn_shared_b, L0_ffn_gamma, L0_ffn_beta)
    x = x + 0.5 * _L1_ffn_ref(_layernorm(x, axis=-1), L1_ffn_router_w, L1_ffn_w1, L1_ffn_b1, L1_ffn_w2, L1_ffn_b2)
    x = x + _L1_attn_ref(_layernorm(x, axis=-1), L1_attn_w_attn, L1_attn_w_proj, L1_attn_ln_w)
    x = x + 0.5 * _L1_ffn_ref(_layernorm(x, axis=-1), L1_ffn_router_w, L1_ffn_w1, L1_ffn_b1, L1_ffn_w2, L1_ffn_b2)
    return x

_drawn_inputs = setup_inputs


def setup_inputs(seed=0):
    import zlib

    import numpy as np

    out = dict(_drawn_inputs(seed))
    spreads = {'L0_ffn_b1': (0.0, 0.1),
     'L0_ffn_b2': (0.0, 0.1),
     'L0_ffn_shared_b': (0.0, 0.1),
     'L0_ffn_gamma': (1.0, 0.2),
     'L0_ffn_beta': (0.0, 0.1),
     'L1_attn_ln_w': (1.0, 0.2),
     'L1_ffn_b1': (0.0, 0.8),
     'L1_ffn_b2': (0.0, 0.8)}
    factors = {'L0_attn_w_in': 8.0,
     'L0_attn_conv_w': 8.0,
     'L0_attn_conv_b': 8.0,
     'L0_attn_w_B': 8.0,
     'L0_attn_w_C': 8.0,
     'L0_attn_w_out': 8.0,
     'L1_ffn_router_w': 6.651,
     'L1_ffn_w1': 8.0,
     'L1_ffn_w2': 8.0}
    for name, (base, spread) in spreads.items():
        noise = np.random.default_rng([zlib.crc32(name.encode()), seed]).standard_normal(out[name].shape)
        drawn = base * np.exp(spread * noise) if base else spread * noise
        out[name] = jnp.asarray(drawn.astype(out[name].dtype))
    for name, factor in factors.items():
        out[name] = (out[name] * factor).astype(out[name].dtype)
    return out
```

```python
from contextlib import ExitStack

import concourse.bass as bass
from concourse import mybir
import numpy as np

F32 = mybir.dt.float32
BF16 = mybir.dt.bfloat16
I32 = mybir.dt.int32
ALU = mybir.AluOpType
ACT = mybir.ActivationFunctionType
AX = mybir.AxisListType

P = 128
B, S, D = 8, 512, 128
N = B * S
NT = N // P
TB = S // P
E = 8
H = 512
HC = H // P
TOP_K = 2
CAPACITY = -(-3 * N // (2 * E))
LN_EPS = 1e-5

W1_AT, W2_AT, B2_AT, B1_AT = 0, H, H + HC * D, H + HC * D + D
EXPERT_W = B1_AT + HC

RING = 4


def ring_multiple(tiles):
    return -(-tiles // RING) * RING


SLOT_TILES_L0 = ring_multiple((TOP_K * N + E * (P - 1)) // P)
SLOT_TILES_L1 = ring_multiple((N + E * (P - 1)) // P)
FAR_AWAY = 1.0e6

DI, DS, DC = 256, 16, 4
IC = DI // P
KEEP, TAKE = 0.9, 0.1

KV, HD, RATIO = 8, 64, 2
QW, KW = RATIO * HD, HD
GROUP_W = QW + KW + HD
ROPE_W = QW + KW
GATE_BIAS = 6.906768
SCORE_SCALE = 2.0 ** 40
SCORE_MIN = 1e-30
DEN_EPS, HEAD_EPS = 1e-6, 1e-9
MASKED = -1.0e30
PAIRS = [(i, j) for i in range(TB) for j in range(i, TB)]
SCORE_AT = {0: 0, 1: S, 3: S + 3 * P, 2: 2 * S}
SCORE_W = 2 * S + 2 * P


def block_at(i, j):
    return SCORE_AT[i] + (j - i) * P


class Chain:

    def __init__(self, engine, sem):
        self.engine, self.sem, self.n = engine, sem, 0

    def __call__(self, instruction):
        self.n += 1
        instruction.then_inc(self.sem, 1)
        self.engine.wait_ge(self.sem, self.n)

    def in_loop(self, instruction, trip, step, steps):
        instruction.then_inc(self.sem, 1)
        self.engine.wait_ge(self.sem, trip * steps + (self.n + step + 1))

    def loop_done(self, trips, steps):
        self.n += trips * steps


def flat(ap):
    return ap.rearrange("p a n -> p (a n)")


class Net:

    def __init__(self, nc, ctx, dram):
        self.nc, self.dram = nc, dram
        self.ctx = ctx
        self.counting = []
        sb = self.sbuf
        self.x = sb("stream", [P, NT, D])
        self.ident = sb("ident", [P, P])
        self.mean = sb("mean", [P, NT])
        self.rstd = sb("rstd", [P, NT])
        self.stats = sb("stats", [P, NT, 6])
        self.ln_tmp = sb("ln_tmp", [P, 4, NT])
        self.eps = sb("eps", [P, 1])
        self.gathered = [self.sem(f"gathered{u}", ctx) for u in range(RING)]
        self.scattered = [self.sem(f"scattered{u}", ctx) for u in range(RING)]
        self.laps = 0
        self.xn_rows = nc.dram_tensor("xn_rows", (N, D), F32, kind="Internal").ap()
        self.y_rows = nc.dram_tensor("y_rows", (TOP_K * N, D), F32, kind="Internal").ap()

    def sbuf(self, name, shape, dtype=F32, ctx=None):
        return (ctx or self.ctx).enter_context(self.nc.sbuf_tensor(name, shape, dtype))

    def psum(self, name, shape, ctx):
        return ctx.enter_context(self.nc.psum_tensor(name, shape, F32))

    def sem(self, name, ctx):
        if not any(ctx is c for c, _ in self.counting):
            numbers = []
            self.counting.append((ctx, numbers))
            ctx.callback(self.zero, numbers)
        handle = ctx.enter_context(self.nc.semaphore(name))
        [numbers for c, numbers in self.counting if c is ctx][0].append(handle.num)
        return handle

    def zero(self, numbers):
        self.counting.pop()
        with self.nc.Block() as block:
            @block.sync
            def _(sp):
                left = sorted(numbers)
                while left:
                    n = next((k for k in range(len(left)) if left[k] != left[0] + k), len(left))
                    sp.sem_clear(range(left[0], left[0] + n))
                    left = left[n:]


def load_inputs(net, ctx):
    nc = net.nc
    loaded, made = net.sem("x_loaded", ctx), net.sem("ident_made", ctx)
    with nc.Block() as block:
        @block.sync
        def _(sp):
            sp.dma_start(net.x[:, :, :], net.dram["x"].rearrange("(t p) d -> p t d", p=P)).then_inc(loaded, 16)
            sp.wait_ge(loaded, 16)

        @block.gpsimd
        def _(pool):
            pool.memset(net.eps[:, :], LN_EPS)
            pool.memset(net.ident[:, :], 0.0).then_inc(made, 1)
            pool.wait_ge(made, 1)
            pool.affine_select(out=net.ident[:, :], in_=net.ident[:, :], compare_op=ALU.not_equal, fill=1.0,
                               base=0, pattern=[[-1, P]], channel_multiplier=1).then_inc(made, 1)


def layer_norm_stats(net, name, src):
    nc = net.nc
    with ExitStack() as ctx:
        step = net.sem(f"{name}_ln_step", ctx)
        var_ready = net.sem(f"{name}_var_ready", ctx)
        std_ready = net.sem(f"{name}_std_ready", ctx)
        var, std, diff, half = (net.ln_tmp[:, k, :] for k in range(4))
        with nc.Block() as block:
            @block.vector
            def _(dve):
                link = Chain(dve, step)
                with dve.Fori(0, NT) as t:
                    dve.bn_stats(flat(net.stats[:, bass.ds(t, 1), :]), flat(src[:, bass.ds(t, 1), :])).then_inc(step, 1)
                link.loop_done(NT, 1)
                dve.wait_ge(step, link.n)
                even, odd = net.stats[:, :, 1], net.stats[:, :, 4]
                link(dve.tensor_tensor(half, even, odd, ALU.add))
                link(dve.tensor_scalar(net.mean[:, :], half, 0.5, None, ALU.mult))
                link(dve.tensor_tensor(diff, even, odd, ALU.subtract))
                link(dve.tensor_tensor(diff, diff, diff, ALU.mult))
                link(dve.tensor_tensor(var, net.stats[:, :, 2], net.stats[:, :, 5], ALU.add))
                link(dve.tensor_scalar(diff, diff, 0.25, None, ALU.mult))
                dve.scalar_tensor_tensor(out=var, in0=var, scalar=1.0 / D, in1=diff,
                                         op0=ALU.mult, op1=ALU.add).then_inc(var_ready, 1)
                dve.wait_ge(std_ready, 1)
                dve.reciprocal(net.rstd[:, :], std).then_inc(step, 1)

            @block.scalar
            def _(act):
                act.wait_ge(var_ready, 1)
                act.activation(std, var, ACT.Sqrt, bias=net.eps[:, 0:1]).then_inc(std_ready, 1)


def mixture(net, name, layer, experts):
    nc, dram = net.nc, net.dram
    two = layer == 0
    choices = TOP_K if two else 1
    tiles = SLOT_TILES_L0 if two else SLOT_TILES_L1
    cols = choices * NT
    rw = D + E if two else E
    pre = f"l{layer}"
    layer_norm_stats(net, name, net.x)
    with ExitStack() as ctx:
        sb = lambda n, s, d=F32: net.sbuf(f"{name}_{n}", s, d, ctx)
        shared_w = sb("shared_w", [P, rw])
        shared_b = sb("shared_b", [P, rw])
        pre_sh = sb("pre_sh", [P, NT, rw])
        weight = sb("weight", [P, TOP_K, NT])
        row_of = sb("row_of", [P, tiles], I32)
        back_of = sb("back_of", [P, tiles], I32)
        tile_expert = sb("tile_expert", [1, tiles], I32)

        with ExitStack() as c1:
            xn = [sb(f"xn{u}", [P, D]) for u in range(2)]
            xt = [sb(f"xt{u}", [P, P]) for u in range(2)]
            t_ps = [net.psum(f"{name}_t_ps{u}", [P, 512], c1) for u in range(2)]
            r_ps = [net.psum(f"{name}_r_ps{u}", [P, 512], c1) for u in range(2)]
            w_loaded = net.sem(f"{name}_w_loaded", c1)
            xn_ready = net.sem(f"{name}_xn_ready", c1)
            xn_turned = net.sem(f"{name}_xn_turned", c1)
            xn_stored = [net.sem(f"{name}_xn_stored{u}", c1) for u in range(2)]
            xt_ready = net.sem(f"{name}_xt_ready", c1)
            routed = net.sem(f"{name}_routed", c1)
            pre_kept = net.sem(f"{name}_pre_kept", c1)
            with nc.Block() as block:
                @block.scalar
                def _(act):
                    act.dma_start(shared_w[:, :], dram[f"{pre}_shared_w"]).then_inc(w_loaded, 16)
                    act.dma_start(shared_b[:, :], dram[f"{pre}_shared_b"]).then_inc(w_loaded, 16)
                    with act.Fori(0, NT // 2) as k:
                        for u in range(2):
                            t = k * 2 + u
                            act.wait_ge(xn_turned, t + 1)
                            act.wait_ge(routed, t + 1)
                            act.activation(xt[u][:, :], t_ps[u][:, 0:P], ACT.Copy).then_inc(xt_ready, 1)

                @block.vector
                def _(dve):
                    dve.wait_ge(w_loaded, 32)
                    with dve.Fori(0, NT // 2) as k:
                        for u in range(2):
                            t = k * 2 + u
                            dve.wait_ge(xn_stored[u], 16 * k)
                            dve.wait_ge(xt_ready, t)
                            dve.tensor_scalar(xn[u][:, :], flat(net.x[:, bass.ds(t, 1), :]),
                                              net.mean[:, bass.ds(t, 1)], net.rstd[:, bass.ds(t, 1)],
                                              ALU.subtract, ALU.mult).then_inc(xn_ready, 1)
                            dve.wait_ge(routed, t + 3)
                            dve.tensor_tensor(flat(pre_sh[:, bass.ds(t, 1), :]), r_ps[u][:, 0:rw],
                                              shared_b[:, :], ALU.add).then_inc(pre_kept, 1)

                @block.sync
                def _(sp):
                    with sp.Fori(0, NT // 2) as k:
                        for u in range(2):
                            t = k * 2 + u
                            sp.wait_ge(xn_ready, t + 1)
                            sp.dma_start(net.xn_rows[bass.ds(t * P, P), :], xn[u][:, :]).then_inc(xn_stored[u], 16)
                    for u in range(2):
                        sp.wait_ge(xn_stored[u], 16 * (NT // 2))

                @block.tensor
                def _(pe):
                    pe.sem_inc(routed, 2)
                    pe.wait_ge(w_loaded, 32)
                    with pe.Fori(0, NT // 2) as k:
                        for u in range(2):
                            t = k * 2 + u
                            pe.wait_ge(xn_ready, t + 1)
                            pe.transpose(t_ps[u][:, 0:P], xn[u][:, :], net.ident[:, :]).then_inc(xn_turned, 1)
                            pe.wait_ge(xt_ready, t + 1)
                            pe.matmul(r_ps[u][:, 0:rw], xt[u][:, :], shared_w[:, :],
                                      start=True, stop=True).then_inc(routed, 1)

        route(net, name, layer, choices, tiles, cols, rw, pre_sh, weight, row_of, back_of, tile_expert)
        expert_tiles(net, name, tiles, experts, row_of, back_of, tile_expert)
        combine(net, name, layer, choices, rw, pre_sh, weight)


def route(net, name, layer, choices, tiles, cols, rw, pre_sh, weight, row_of, back_of, tile_expert):
    nc = net.nc
    two = layer == 0
    G = 16
    with ExitStack() as ctx:
        sb = lambda n, s, d=F32: net.sbuf(f"{name}_{n}", s, d, ctx)
        sem = lambda n: net.sem(f"{name}_{n}", ctx)
        before = sb("before", [P, P])
        ones = sb("ones", [P, P])
        preference = sb("preference", [P, E])
        column = sb("column", [P, P])
        token_id = sb("token_id", [P, cols])
        not_first = sb("not_first", [P, E, NT])
        big = sb("big", [P, NT, E])
        prob = sb("prob", [P, NT, E])
        pick = [sb(f"pick{c}", [P, NT, E]) for c in range(2)]
        chosen = sb("chosen", [P, NT, E])
        best = [sb(f"best{c}", [P, NT]) for c in range(2)]
        row = sb("row", [P, NT])
        by_expert = sb("by_expert", [P, E, NT])
        so_far = sb("so_far", [P, E, NT])
        rank = sb("rank", [P, NT, E])
        counts = sb("counts", [P, 4, E])
        counts_i = sb("counts_i", [P, E], I32)
        slot = sb("slot", [P, choices, NT])
        slot_i = sb("slot_i", [P, 2, cols], I32)
        hi_lo = sb("hi_lo", [P, 2, cols])
        lo_hot = [sb(f"lo_hot{u}", [P, G, P]) for u in range(2)]
        hi_hot = [sb(f"hi_hot{u}", [P, G, tiles]) for u in range(2)]
        ends = sb("ends", [P, tiles, E])
        table = sb("table", [P, 4, tiles])
        cnt_ps = net.psum(f"{name}_cnt_ps", [P, 2, NT * E], ctx)
        tab_ps = net.psum(f"{name}_tab_ps", [P, 512], ctx)
        made, step, exps_ready, logits_ready = sem("r_made"), sem("r_step"), sem("r_exps"), sem("r_logits")
        chosen_ready, counted, hots_ready, hots_used = sem("r_chosen"), sem("r_counted"), sem("r_hots"), sem("r_used")

        with nc.Block() as block:
            @block.gpsimd
            def _(pool):
                link = Chain(pool, made)
                link(pool.memset(ones[:, :], 1.0))
                link(pool.memset(not_first[:, :, :], 1.0))
                link(pool.memset(not_first[:, :, 0:1], 0.0))
                link(pool.affine_select(out=before[:, :], in_=ones[:, :], compare_op=ALU.is_gt, fill=0.0,
                                        base=0, pattern=[[1, P]], channel_multiplier=-1))
                link(pool.iota(column[:, :], [[1, P]], base=0, channel_multiplier=0,
                               allow_small_or_imprecise_dtypes=True))
                link(pool.iota(preference[:, :], [[-1, E]], base=E, channel_multiplier=0,
                               allow_small_or_imprecise_dtypes=True))
                link(pool.iota(token_id[:, :], [[P, cols]], base=1, channel_multiplier=1,
                               allow_small_or_imprecise_dtypes=True))

            @block.scalar
            def _(act):
                act.wait_ge(logits_ready, 1)
                act.activation(prob[:, :, :], prob[:, :, :], ACT.Exp).then_inc(exps_ready, 1)

            @block.tensor
            def _(pe):
                pe.wait_ge(made, 7)
                pe.wait_ge(chosen_ready, 1)
                hits = chosen[:, :, :].rearrange("p t e -> p (t e)")
                pe.matmul(cnt_ps[:, 0, :], before[:, :], hits, start=True, stop=True)
                pe.matmul(cnt_ps[:, 1, :], ones[:, :], hits, start=True, stop=True,
                          skip_group_check=True).then_inc(counted, 1)
                for r in range(cols // G):
                    pe.wait_ge(hots_ready, r + 1)
                    for g in range(G):
                        last = pe.matmul(tab_ps[:, 0:tiles], lo_hot[r % 2][:, g, :], hi_hot[r % 2][:, g, :],
                                         start=r == 0 and g == 0, stop=r == cols // G - 1 and g == G - 1)
                    last.then_inc(hots_used, 1)

            @block.vector
            def _(dve):
                link = Chain(dve, step)
                dve.wait_ge(made, 7)
                logits = pre_sh[:, :, rw - E:rw]
                over_e = lambda a: a.unsqueeze(2).broadcast_to([P, NT, E])
                link(dve.tensor_reduce(row[:, :], logits, AX.X, ALU.max))
                dve.tensor_tensor(prob[:, :, :], logits, over_e(row[:, :]), ALU.subtract).then_inc(logits_ready, 1)
                dve.wait_ge(exps_ready, 1)
                link(dve.tensor_reduce(row[:, :], prob[:, :, :], AX.X, ALU.add))
                link(dve.reciprocal(row[:, :], row[:, :]))
                link(dve.tensor_tensor(prob[:, :, :], prob[:, :, :], over_e(row[:, :]), ALU.mult))
                prefer = preference[:, :].unsqueeze(1).broadcast_to([P, NT, E])
                for c in range(choices):
                    link(dve.tensor_reduce(best[c][:, :], prob[:, :, :], AX.X, ALU.max))
                    link(dve.tensor_tensor(big[:, :, :], prob[:, :, :], over_e(best[c][:, :]), ALU.is_equal))
                    link(dve.tensor_tensor(big[:, :, :], big[:, :, :], prefer, ALU.mult))
                    link(dve.tensor_reduce(row[:, :], big[:, :, :], AX.X, ALU.max))
                    link(dve.tensor_tensor(pick[c][:, :, :], big[:, :, :], over_e(row[:, :]), ALU.is_equal))
                    if c + 1 < choices:
                        link(dve.scalar_tensor_tensor(out=prob[:, :, :], in0=pick[c][:, :, :], scalar=-2.0,
                                                      in1=prob[:, :, :], op0=ALU.mult, op1=ALU.add))
                if two:
                    link(dve.tensor_tensor(chosen[:, :, :], pick[0][:, :, :], pick[1][:, :, :], ALU.add))
                else:
                    link(dve.tensor_copy(chosen[:, :, :], pick[0][:, :, :]))
                dve.sem_inc(chosen_ready, 1)
                if two:
                    link(dve.tensor_tensor(row[:, :], best[0][:, :], best[1][:, :], ALU.add))
                    link(dve.reciprocal(row[:, :], row[:, :]))
                    for c in range(2):
                        link(dve.tensor_tensor(weight[:, c, :], best[c][:, :], row[:, :], ALU.mult))
                dve.wait_ge(counted, 1)
                totals = cnt_ps[:, 1, :].rearrange("p (t e) -> p e t", e=E)
                link(dve.tensor_copy(by_expert[:, :, :], totals))
                link(dve.tensor_tensor_scan(so_far[:, :, :].rearrange("p e t -> p (e t)"),
                                            not_first[:, :, :].rearrange("p e t -> p (e t)"),
                                            by_expert[:, :, :].rearrange("p e t -> p (e t)"), 0.0,
                                            ALU.mult, ALU.add))
                link(dve.tensor_copy(counts[:, 0, :], so_far[:, :, NT - 1]))
                link(dve.tensor_tensor(so_far[:, :, :], so_far[:, :, :], by_expert[:, :, :], ALU.subtract))
                link(dve.tensor_tensor(rank[:, :, :], cnt_ps[:, 0, :].rearrange("p (t e) -> p t e", e=E),
                                       so_far[:, :, :].rearrange("p e t -> p t e"), ALU.add))
                if not two:
                    link(dve.tensor_scalar(counts[:, 0, :], counts[:, 0, :], float(CAPACITY), None, ALU.min))
                link(dve.tensor_scalar(counts_i[:, :], counts[:, 0, :], float(P - 1), None, ALU.add))
                link(dve.tensor_scalar(counts_i[:, :], counts_i[:, :], 7, None, ALU.arith_shift_right))
                link(dve.tensor_copy(counts[:, 1, :], counts_i[:, :]))
                link(dve.tensor_tensor_scan(counts[:, 2, :], ones[:, 0:E], counts[:, 1, :], 0.0, ALU.mult, ALU.add))
                link(dve.tensor_tensor(counts[:, 3, :], counts[:, 2, :], counts[:, 1, :], ALU.subtract))
                link(dve.tensor_scalar(counts[:, 3, :], counts[:, 3, :], float(P), None, ALU.mult))
                if not two:
                    link(dve.tensor_tensor(big[:, :, :], rank[:, :, :], pick[0][:, :, :], ALU.mult))
                    link(dve.tensor_reduce(row[:, :], big[:, :, :], AX.X, ALU.add))
                    link(dve.tensor_scalar(weight[:, 1, :], row[:, :], float(CAPACITY), None, ALU.is_lt))
                    link(dve.tensor_tensor(weight[:, 0, :], weight[:, 1, :], best[0][:, :], ALU.mult))
                    link(dve.tensor_scalar(weight[:, 0, :], weight[:, 0, :], 0.5, None, ALU.mult))
                    link(dve.tensor_scalar(weight[:, 1, :], weight[:, 1, :], -FAR_AWAY, FAR_AWAY, ALU.mult, ALU.add))
                link(dve.tensor_tensor(rank[:, :, :], rank[:, :, :],
                                       counts[:, 3, :].unsqueeze(1).broadcast_to([P, NT, E]), ALU.add))
                for c in range(choices):
                    link(dve.tensor_tensor(big[:, :, :], rank[:, :, :], pick[c][:, :, :], ALU.mult))
                    link(dve.tensor_reduce(slot[:, c, :], big[:, :, :], AX.X, ALU.add))
                if not two:
                    link(dve.tensor_tensor(slot[:, 0, :], slot[:, 0, :], weight[:, 1, :], ALU.add))
                flat_slot = slot[:, :, :].rearrange("p c t -> p (c t)")
                link(dve.tensor_copy(slot_i[:, 0, :], flat_slot))
                link(dve.tensor_scalar(slot_i[:, 1, :], slot_i[:, 0, :], P - 1, None, ALU.bitwise_and))
                link(dve.tensor_scalar(slot_i[:, 0, :], slot_i[:, 0, :], 7, None, ALU.arith_shift_right))
                link(dve.tensor_copy(hi_lo[:, :, :], slot_i[:, :, :]))
                for r in range(cols // G):
                    if r >= 2:
                        dve.wait_ge(hots_used, r - 1)
                    at = slice(r * G, (r + 1) * G)
                    lo = hi_lo[:, 1, at].unsqueeze(2).broadcast_to([P, G, P])
                    hi = hi_lo[:, 0, at].unsqueeze(2).broadcast_to([P, G, tiles])
                    ids = token_id[:, at].unsqueeze(2).broadcast_to([P, G, tiles])
                    link(dve.tensor_tensor(lo_hot[r % 2][:, :, :], column[:, :].unsqueeze(1).broadcast_to([P, G, P]),
                                           lo, ALU.is_equal))
                    link(dve.tensor_tensor(hi_hot[r % 2][:, :, :],
                                           column[:, 0:tiles].unsqueeze(1).broadcast_to([P, G, tiles]), hi, ALU.is_equal))
                    dve.tensor_tensor(hi_hot[r % 2][:, :, :], hi_hot[r % 2][:, :, :], ids,
                                      ALU.mult).then_inc(hots_ready, 1)
                link(dve.tensor_tensor(ends[:, :, :], column[:, 0:tiles].unsqueeze(2).broadcast_to([P, tiles, E]),
                                       counts[:, 2, :].unsqueeze(1).broadcast_to([P, tiles, E]), ALU.is_ge))
                link(dve.tensor_reduce(table[:, 0, :], ends[:, :, :], AX.X, ALU.add))
                link(dve.tensor_scalar(tile_expert[:, :], table[0:1, 0, :], float(E - 1), None, ALU.min))
                dve.wait_ge(hots_used, cols // G)
                full = table[:, 1, :]
                link(dve.tensor_scalar(full, tab_ps[:, 0:tiles], 1.0, None, ALU.subtract))
                link(dve.tensor_scalar(table[:, 2, :], full, 0.0, 1.0e6, ALU.is_lt, ALU.mult))
                link(dve.tensor_tensor(back_of[:, :], full, table[:, 2, :], ALU.add))
                link(dve.tensor_scalar(table[:, 2, :], full, float(N), float(-N), ALU.is_ge, ALU.mult))
                link(dve.tensor_tensor(table[:, 3, :], full, table[:, 2, :], ALU.add))
                link(dve.tensor_scalar(row_of[:, :], table[:, 3, :], 0.0, None, ALU.max))


def expert_tiles(net, name, tiles, experts, row_of, back_of, tile_expert):
    nc = net.nc
    R = RING
    trips = tiles // R
    with ExitStack() as ctx:
        sb = lambda n, s, d=F32: net.sbuf(f"{name}_{n}", s, d, ctx)
        sem = lambda n: net.sem(f"{name}_{n}", ctx)
        xg = [sb(f"xg{u}", [P, D]) for u in range(R)]
        xg_t = [sb(f"xg_t{u}", [P, P]) for u in range(2)]
        wb = [sb(f"wb{u}", [P, EXPERT_W]) for u in range(2)]
        hid = [sb(f"hid{u}", [P, HC, P]) for u in range(2)]
        ys = [sb(f"ys{u}", [P, D]) for u in range(R)]
        row_ix = [sb(f"row_ix{u}", [P, 1], I32) for u in range(R)]
        back_ix = [sb(f"back_ix{u}", [P, 1], I32) for u in range(R)]
        t_ps = [net.psum(f"{name}_gt_ps{u}", [P, 512], ctx) for u in range(2)]
        h_ps = [net.psum(f"{name}_h_ps{u}", [P, HC, P], ctx) for u in range(2)]
        y_ps = [net.psum(f"{name}_y_ps{u}", [P, 512], ctx) for u in range(2)]
        gathered, scattered, past = net.gathered, net.scattered, 16 * net.laps
        net.laps += trips
        row_ix_ready, back_ix_ready = sem("row_ix_ready"), sem("back_ix_ready")
        passed = sem("passed")
        turned, xt_ready, w_ready, h_ready = sem("turned"), sem("gxt_ready"), sem("w_ready"), sem("h_ready")
        act_ready, y_ready, y_kept = sem("act_ready"), sem("y_ready"), sem("y_kept")
        with nc.Block() as block:
            @block.gpsimd
            def _(pool):
                def gather(u):
                    pool.indirect_dma_start(xg[u][:, :], None, net.xn_rows,
                                            bass.IndirectOffsetOnAxis(ap=row_ix[u][:, :], axis=0)
                                            ).then_inc(gathered[u], 16)

                for u in range(R):
                    pool.tensor_copy(row_ix[u][:, :], row_of[:, u:u + 1]).then_inc(row_ix_ready, 1)
                for u in range(R):
                    pool.wait_ge(row_ix_ready, u + 1)
                    gather(u)

                def scatter(u):
                    pool.indirect_dma_start(net.y_rows, bass.IndirectOffsetOnAxis(ap=back_ix[u][:, :], axis=0),
                                            ys[u][:, :], None, bounds_check=TOP_K * N - 1, oob_is_err=False
                                            ).then_inc(scattered[u], 16)

                def until(sem, count):
                    pool.wait_ge(sem, count)
                    pool.sem_inc(passed, 1)

                with pool.Fori(0, trips - 1) as k:
                    for u in range(R):
                        j = k * R + u
                        until(turned, j + 1)
                        pool.tensor_copy(row_ix[u][:, :], row_of[:, bass.ds(j + R, 1)]).then_inc(row_ix_ready, 1)
                        until(scattered[u], 16 * k + past)
                        pool.tensor_copy(back_ix[u][:, :], back_of[:, bass.ds(j, 1)]).then_inc(back_ix_ready, 1)
                        until(row_ix_ready, j + (R + 1))
                        gather(u)
                        until(back_ix_ready, j + 1)
                        until(y_kept, j + 1)
                        scatter(u)
                for u in range(R):
                    j = tiles - R + u
                    until(scattered[u], 16 * (trips - 1) + past)
                    pool.tensor_copy(back_ix[u][:, :], back_of[:, j:j + 1]).then_inc(back_ix_ready, 1)
                    until(back_ix_ready, j + 1)
                    until(y_kept, j + 1)
                    scatter(u)
                for u in range(R):
                    pool.wait_ge(scattered[u], 16 * trips + past)

            @block.vector
            def _(dve):
                def weights(j, u):
                    e = dve.value_load(tile_expert[0:1, bass.ds(j, 1)], min_val=0, max_val=E - 1)
                    dve.tensor_copy(wb[u][:, :], flat(experts[:, bass.ds(e, 1), :])).then_inc(w_ready, 1)

                def keep(j, u, r):
                    dve.wait_ge(y_ready, j + 1)
                    dve.wait_ge(scattered[r], 16 * (j // R) + past)
                    dve.tensor_tensor(ys[r][:, :], y_ps[u][:, 0:D], wb[u][:, B2_AT:B2_AT + D],
                                      ALU.add).then_inc(y_kept, 1)

                weights(0, 0)
                weights(1, 1)
                with dve.Fori(0, trips - 1) as k:
                    for r in range(R):
                        j = k * R + r
                        dve.wait_ge(y_ready, j + 1)
                        dve.wait_ge(scattered[r], 16 * k + past)
                        dve.tensor_tensor(ys[r][:, :], y_ps[r % 2][:, 0:D], wb[r % 2][:, B2_AT:B2_AT + D],
                                          ALU.add).then_inc(y_kept, 1)
                        dve.wait_ge(y_kept, j + 1)
                        weights(j + 2, r % 2)
                for j in range(tiles - R, tiles):
                    keep(j, j % 2, j % R)
                    if j + 2 < tiles:
                        dve.wait_ge(y_kept, j + 1)
                        weights(j + 2, j % 2)

            @block.scalar
            def _(act):
                def turn_copy(j, u):
                    act.wait_ge(turned, j + 1)
                    act.activation(xg_t[u][:, :], t_ps[u][:, 0:P], ACT.Copy).then_inc(xt_ready, 1)

                def gelu(j, u):
                    act.wait_ge(h_ready, j + 1)
                    for k in range(HC):
                        last = act.activation(hid[u][:, k, :], h_ps[u][:, k, :], ACT.Gelu,
                                              bias=wb[u][:, B1_AT + k:B1_AT + k + 1])
                    last.then_inc(act_ready, 1)

                turn_copy(0, 0)
                turn_copy(1, 1)
                gelu(0, 0)
                with act.Fori(0, trips - 1) as t:
                    for r in range(R):
                        j = t * R + r
                        turn_copy(j + 2, r % 2)
                        act.wait_ge(y_ready, j)
                        gelu(j + 1, (r + 1) % 2)
                for j in range(tiles - R, tiles - 1):
                    if j + 2 < tiles:
                        turn_copy(j + 2, j % 2)
                    act.wait_ge(y_ready, j)
                    gelu(j + 1, (j + 1) % 2)

            @block.tensor
            def _(pe):
                def turn(lap, j, r):
                    pe.wait_ge(gathered[r], 16 * lap + (16 + past))
                    pe.transpose(t_ps[r % 2][:, 0:P], xg[r][:, :], net.ident[:, :]).then_inc(turned, 1)

                def hidden(j, u):
                    pe.wait_ge(xt_ready, j + 1)
                    pe.wait_ge(w_ready, j + 1)
                    for k in range(HC):
                        last = pe.matmul(h_ps[u][:, k, :], wb[u][:, k * P:(k + 1) * P], xg_t[u][:, :],
                                         start=True, stop=True, skip_group_check=True)
                    last.then_inc(h_ready, 1)

                def output(j, u):
                    pe.wait_ge(act_ready, j + 1)
                    for k in range(HC):
                        last = pe.matmul(y_ps[u][:, 0:D], hid[u][:, k, :], wb[u][:, W2_AT + k * D:W2_AT + (k + 1) * D],
                                         start=k == 0, stop=k == HC - 1)
                    last.then_inc(y_ready, 1)

                turn(0, 0, 0)
                turn(0, 1, 1)
                hidden(0, 0)
                with pe.Fori(0, trips - 1) as t:
                    for r in range(R):
                        j = t * R + r
                        turn(t + (r + 2) // R, j + 2, (r + 2) % R)
                        hidden(j + 1, (r + 1) % 2)
                        pe.wait_ge(y_kept, j)
                        output(j, r % 2)
                for j in range(tiles - R, tiles):
                    if j + 2 < tiles:
                        turn((j + 2) // R, j + 2, (j + 2) % R)
                    if j + 1 < tiles:
                        hidden(j + 1, (j + 1) % 2)
                    pe.wait_ge(y_kept, j - 1)
                    output(j, j % 2)


def combine(net, name, layer, choices, rw, pre_sh, weight):
    nc, dram = net.nc, net.dram
    two = layer == 0
    with ExitStack() as ctx:
        sb = lambda n, s, d=F32: net.sbuf(f"{name}_{n}", s, d, ctx)
        sem = lambda n: net.sem(f"{name}_{n}", ctx)
        yl = [sb(f"yl{u}", [P, choices, D]) for u in range(4)]
        mixed = sb("mixed", [P, NT, D])
        norm_w = sb("norm_w", [P, 2, D])
        loaded = [sem(f"y_loaded{u}") for u in range(4)]
        w_loaded, step, used, shared_ready = sem("norm_w_loaded"), sem("c_step"), sem("y_used"), sem("shared_ready")
        rows = net.y_rows.rearrange("(c t p) d -> t p c d", c=TOP_K, p=P)
        with nc.Block() as block:
            @block.sync
            def _(sp):
                if two:
                    sp.dma_start(norm_w[:, :, :], dram["l0_norm_w"]).then_inc(w_loaded, 16)
                sp.sem_inc(used, 4)
                with sp.Fori(0, NT // 4) as k:
                    for u in range(4):
                        t = k * 4 + u
                        sp.wait_ge(used, t + 1)
                        sp.dma_start(yl[u][:, :, :],
                                     rows[bass.ds(t, 1), :, 0:choices, :].rearrange("a p c d -> p (a c) d")
                                     ).then_inc(loaded[u], 16)

            if two:
                @block.scalar
                def _(act):
                    for t in range(0, NT, 8):
                        last = act.activation(mixed[:, t:t + 8, :], pre_sh[:, t:t + 8, 0:D], ACT.Gelu)
                        last.then_inc(shared_ready, 8)

            @block.vector
            def _(dve):
                link = Chain(dve, step)
                if two:
                    dve.wait_ge(w_loaded, 16)
                    link(dve.tensor_scalar(norm_w[:, :, :], norm_w[:, :, :], 0.5, None, ALU.mult))
                    link(dve.tensor_tensor(net.x[:, :, :], net.x[:, :, :],
                                           norm_w[:, 1, :].unsqueeze(1).broadcast_to([P, NT, D]), ALU.add))
                with dve.Fori(0, NT // 4) as k:
                    for u in range(4):
                        t = k * 4 + u
                        here = flat(mixed[:, bass.ds(t, 1), :])
                        dve.wait_ge(loaded[u], 16 * k + 16)
                        if two:
                            dve.wait_ge(shared_ready, t + 1)
                            link.in_loop(dve.tensor_scalar(here, here, 0.5, None, ALU.mult), k, u * 2, 8)
                            link.in_loop(dve.scalar_tensor_tensor(
                                out=here, in0=yl[u][:, 0, :], scalar=weight[:, 0, bass.ds(t, 1)], in1=here,
                                op0=ALU.mult, op1=ALU.add), k, u * 2 + 1, 8)
                            last = dve.scalar_tensor_tensor(
                                out=here, in0=yl[u][:, 1, :], scalar=weight[:, 1, bass.ds(t, 1)], in1=here,
                                op0=ALU.mult, op1=ALU.add)
                            last.then_inc(used, 1)
                        else:
                            here = flat(net.x[:, bass.ds(t, 1), :])
                            dve.scalar_tensor_tensor(
                                out=here, in0=yl[u][:, 0, :], scalar=weight[:, 0, bass.ds(t, 1)], in1=here,
                                op0=ALU.mult, op1=ALU.add).then_inc(used, 1)
                dve.wait_ge(used, NT + 4)
        if two:
            add_normalised(net, name, mixed, norm_w)


def add_normalised(net, name, mixed, norm_w):
    nc = net.nc
    layer_norm_stats(net, f"{name}_out", mixed)
    with ExitStack() as ctx:
        normed, scaled, added = (net.sem(f"{name}_{n}", ctx) for n in ("normed", "scaled", "added"))
        with nc.Block() as block:
            @block.vector
            def _(dve):
                with dve.Fori(0, NT) as t:
                    here = flat(mixed[:, bass.ds(t, 1), :])
                    dve.tensor_scalar(here, here, net.mean[:, bass.ds(t, 1)], net.rstd[:, bass.ds(t, 1)],
                                      ALU.subtract, ALU.mult).then_inc(normed, 1)
                dve.wait_ge(normed, NT)
                dve.tensor_tensor(mixed[:, :, :], mixed[:, :, :],
                                  norm_w[:, 0, :].unsqueeze(1).broadcast_to([P, NT, D]), ALU.mult).then_inc(scaled, 1)
                dve.wait_ge(scaled, 1)
                dve.tensor_tensor(net.x[:, :, :], net.x[:, :, :], mixed[:, :, :], ALU.add).then_inc(added, 1)


def mamba(net):
    nc, dram = net.nc, net.dram
    layer_norm_stats(net, "mb", net.x)
    with ExitStack() as ctx:
        sb = lambda n, s, d=F32: net.sbuf(f"mb_{n}", s, d, ctx)
        sem = lambda n: net.sem(f"mb_{n}", ctx)
        w_in = sb("w_in", [P, 2 * DI])
        w_out = sb("w_out", [P, IC, D])
        w_b = sb("w_b", [P, IC, DS])
        w_c = sb("w_c", [DS, DI])
        conv_w = sb("conv_w", [P, IC, DC])
        conv_b = sb("conv_b", [P, IC])
        keep = sb("keep", [DS, S])
        xn = [sb(f"xn{u}", [P, TB, D]) for u in range(2)]
        xt = [sb(f"xt{u}", [P, S]) for u in range(2)]
        xp = [sb(f"xp{u}", [P, IC, S + DC - 1]) for u in range(2)]
        conv = [sb(f"conv{u}", [P, IC, S]) for u in range(2)]
        xc = [sb(f"xc{u}", [P, IC, S]) for u in range(2)]
        gate = [sb(f"gate{u}", [P, IC, S]) for u in range(2)]
        taken = [sb(f"taken{u}", [DS, S]) for u in range(2)]
        state = [sb(f"state{u}", [DS, S]) for u in range(2)]
        gated = [sb(f"gated{u}", [P, IC, S]) for u in range(2)]
        t_ps = net.psum("mb_t_ps", [P, S], ctx)
        z_ps = net.psum("mb_z_ps", [P, 2 * IC, S], ctx)
        u_ps = net.psum("mb_u_ps", [P, S], ctx)
        y_ps = net.psum("mb_y_ps", [P, IC, S], ctx)
        w_loaded, padded, xn_ready, turned, xt_ready = (sem(n) for n in ("w_loaded", "padded", "xn_ready", "turned", "xt_ready"))
        xz_ready, xp_ready, conv_step, conv_ready, xc_ready = (sem(n) for n in ("xz_ready", "xp_ready", "conv_step", "conv_ready", "xc_ready"))
        gate_ready, u_ready, taken_ready, state_ready = (sem(n) for n in ("gate_ready", "u_ready", "taken_ready", "state_ready"))
        y_ready, gated_ready, o_ready, added = (sem(n) for n in ("y_ready", "gated_ready", "o_ready", "added"))
        loads = [(w_in, "w_in"), (w_out, "w_out"), (w_b, "w_b"), (w_c, "w_c"), (conv_w, "conv_w"), (conv_b, "conv_b")]
        with nc.Block() as block:
            @block.sync
            def _(sp):
                for dst, src in loads:
                    sp.dma_start(dst[:], dram[src]).then_inc(w_loaded, 16)

            @block.gpsimd
            def _(pool):
                for u in range(2):
                    pool.memset(xp[u][:, :, 0:DC - 1], 0.0).then_inc(padded, 1)
                pool.memset(keep[:, :], KEEP).then_inc(padded, 1)

            @block.vector
            def _(dve):
                dve.wait_ge(w_loaded, 16 * len(loads))
                dve.wait_ge(padded, 3)
                with dve.Fori(0, B // 2) as k:
                    for u in range(2):
                        b = k * 2 + u
                        dve.wait_ge(turned, b)
                        for t in range(TB):
                            at = b * TB + t
                            dve.tensor_scalar(xn[u][:, t, :], flat(net.x[:, bass.ds(at, 1), :]),
                                              net.mean[:, bass.ds(at, 1)], net.rstd[:, bass.ds(at, 1)],
                                              ALU.subtract, ALU.mult).then_inc(xn_ready, 1)
                        dve.wait_ge(xp_ready, b + 1)
                        for c in range(IC):
                            for j in range(DC):
                                if j == 0:
                                    ins = dve.tensor_scalar(conv[u][:, c, :], xp[u][:, c, 0:S], conv_w[:, c, 0:1],
                                                            None, ALU.mult)
                                else:
                                    ins = dve.scalar_tensor_tensor(
                                        out=conv[u][:, c, :], in0=xp[u][:, c, j:j + S], scalar=conv_w[:, c, j:j + 1],
                                        in1=conv[u][:, c, :], op0=ALU.mult, op1=ALU.add)
                                if j < DC - 1:
                                    ins.then_inc(conv_step, 1)
                                    dve.wait_ge(conv_step, b * (IC * (DC - 1)) + (c * (DC - 1) + j + 1))
                            ins.then_inc(conv_ready, 1)
                        dve.wait_ge(taken_ready, b + 1)
                        dve.tensor_tensor_scan(state[u][:, :], keep[:, :], taken[u][:, :], 0.0,
                                               ALU.mult, ALU.add).then_inc(state_ready, 1)
                        dve.wait_ge(gate_ready, b + 1)
                        dve.wait_ge(y_ready, b + 1)
                        dve.tensor_tensor(gated[u][:, :, :], y_ps[:, :, :], gate[u][:, :, :],
                                          ALU.mult).then_inc(gated_ready, 1)
                        dve.wait_ge(o_ready, b + 1)
                        rows = net.x[:, bass.ds(b * TB, TB), :]
                        dve.tensor_tensor(rows, rows, y_ps[:, 0, :].rearrange("p (t d) -> p t d", t=TB),
                                          ALU.add).then_inc(added, 1)

            @block.scalar
            def _(act):
                with act.Fori(0, B // 2) as k:
                    for u in range(2):
                        b = k * 2 + u
                        act.wait_ge(turned, b + 1)
                        act.activation(xt[u][:, :], t_ps[:, :], ACT.Copy).then_inc(xt_ready, 1)
                        act.wait_ge(xz_ready, b + 1)
                        act.activation(xp[u][:, :, DC - 1:], z_ps[:, 0:IC, :], ACT.Copy).then_inc(xp_ready, 1)
                        act.activation(gate[u][:, :, :], z_ps[:, IC:, :], ACT.Silu).then_inc(gate_ready, 1)
                        for c in range(IC):
                            act.wait_ge(conv_ready, b * IC + (c + 1))
                            act.activation(xc[u][:, c, :], conv[u][:, c, :], ACT.Silu,
                                           bias=conv_b[:, c:c + 1]).then_inc(xc_ready, 1)
                        act.wait_ge(u_ready, b + 1)
                        act.activation(taken[u][:, :], u_ps[0:DS, :], ACT.Copy, scale=TAKE).then_inc(taken_ready, 1)

            @block.tensor
            def _(pe):
                pe.wait_ge(w_loaded, 16 * len(loads))
                with pe.Fori(0, B // 2) as k:
                    for u in range(2):
                        b = k * 2 + u
                        pe.wait_ge(xt_ready, b)
                        for t in range(TB):
                            pe.wait_ge(xn_ready, b * TB + (t + 1))
                            last = pe.transpose(t_ps[:, t * P:(t + 1) * P], xn[u][:, t, :], net.ident[:, :])
                        last.then_inc(turned, 1)
                        pe.wait_ge(xt_ready, b + 1)
                        pe.wait_ge(gate_ready, b)
                        for c in range(2 * IC):
                            last = pe.matmul(z_ps[:, c, :], w_in[:, c * P:(c + 1) * P], xt[u][:, :],
                                             start=True, stop=True)
                        last.then_inc(xz_ready, 1)
                        for c in range(IC):
                            pe.wait_ge(xc_ready, b * IC + (c + 1))
                            last = pe.matmul(u_ps[0:DS, :], w_b[:, c, :], xc[u][:, c, :],
                                             start=c == 0, stop=c == IC - 1)
                        last.then_inc(u_ready, 1)
                        pe.wait_ge(state_ready, b + 1)
                        pe.wait_ge(added, b)
                        for c in range(IC):
                            last = pe.matmul(y_ps[:, c, :], w_c[:, c * P:(c + 1) * P], state[u][:, :],
                                             start=True, stop=True)
                        last.then_inc(y_ready, 1)
                        pe.wait_ge(gated_ready, b + 1)
                        for t in range(TB):
                            for c in range(IC):
                                last = pe.matmul(y_ps[:, 0, t * P:(t + 1) * P], gated[u][:, c, t * P:(t + 1) * P],
                                                 w_out[:, c, :], start=c == 0, stop=c == IC - 1,
                                                 skip_group_check=True)
                        last.then_inc(o_ready, 1)


def power_attention(net):
    nc, dram = net.nc, net.dram
    layer_norm_stats(net, "pa", net.x)
    with ExitStack() as ctx:
        sb = lambda n, s, d=F32: net.sbuf(f"pa_{n}", s, d, ctx)
        sem = lambda n: net.sem(f"pa_{n}", ctx)
        w_g = sb("w_group", [P, KV, GROUP_W])
        w_gate = sb("w_gate", [P, KV])
        w_proj = sb("w_proj", [P, KV, D])
        ln_w = sb("ln_w", [P, 1])
        v_mean = sb("v_mean", [P, KV])
        rope_c = sb("rope_c", [P, TB, ROPE_W])
        rope_s = sb("rope_s", [P, TB, ROPE_W])
        select = sb("select", [KV, KV, P])
        ident_b = sb("ident_b", [P, P], BF16)
        mask_b = sb("mask_b", [P, P], BF16)
        one = sb("one", [P, S])
        score_min = sb("score_min", [P, 1])
        head_eps = sb("head_eps", [P, 1])
        xn = sb("xn", [P, TB, D])
        xt = sb("xt", [P, S])
        gate_x = sb("gate_x", [KV, S])
        gate_e = sb("gate_e", [KV, S])
        gate_sum = sb("gate_sum", [KV, S])
        neg_gate = sb("neg_gate", [P, TB, KV])
        rope_a = sb("rope_a", [P, TB, ROPE_W])
        rope_b = sb("rope_b", [P, TB, ROPE_W])
        qk = [sb(f"qk{u}", [P, TB, QW + 2 * KW]) for u in range(2)]
        q_t = [sb(f"q_t{u}", [P, S]) for u in range(2)]
        k_t = [sb(f"k_t{u}", [P, S]) for u in range(2)]
        v = [sb(f"v{u}", [P, TB, HD + 1]) for u in range(2)]
        decay = [sb(f"decay{u}", [P, SCORE_W]) for u in range(2)]
        a = [sb(f"a{u}", [P, SCORE_W]) for u in range(2)]
        top = sb("top", [P, S])
        top_row = sb("top_row", [P, TB])
        den = sb("den", [P, TB])
        y = [sb(f"y{u}", [P, TB, RATIO, HD]) for u in range(2)]
        y_sq = sb("y_sq", [P, TB, HD])
        sq_sum = sb("sq_sum", [P, TB, RATIO])
        y_rstd = [sb(f"y_rstd{u}", [P, TB, RATIO]) for u in range(2)]
        y_t = sb("y_t", [P, KV, S])
        s_ps = net.psum("pa_s_ps", [P, 3 * S], ctx)
        p_ps = net.psum("pa_p_ps", [P, TB, GROUP_W], ctx)
        o_ps = net.psum("pa_o_ps", [P, S], ctx)
        t_ps = net.psum("pa_t_ps", [P, S], ctx)
        g_ps = net.psum("pa_g_ps", [P, S], ctx)
        o_view = o_ps[:, 0:TB * (HD + 1)].rearrange("p (t d) -> p t d", t=TB)
        names = ("w_loaded made prepared setup xn_ready x_turned xt_ready gate_z gate_x gate_na gate_exp gate_ln gate_log "
                 "gate_sum gate_passed gate_turned neg_gate projected rope_ab roped v_ready q_turned q_ready k_turned k_ready "
                 "spread decay_off masked decay_ready scored squared weighed topped_step topped top_turned top_read "
                 "valued den_step den_ready y_raw y_squared sq_summed y_ln y_rstd y_ready y_turned y_copied out_ready added")
        m = {n: sem(n) for n in names.split()}
        loads = [(w_g, "w_group"), (w_gate, "w_gate"), (w_proj, "w_proj"), (ln_w, "ln_w"),
                 (rope_c, "rope_c"), (rope_s, "rope_s"), (select, "select")]

        with nc.Block() as block:
            @block.sync
            def _(sp):
                for dst, src in loads:
                    sp.dma_start(dst[:], dram[src]).then_inc(m["w_loaded"], 16)

            @block.gpsimd
            def _(pool):
                link = Chain(pool, m["made"])
                link(pool.memset(one[:, :], 1.0))
                link(pool.memset(score_min[:, :], SCORE_SCALE * SCORE_MIN))
                link(pool.memset(head_eps[:, :], HEAD_EPS))
                for u in range(2):
                    link(pool.memset(v[u][:, :, HD:], 1.0))
                link(pool.memset(mask_b[:, :], 0.0))
                link(pool.affine_select(out=mask_b[:, :], in_=mask_b[:, :], compare_op=ALU.is_ge, fill=MASKED,
                                        base=0, pattern=[[1, P]], channel_multiplier=-1))

            @block.vector
            def _(dve):
                link = Chain(dve, m["prepared"])
                link(dve.tensor_copy(ident_b[:, :], net.ident[:, :]))
                dve.wait_ge(m["w_loaded"], 16 * len(loads))
                values = w_g[:, :, ROPE_W:]
                link(dve.tensor_reduce(v_mean[:, :], values, AX.X, ALU.add))
                link(dve.tensor_scalar(v_mean[:, :], v_mean[:, :], 1.0 / HD, None, ALU.mult))
                link(dve.tensor_tensor(values, values, v_mean[:, :].unsqueeze(2).broadcast_to([P, KV, HD]), ALU.subtract))
                link(dve.tensor_scalar(w_proj[:, :, :], w_proj[:, :, :], ln_w[:, 0:1], None, ALU.mult))

        with nc.Block() as block:
            @block.vector
            def _(dve):
                with dve.Fori(0, B) as b:
                    def rope(g):
                        dve.wait_ge(m["projected"], b * KV + (g + 1))
                        dve.wait_ge(m["v_ready"], b * KV + (g + 1))
                        dve.wait_ge(m["roped"], b * KV + g)
                        pairs = lambda ap: ap.rearrange("p t (h two) -> p t h two", two=2)
                        dve.tensor_tensor(rope_a[:, :, :], p_ps[:, :, 0:ROPE_W], rope_c[:, :, :],
                                          ALU.mult).then_inc(m["rope_ab"], 1)
                        dve.tensor_tensor(pairs(rope_b[:, :, :]), pairs(p_ps[:, :, 0:ROPE_W])[:, :, :, ::-1],
                                          pairs(rope_s[:, :, :]), ALU.mult).then_inc(m["rope_ab"], 1)

                    def weigh(g, u):
                        n = b * (2 * KV) + (2 * g + u + 1)
                        dve.wait_ge(m["squared"], n)
                        dve.wait_ge(m["decay_ready"], b * KV + (g + 1))
                        dve.tensor_tensor(a[u][:, :], a[u][:, :], decay[g % 2][:, :], ALU.mult).then_inc(m["weighed"], 1)

                    def largest(g, u):
                        n = b * (2 * KV) + (2 * g + u)
                        dve.wait_ge(m["weighed"], n + 1)
                        dve.wait_ge(m["top_turned"], n)
                        at = lambda i: a[u][:, block_at(i, i):block_at(i, i) + (TB - i) * P]
                        dve.tensor_tensor(top[:, P:], a[u][:, P:S], at(1), ALU.max).then_inc(m["topped_step"], 1)
                        dve.wait_ge(m["topped_step"], 2 * n + 1)
                        dve.tensor_tensor(top[:, 2 * P:], top[:, 2 * P:], at(2), ALU.max).then_inc(m["topped_step"], 1)
                        dve.wait_ge(m["topped_step"], 2 * n + 2)
                        dve.tensor_tensor(top[:, 3 * P:], top[:, 3 * P:], at(3), ALU.max).then_inc(m["topped"], 1)

                    def divide(g, u):
                        n = b * (2 * KV) + (2 * g + u)
                        dve.wait_ge(m["top_turned"], n + 1)
                        dve.tensor_reduce(top_row[:, :], t_ps[:, :].rearrange("p (t s) -> p t s", t=TB), AX.X,
                                          ALU.max).then_inc(m["top_read"], 1)
                        dve.wait_ge(m["top_read"], n + 1)
                        dve.wait_ge(m["valued"], n + 1)
                        dve.scalar_tensor_tensor(out=den[:, :], in0=top_row[:, :], scalar=DEN_EPS, in1=o_view[:, :, HD],
                                                 op0=ALU.mult, op1=ALU.add).then_inc(m["den_step"], 1)
                        dve.wait_ge(m["den_step"], n + 1)
                        dve.reciprocal(den[:, :], den[:, :]).then_inc(m["den_ready"], 1)
                        dve.wait_ge(m["den_ready"], n + 1)
                        if u == 0:
                            dve.wait_ge(m["y_turned"], max(g - 1, 0) + b * KV)
                        dve.tensor_tensor(y[g % 2][:, :, u, :], o_view[:, :, 0:HD],
                                          den[:, :].unsqueeze(2).broadcast_to([P, TB, HD]), ALU.mult).then_inc(m["y_raw"], 1)

                    def sum_squares(g, u):
                        n = b * (2 * KV) + (2 * g + u)
                        dve.wait_ge(m["y_squared"], n + 1)
                        dve.wait_ge(m["y_ln"], b * KV + g)
                        dve.tensor_reduce(sq_sum[:, :, u], y_sq[:, :, :], AX.X, ALU.add).then_inc(m["sq_summed"], 1)

                    for t in range(TB):
                        at = b * TB + t
                        dve.wait_ge(m["x_turned"], b)
                        dve.tensor_scalar(xn[:, t, :], flat(net.x[:, bass.ds(at, 1), :]), net.mean[:, bass.ds(at, 1)],
                                          net.rstd[:, bass.ds(at, 1)], ALU.subtract, ALU.mult).then_inc(m["xn_ready"], 1)
                    dve.wait_ge(m["gate_z"], b + 1)
                    dve.tensor_scalar(gate_x[:, :], g_ps[0:KV, :], GATE_BIAS, None, ALU.add).then_inc(m["gate_x"], 1)
                    dve.wait_ge(m["gate_x"], b + 1)
                    dve.scalar_tensor_tensor(out=gate_e[:, :], in0=gate_x[:, :], scalar=-1.0, in1=gate_x[:, :],
                                             op0=ALU.mult, op1=ALU.min).then_inc(m["gate_na"], 1)
                    dve.wait_ge(m["gate_ln"], b + 1)
                    dve.scalar_tensor_tensor(out=gate_x[:, :], in0=gate_x[:, :], scalar=0.0, in1=gate_e[:, :],
                                             op0=ALU.min, op1=ALU.subtract).then_inc(m["gate_log"], 1)
                    dve.wait_ge(m["gate_log"], b + 1)
                    dve.tensor_tensor_scan(gate_sum[:, :], one[0:KV, :], gate_x[:, :], 0.0,
                                           ALU.mult, ALU.add).then_inc(m["gate_sum"], 1)
                    dve.wait_ge(m["gate_turned"], b + 1)
                    dve.tensor_scalar(neg_gate[:, :, :].rearrange("p t g -> p (t g)"), g_ps[:, 0:TB * KV], -1.0, None,
                                      ALU.mult).then_inc(m["neg_gate"], 1)
                    rope(0)
                    for g in range(KV):
                        weigh(g, 0)
                        if g + 1 < KV:
                            rope(g + 1)
                        largest(g, 0)
                        weigh(g, 1)
                        divide(g, 0)
                        largest(g, 1)
                        sum_squares(g, 0)
                        divide(g, 1)
                        sum_squares(g, 1)
                    dve.wait_ge(m["out_ready"], b + 1)
                    rows = net.x[:, bass.ds(b * TB, TB), :]
                    dve.tensor_tensor(rows, rows, g_ps[:, :].rearrange("p (t d) -> p t d", t=TB),
                                      ALU.add).then_inc(m["added"], 1)

            @block.gpsimd
            def _(pool):
                with pool.Fori(0, B) as b:
                    def add_up(g):
                        pool.wait_ge(m["rope_ab"], b * (2 * KV) + (2 * g + 2))
                        pool.wait_ge(m["k_turned"], b * KV + max(g - 1, 0))
                        pool.tensor_tensor(qk[g % 2][:, :, ROPE_W:], rope_a[:, :, QW:], rope_b[:, :, QW:],
                                           ALU.add)
                        pool.tensor_tensor(qk[g % 2][:, :, 0:ROPE_W], rope_a[:, :, :], rope_b[:, :, :],
                                           ALU.add).then_inc(m["roped"], 1)

                    def scale(g):
                        pool.wait_ge(m["y_rstd"], b * KV + (g + 1))
                        pool.tensor_tensor(y[g % 2][:, :, :, :].rearrange("p t u d -> p (t u) d"),
                                           y[g % 2][:, :, :, :].rearrange("p t u d -> p (t u) d"),
                                           y_rstd[g % 2][:, :, :].rearrange("p t u -> p (t u)").unsqueeze(2)
                                           .broadcast_to([P, TB * RATIO, HD]), ALU.mult).then_inc(m["y_ready"], 1)

                    add_up(0)
                    for g in range(KV):
                        if g >= 1:
                            scale(g - 1)
                        if g + 1 < KV:
                            add_up(g + 1)
                    scale(KV - 1)

            @block.scalar
            def _(act):
                with act.Fori(0, B) as b:
                    def square(g, u):
                        n = b * (2 * KV) + (2 * g + u)
                        act.wait_ge(m["scored"], n + 1)
                        act.wait_ge(m["top_turned"], b * (2 * KV) + max(2 * g + u - 1, 0))
                        act.wait_ge(m["valued"], b * (2 * KV) + max(2 * g + u - 1, 0))
                        act.activation(a[u][:, :], s_ps[:, 0:SCORE_W], ACT.Square, bias=score_min[:, 0:1],
                                       scale=SCORE_SCALE * HD ** -0.5).then_inc(m["squared"], 1)

                    def keep_v(g):
                        act.wait_ge(m["projected"], b * KV + (g + 1))
                        act.wait_ge(m["valued"], b * (2 * KV) + max(2 * g - 2, 0))
                        act.activation(v[g % 2][:, :, 0:HD], p_ps[:, :, ROPE_W:], ACT.Copy).then_inc(m["v_ready"], 1)

                    def decay_off(g):
                        act.wait_ge(m["spread"], b * KV + (g + 1))
                        act.wait_ge(m["neg_gate"], b + 1)
                        act.wait_ge(m["weighed"], b * (2 * KV) + max(2 * g - 2, 0))
                        for i in range(TB - 1):
                            at = block_at(i, i + 1)
                            last = act.activation(decay[g % 2][:, at:at + (TB - 1 - i) * P], g_ps[:, (i + 1) * P:],
                                                  ACT.Exp, bias=neg_gate[:, i, g:g + 1])
                        last.then_inc(m["decay_off"], 1)

                    def decay_diagonal(g):
                        act.wait_ge(m["masked"], b * KV + (g + 1))
                        for i in range(TB):
                            at = block_at(i, i)
                            last = act.activation(decay[g % 2][:, at:at + P], g_ps[:, i * P:(i + 1) * P],
                                                  ACT.Exp, bias=neg_gate[:, i, g:g + 1])
                        last.then_inc(m["decay_ready"], 1)

                    def copy_qk(g):
                        act.wait_ge(m["q_turned"], b * KV + (g + 1))
                        act.wait_ge(m["scored"], b * (2 * KV) + max(2 * g - 2, 0))
                        act.activation(q_t[g % 2][:, :], t_ps[:, :], ACT.Copy).then_inc(m["q_ready"], 1)
                        act.wait_ge(m["k_turned"], b * KV + (g + 1))
                        act.activation(k_t[g % 2][:, :], t_ps[:, :], ACT.Copy).then_inc(m["k_ready"], 1)

                    def square_y(g, u):
                        n = b * (2 * KV) + (2 * g + u)
                        act.wait_ge(m["y_raw"], n + 1)
                        act.wait_ge(m["sq_summed"], n)
                        act.activation(y_sq[:, :, :], y[g % 2][:, :, u, :], ACT.Square).then_inc(m["y_squared"], 1)

                    def inverse_root(g):
                        act.wait_ge(m["sq_summed"], b * (2 * KV) + (2 * g + 2))
                        act.wait_ge(m["y_ready"], b * KV + max(g - 1, 0))
                        act.activation(y_rstd[g % 2][:, :, :], sq_sum[:, :, :], ACT.Ln, bias=head_eps[:, 0:1],
                                       scale=1.0 / HD).then_inc(m["y_ln"], 1)
                        act.wait_ge(m["y_ln"], b * KV + (g + 1))
                        act.activation(y_rstd[g % 2][:, :, :], y_rstd[g % 2][:, :, :], ACT.Exp,
                                       scale=-0.5).then_inc(m["y_rstd"], 1)

                    def copy_y(g):
                        act.wait_ge(m["y_turned"], b * KV + (g + 1))
                        act.activation(y_t[:, g, :], t_ps[:, :], ACT.Copy).then_inc(m["y_copied"], 1)

                    act.wait_ge(m["x_turned"], b + 1)
                    act.activation(xt[:, :], g_ps[:, :], ACT.Copy).then_inc(m["xt_ready"], 1)
                    act.wait_ge(m["gate_na"], b + 1)
                    act.activation(gate_e[:, :], gate_e[:, :], ACT.Exp).then_inc(m["gate_exp"], 1)
                    act.wait_ge(m["gate_exp"], b + 1)
                    act.activation(gate_e[:, :], gate_e[:, :], ACT.Ln, bias=one[0:KV, 0:1]).then_inc(m["gate_ln"], 1)
                    keep_v(0)
                    decay_off(0)
                    decay_diagonal(0)
                    copy_qk(0)
                    for g in range(KV):
                        square(g, 0)
                        if g >= 1:
                            inverse_root(g - 1)
                        if g + 1 < KV:
                            keep_v(g + 1)
                        square(g, 1)
                        if g >= 1:
                            copy_y(g - 1)
                        if g + 1 < KV:
                            decay_off(g + 1)
                        square_y(g, 0)
                        if g + 1 < KV:
                            decay_diagonal(g + 1)
                            copy_qk(g + 1)
                        square_y(g, 1)
                    inverse_root(KV - 1)
                    copy_y(KV - 1)

            @block.tensor
            def _(pe):
                with pe.Fori(0, B) as b:
                    def t_ps_free(tops, qs, ys):
                        pe.wait_ge(m["top_read"], b * (2 * KV) + tops)
                        pe.wait_ge(m["k_ready"], b * KV + qs)
                        pe.wait_ge(m["y_copied"], b * KV + ys)

                    def project(g):
                        pe.wait_ge(m["rope_ab"], b * (2 * KV) + 2 * g)
                        pe.wait_ge(m["v_ready"], b * KV + g)
                        for t in range(TB):
                            last = pe.matmul(p_ps[:, t, :], xt[:, t * P:(t + 1) * P], w_g[:, g, :],
                                             start=True, stop=True, skip_group_check=True)
                        last.then_inc(m["projected"], 1)

                    def turn_qk(g, tops, ys):
                        pe.wait_ge(m["roped"], b * KV + (g + 1))
                        t_ps_free(tops, g, ys)
                        for t in range(TB):
                            last = pe.transpose(t_ps[:, t * P:(t + 1) * P], qk[g % 2][:, t, 0:QW], net.ident[:, :])
                        last.then_inc(m["q_turned"], 1)
                        pe.wait_ge(m["q_ready"], b * KV + (g + 1))
                        for t in range(TB):
                            last = pe.transpose(t_ps[:, t * P:(t + 1) * P], qk[g % 2][:, t, QW:], net.ident[:, :])
                        last.then_inc(m["k_turned"], 1)

                    def spread(g):
                        pe.wait_ge(m["decay_ready"], b * KV + g)
                        pe.matmul(g_ps[:, :], select[:, g, :], gate_sum[:, :], start=True, stop=False,
                                  skip_group_check=True).then_inc(m["spread"], 1)

                    def mask(g):
                        pe.wait_ge(m["decay_off"], b * KV + (g + 1))
                        pe.matmul(g_ps[:, :].rearrange("p (t s) -> p t s", t=TB), ident_b[:, :],
                                  mask_b[:, :].unsqueeze(1).broadcast_to([P, TB, P]), start=False, stop=True,
                                  skip_group_check=True).then_inc(m["masked"], 1)

                    def score(g, u):
                        n = b * (2 * KV) + (2 * g + u)
                        pe.wait_ge(m["k_ready"], b * KV + (g + 1))
                        pe.wait_ge(m["squared"], n)
                        rows = slice(u * HD, (u + 1) * HD)
                        for i in range(TB):
                            at = block_at(i, i)
                            last = pe.matmul(s_ps[:, at:at + (TB - i) * P], k_t[g % 2][rows, i * P:(i + 1) * P],
                                             q_t[g % 2][rows, i * P:], start=True, stop=True, skip_group_check=True)
                        last.then_inc(m["scored"], 1)

                    def value(g, u):
                        n = b * (2 * KV) + (2 * g + u)
                        pe.wait_ge(m["weighed"], n + 1)
                        pe.wait_ge(m["v_ready"], b * KV + (g + 1))
                        pe.wait_ge(m["y_raw"], n)
                        for j in range(TB):
                            for i in range(j + 1):
                                at = block_at(i, j)
                                last = pe.matmul(o_view[:, j, :], a[u][:, at:at + P], v[g % 2][:, i, :],
                                                 start=i == 0, stop=i == j, skip_group_check=True)
                        last.then_inc(m["valued"], 1)

                    def turn_top(g, u, qs, ys):
                        n = b * (2 * KV) + (2 * g + u)
                        pe.wait_ge(m["topped"], n + 1)
                        t_ps_free(2 * g + u, qs, ys)
                        for t in range(TB):
                            src = a[u] if t == 0 else top
                            last = pe.transpose(t_ps[:, t * P:(t + 1) * P], src[:, t * P:(t + 1) * P], net.ident[:, :])
                        last.then_inc(m["top_turned"], 1)

                    def turn_y(g, tops, qs):
                        pe.wait_ge(m["y_ready"], b * KV + (g + 1))
                        t_ps_free(tops, qs, g)
                        for t in range(TB):
                            last = pe.transpose(t_ps[:, t * P:(t + 1) * P],
                                                y[g % 2][:, t, :, :].rearrange("p u d -> p (u d)"), net.ident[:, :])
                        last.then_inc(m["y_turned"], 1)

                    pe.wait_ge(m["added"], b)
                    for t in range(TB):
                        pe.wait_ge(m["xn_ready"], b * TB + (t + 1))
                        last = pe.transpose(g_ps[:, t * P:(t + 1) * P], xn[:, t, :], net.ident[:, :])
                    last.then_inc(m["x_turned"], 1)
                    pe.wait_ge(m["xt_ready"], b + 1)
                    pe.matmul(g_ps[0:KV, :], w_gate[:, :], xt[:, :], start=True, stop=True,
                              skip_group_check=True).then_inc(m["gate_z"], 1)
                    project(0)
                    pe.wait_ge(m["gate_sum"], b + 1)
                    pe.sem_inc(m["gate_passed"], 1)
                    for t in range(TB):
                        last = pe.transpose(g_ps[:, t * KV:(t + 1) * KV], gate_sum[:, t * P:(t + 1) * P],
                                            net.ident[0:KV, 0:KV])
                    last.then_inc(m["gate_turned"], 1)
                    pe.wait_ge(m["neg_gate"], b + 1)
                    spread(0)
                    mask(0)
                    turn_qk(0, 0, 0)
                    for g in range(KV):
                        score(g, 0)
                        if g + 1 < KV:
                            project(g + 1)
                        score(g, 1)
                        if g >= 1:
                            turn_y(g - 1, 2 * g, g + 1)
                        value(g, 0)
                        turn_top(g, 0, g + 1, g)
                        if g + 1 < KV:
                            spread(g + 1)
                        value(g, 1)
                        if g + 1 < KV:
                            mask(g + 1)
                            turn_qk(g + 1, 2 * g + 1, g)
                        turn_top(g, 1, min(g + 2, KV), g)
                    turn_y(KV - 1, 2 * KV, KV)
                    pe.wait_ge(m["y_copied"], b * KV + KV)
                    for t in range(TB):
                        for g in range(KV):
                            last = pe.matmul(g_ps[:, t * P:(t + 1) * P], y_t[:, g, t * P:(t + 1) * P], w_proj[:, g, :],
                                             start=g == 0, stop=g == KV - 1, skip_group_check=True)
                    last.then_inc(m["out_ready"], 1)


def program(nc, dram, out, stages):
    with ExitStack() as ctx:
        net = Net(nc, ctx, dram)
        load_inputs(net, ctx)
        stages(net)
        stored = net.sem("out_stored", ctx)
        with nc.Block() as block:
            @block.sync
            def _(sp):
                sp.dma_start(out.rearrange("b (t p) d -> p (b t) d", p=P), net.x[:, :, :]).then_inc(stored, 16)
                sp.wait_ge(stored, 16)


def load_experts(net, name, source, ctx):
    experts = net.sbuf(name, [P, E, EXPERT_W], F32, ctx)
    loaded = net.sem(f"{name}_loaded", ctx)
    with net.nc.Block() as block:
        @block.sync
        def _(sp):
            sp.dma_start(experts[:, :, :], net.dram[source]).then_inc(loaded, 16)
            sp.wait_ge(loaded, 16)
    return experts


def whole_net(net):
    with ExitStack() as ctx:
        l0 = load_experts(net, "l0_experts", "l0_experts", ctx)
        mixture(net, "m0", 0, l0)
        mamba(net)
        mixture(net, "m1", 0, l0)
    with ExitStack() as ctx:
        l1 = load_experts(net, "l1_experts", "l1_experts", ctx)
        mixture(net, "m2", 1, l1)
        power_attention(net)
        mixture(net, "m3", 1, l1)


def rope_tables():
    div = (2.0 * np.pi / float(S) ** (np.arange(0, HD, 2, dtype=np.float32) / HD)).astype(np.float32)
    angle = (np.arange(S, dtype=np.float32)[:, None] * div[None, :]).astype(np.float64)
    cos = np.repeat(np.cos(angle), 2, 1)
    sin = np.repeat(np.sin(angle), 2, 1) * np.tile([-1.0, 1.0], HD // 2)
    place = lambda z: np.tile(z, (1, RATIO + 1)).reshape(TB, P, ROPE_W).transpose(1, 0, 2).astype(np.float32)
    return place(cos), place(sin)


def lay_out(i):
    i = {k: np.asarray(v) for k, v in i.items()}

    def experts(w1, b1, w2, b2):
        out = np.empty((P, E, EXPERT_W), np.float32)
        out[:, :, W1_AT:W2_AT] = w1.transpose(1, 0, 2)
        out[:, :, W2_AT:B2_AT] = w2.reshape(E, HC, P, D).transpose(2, 0, 1, 3).reshape(P, E, HC * D)
        out[:, :, B2_AT:B1_AT] = b2[None]
        out[:, :, B1_AT:] = b1.reshape(E, HC, P).transpose(2, 0, 1)
        return out

    def rows(v):
        return np.ascontiguousarray(np.broadcast_to(v, (P,) + v.shape))

    a = {"x": i["L0_attn_x"].reshape(N, D)}
    a["l0_experts"] = experts(i["L0_ffn_W1"], i["L0_ffn_b1"], i["L0_ffn_W2"], i["L0_ffn_b2"])
    a["l1_experts"] = experts(i["L1_ffn_w1"], i["L1_ffn_b1"], i["L1_ffn_w2"], i["L1_ffn_b2"])
    a["l0_shared_w"] = np.concatenate([i["L0_ffn_shared_W"], i["L0_ffn_gate_W"]], 1)
    a["l0_shared_b"] = rows(np.concatenate([i["L0_ffn_shared_b"], np.zeros(E, np.float32)]))
    a["l1_shared_w"] = np.ascontiguousarray(i["L1_ffn_router_w"].T)
    a["l1_shared_b"] = rows(np.zeros(E, np.float32))
    a["w_in"] = i["L0_attn_w_in"]
    a["w_out"] = i["L0_attn_w_out"].reshape(IC, P, D).transpose(1, 0, 2)
    a["w_b"] = i["L0_attn_w_B"].reshape(IC, P, DS).transpose(1, 0, 2)
    a["w_c"] = i["L0_attn_w_C"]
    a["conv_w"] = i["L0_attn_conv_w"].reshape(IC, P, DC).transpose(1, 0, 2)
    a["conv_b"] = i["L0_attn_conv_b"].reshape(IC, P).T
    w = i["L1_attn_w_attn"]
    q, k, v = np.split(w[:, :2048], [1024, 1536], 1)
    a["w_group"] = np.concatenate([q.reshape(D, KV, QW), k.reshape(D, KV, HD), v.reshape(D, KV, HD)], 2)
    a["w_gate"] = w[:, 2048:]
    a["w_proj"] = i["L1_attn_w_proj"].reshape(KV, P, D).transpose(1, 0, 2)
    a["ln_w"] = np.tile(i["L1_attn_ln_w"], RATIO)[:, None]
    a["rope_c"], a["rope_s"] = rope_tables()
    a["select"] = np.repeat(np.eye(KV, dtype=np.float32)[:, :, None], P, 2)
    a["l0_norm_w"] = rows(np.stack([i["L0_ffn_gamma"], i["L0_ffn_beta"]]))
    return a


def build(nc, arrays):
    dram = {n: nc.dram_tensor(f"in_{n}_dram", v.shape, F32, kind="ExternalInput").ap() for n, v in arrays.items()}
    out = nc.dram_tensor("out_dram", (B, S, D), F32, kind="ExternalOutput").ap()
    program(nc, dram, out, whole_net)


def kernel(**inputs):
    import concourse.bacc as _bacc
    from concourse.bass_utils import run_bass_kernel_spmd as _run

    nc = _bacc.Bacc("TRN2", target_bir_lowering=False, num_devices=1)
    arrays = {n: np.ascontiguousarray(v) for n, v in lay_out(inputs).items()}
    build(nc, arrays)
    r = _run(nc, [{f"in_{n}_dram": v for n, v in arrays.items()}], core_ids=[0])
    return r.results[0]["out_dram"]
```

```python
from contextlib import ExitStack

import concourse.bass as bass
from concourse import mybir
import numpy as np

F32 = mybir.dt.float32
BF16 = mybir.dt.bfloat16
I32 = mybir.dt.int32
ALU = mybir.AluOpType
ACT = mybir.ActivationFunctionType
AX = mybir.AxisListType

P = 128
B, S, D = 8, 512, 128
N = B * S
NT = N // P
TB = S // P
E = 8
H = 512
HC = H // P
TOP_K = 2
CAPACITY = -(-3 * N // (2 * E))
LN_EPS = 1e-5

W1_AT, W2_AT, B2_AT, B1_AT = 0, H, H + HC * D, H + HC * D + D
EXPERT_W = B1_AT + HC

RING = 4


def ring_multiple(tiles):
    return -(-tiles // RING) * RING


SLOT_TILES_L0 = ring_multiple((TOP_K * N + E * (P - 1)) // P)
SLOT_TILES_L1 = ring_multiple((N + E * (P - 1)) // P)
FAR_AWAY = 1.0e6

DI, DS, DC = 256, 16, 4
IC = DI // P
KEEP, TAKE = 0.9, 0.1

KV, HD, RATIO = 8, 64, 2
QW, KW = RATIO * HD, HD
GROUP_W = QW + KW + HD
ROPE_W = QW + KW
GATE_BIAS = 6.906768
SCORE_SCALE = 2.0 ** 40
SCORE_MIN = 1e-30
DEN_EPS, HEAD_EPS = 1e-6, 1e-9
MASKED = -1.0e30
PAIRS = [(i, j) for i in range(TB) for j in range(i, TB)]
SCORE_AT = {0: 0, 1: S, 3: S + 3 * P, 2: 2 * S}
SCORE_W = 2 * S + 2 * P


def block_at(i, j):
    return SCORE_AT[i] + (j - i) * P


class Counter:

    LEAD = 4

    def __init__(self, sem):
        self.sem = sem

    def wait(self, engine, count):
        engine.wait_ge(self.sem, count + self.LEAD)

    def by(self, instruction):
        instruction.then_inc(self.sem, 1)


class Chain:

    def __init__(self, engine, sem):
        self.engine, self.sem, self.n = engine, sem, 0

    def __call__(self, instruction):
        self.n += 1
        instruction.then_inc(self.sem, 1)
        self.engine.wait_ge(self.sem, self.n)

    def in_loop(self, instruction, trip, step, steps):
        instruction.then_inc(self.sem, 1)
        self.engine.wait_ge(self.sem, trip * steps + (self.n + step + 1))

    def loop_done(self, trips, steps):
        self.n += trips * steps


def flat(ap):
    return ap.rearrange("p a n -> p (a n)")


class Net:

    def __init__(self, nc, ctx, dram):
        self.nc, self.dram = nc, dram
        self.ctx = ctx
        self.counting = []
        sb = self.sbuf
        self.x = sb("stream", [P, NT, D])
        self.ident = sb("ident", [P, P])
        self.mean = sb("mean", [P, NT])
        self.rstd = sb("rstd", [P, NT])
        self.stats = sb("stats", [P, NT, 6])
        self.ln_tmp = sb("ln_tmp", [P, 4, NT])
        self.eps = sb("eps", [P, 1])
        self.gathered = [self.sem(f"gathered{u}", ctx) for u in range(RING)]
        self.scattered = [self.sem(f"scattered{u}", ctx) for u in range(RING)]
        self.laps = 0
        self.xn_rows = nc.dram_tensor("xn_rows", (N, D), F32, kind="Internal").ap()
        self.y_rows = nc.dram_tensor("y_rows", (TOP_K * N, D), F32, kind="Internal").ap()

    def sbuf(self, name, shape, dtype=F32, ctx=None):
        return (ctx or self.ctx).enter_context(self.nc.sbuf_tensor(name, shape, dtype))

    def psum(self, name, shape, ctx):
        return ctx.enter_context(self.nc.psum_tensor(name, shape, F32))

    def sem(self, name, ctx):
        if not any(ctx is c for c, _ in self.counting):
            numbers = []
            self.counting.append((ctx, numbers))
            ctx.callback(self.zero, numbers)
        handle = ctx.enter_context(self.nc.semaphore(name))
        [numbers for c, numbers in self.counting if c is ctx][0].append(handle.num)
        return handle

    def counters(self, names, prefix, ctx):
        found = {n: Counter(self.sem(f"{prefix}_{n}", ctx)) for n in names.split()}
        with self.nc.Block() as block:
            @block.sync
            def _(sp):
                for c in found.values():
                    sp.sem_inc(c.sem, Counter.LEAD)
        return found

    def zero(self, numbers):
        self.counting.pop()
        with self.nc.Block() as block:
            @block.sync
            def _(sp):
                left = sorted(numbers)
                while left:
                    n = next((k for k in range(len(left)) if left[k] != left[0] + k), len(left))
                    sp.sem_clear(range(left[0], left[0] + n))
                    left = left[n:]


def load_inputs(net, ctx):
    nc = net.nc
    loaded, made = net.sem("x_loaded", ctx), net.sem("ident_made", ctx)
    zeros = net.sbuf("zeros", [P, TOP_K * N // (RING * P), D], F32, ctx)
    with nc.Block() as block:
        @block.sync
        def _(sp):
            sp.dma_start(net.x[:, :, :], net.dram["x"].rearrange("(t p) d -> p t d", p=P)).then_inc(loaded, 16)
            sp.wait_ge(loaded, 16)

        @block.gpsimd
        def _(pool):
            pool.memset(net.eps[:, :], LN_EPS)
            pool.memset(net.ident[:, :], 0.0).then_inc(made, 1)
            pool.wait_ge(made, 1)
            pool.affine_select(out=net.ident[:, :], in_=net.ident[:, :], compare_op=ALU.not_equal, fill=1.0,
                               base=0, pattern=[[-1, P]], channel_multiplier=1).then_inc(made, 1)
            pool.memset(zeros[:, :, :], 0.0).then_inc(made, 1)
            pool.wait_ge(made, 3)
            parts = net.y_rows.rearrange("(u p r) d -> u p r d", u=RING, p=P)
            for u in range(RING):
                pool.dma_start(parts[u], zeros[:, :, :]).then_inc(net.scattered[u], 16)
            for u in range(RING):
                pool.wait_ge(net.scattered[u], 16)


def layer_norm_stats(net, name, src=None):
    nc = net.nc
    with ExitStack() as ctx:
        step = net.sem(f"{name}_ln_step", ctx)
        var_ready = net.sem(f"{name}_var_ready", ctx)
        std_ready = net.sem(f"{name}_std_ready", ctx)
        var, std, diff, half = (net.ln_tmp[:, k, :] for k in range(4))
        with nc.Block() as block:
            @block.vector
            def _(dve):
                link = Chain(dve, step)
                if src is not None:
                    with dve.Fori(0, NT // 8) as k:
                        for u in range(8):
                            t = bass.ds(k * 8 + u, 1)
                            last = dve.bn_stats(flat(net.stats[:, t, :]), flat(src[:, t, :]))
                        last.then_inc(step, 1)
                    link.loop_done(NT // 8, 1)
                    dve.wait_ge(step, link.n)
                even, odd = net.stats[:, :, 1], net.stats[:, :, 4]
                link(dve.tensor_tensor(half, even, odd, ALU.add))
                link(dve.tensor_scalar(net.mean[:, :], half, 0.5, None, ALU.mult))
                link(dve.tensor_tensor(diff, even, odd, ALU.subtract))
                link(dve.tensor_tensor(diff, diff, diff, ALU.mult))
                link(dve.tensor_tensor(var, net.stats[:, :, 2], net.stats[:, :, 5], ALU.add))
                link(dve.tensor_scalar(diff, diff, 0.25, None, ALU.mult))
                dve.scalar_tensor_tensor(out=var, in0=var, scalar=1.0 / D, in1=diff,
                                         op0=ALU.mult, op1=ALU.add).then_inc(var_ready, 1)
                dve.wait_ge(std_ready, 1)
                dve.reciprocal(net.rstd[:, :], std).then_inc(step, 1)

            @block.scalar
            def _(act):
                act.wait_ge(var_ready, 1)
                act.activation(std, var, ACT.Sqrt, bias=net.eps[:, 0:1]).then_inc(std_ready, 1)


def mixture(net, name, layer, experts):
    nc, dram = net.nc, net.dram
    two = layer == 0
    choices = TOP_K if two else 1
    tiles = SLOT_TILES_L0 if two else SLOT_TILES_L1
    cols = choices * NT
    rw = D + E if two else E
    pre = f"l{layer}"
    layer_norm_stats(net, name, net.x)
    with ExitStack() as ctx:
        sb = lambda n, s, d=F32: net.sbuf(f"{name}_{n}", s, d, ctx)
        shared_w = sb("shared_w", [P, rw])
        shared_b = sb("shared_b", [P, rw])
        pre_sh = sb("pre_sh", [P, NT, rw])
        mixed = sb("mixed", [P, NT, D]) if two else None
        weight = sb("weight", [P, TOP_K, NT])
        row_of = sb("row_of", [P, tiles], I32)
        back_of = sb("back_of", [P, tiles], I32)
        tile_expert = sb("tile_expert", [1, tiles], I32)

        meet_tokens(net, name, rw, pre_sh, shared_w, shared_b, (f"{pre}_shared_w", f"{pre}_shared_b"), store=True)
        route(net, name, layer, choices, tiles, cols, rw, pre_sh, mixed, weight, row_of, back_of, tile_expert)
        expert_tiles(net, name, tiles, experts, row_of, back_of, tile_expert)
        combine(net, name, layer, choices, mixed, weight)


def pipelined(engine, ahead, behind, steps):
    ahead(0, 0)
    with engine.Fori(0, steps // 2 - 1) as k:
        for u in range(2):
            ahead(k * 2 + (u + 1), 1 - u)
            behind(k * 2 + u, u)
    ahead(steps - 1, 1)
    behind(steps - 2, 0)
    behind(steps - 1, 1)


def meet_tokens(net, name, width, met, weights, bias, sources, store=False, kept=None):
    nc, dram = net.nc, net.dram
    steps = NT // TB
    with ExitStack() as ctx:
        xn = [net.sbuf(f"{name}_xn{u}", [P, TB, D], F32, ctx) for u in range(2)]
        xt = [net.sbuf(f"{name}_xt{u}", [P, S], F32, ctx) for u in range(2)]
        t_ps = [net.psum(f"{name}_t_ps{u}", [P, S], ctx) for u in range(2)]
        m_ps = [net.psum(f"{name}_m_ps{u}", [P, 2, 512], ctx) for u in range(2)]
        w_loaded = net.sem(f"{name}_w_loaded", ctx)
        stored = net.sem(f"{name}_xn_stored", ctx)
        c = net.counters("xn_ready xn_turned xn_free xt_ready met met_kept", name, ctx)
        with nc.Block() as block:
            @block.scalar
            def _(act):
                act.dma_start(weights[:, :], dram[sources[0]]).then_inc(w_loaded, 16)
                if bias is not None:
                    act.dma_start(bias[:, :], dram[sources[1]]).then_inc(w_loaded, 16)

                def copy(n, u):
                    c["xn_turned"].wait(act, n + 1)
                    c["met"].wait(act, n - 1)
                    c["xt_ready"].by(act.activation(xt[u][:, :], t_ps[u][:, :], ACT.Copy))

                pipelined(act, copy, lambda n, u: None, steps)

            @block.vector
            def _(dve):
                def normalise(n, u):
                    if store:
                        c["xn_free"].wait(dve, n - 1)
                    c["xn_turned"].wait(dve, n - 1)
                    for t in range(TB):
                        at = n * TB + t
                        last = dve.tensor_scalar(xn[u][:, t, :], flat(net.x[:, bass.ds(at, 1), :]),
                                                 net.mean[:, bass.ds(at, 1)], net.rstd[:, bass.ds(at, 1)],
                                                 ALU.subtract, ALU.mult)
                    c["xn_ready"].by(last)

                def keep(n, u):
                    c["met"].wait(dve, n + 1)
                    for h in range(2):
                        out = met[:, bass.ds(n * TB + 2 * h, 2), :]
                        ps = m_ps[u][:, h, 0:2 * width].rearrange("p (t w) -> p t w", t=2)
                        last = (dve.tensor_tensor(out, ps, bias[:, :].unsqueeze(1).broadcast_to([P, 2, width]), ALU.add)
                                if bias is not None else dve.tensor_copy(out, ps))
                    c["met_kept"].by(last)

                dve.wait_ge(w_loaded, 32 if bias is not None else 16)
                pipelined(dve, normalise, keep, steps)

            @block.tensor
            def _(pe):
                def turn(n, u):
                    c["xn_ready"].wait(pe, n + 1)
                    c["xt_ready"].wait(pe, n - 1)
                    for t in range(TB):
                        last = pe.transpose(t_ps[u][:, t * P:(t + 1) * P], xn[u][:, t, :], net.ident[:, :])
                    c["xn_turned"].by(last)

                def meet(n, u):
                    c["xt_ready"].wait(pe, n + 1)
                    c["met_kept"].wait(pe, n - 1)
                    for t in range(TB):
                        last = pe.matmul(m_ps[u][:, t // 2, (t % 2) * width:(t % 2 + 1) * width],
                                         xt[u][:, t * P:(t + 1) * P], weights[:, :],
                                         start=True, stop=True, skip_group_check=True)
                    c["met"].by(last)

                pe.wait_ge(w_loaded, 32 if bias is not None else 16)
                pipelined(pe, turn, meet, steps)

            if store:
                @block.sync
                def _(sp):
                    rows = net.xn_rows.rearrange("(n t p) d -> n p t d", t=TB, p=P)
                    with sp.Fori(0, steps // 2) as k:
                        for u in range(2):
                            n = k * 2 + u
                            c["xn_ready"].wait(sp, n + 1)
                            sp.dma_start(rows[bass.ds(n, 1)].rearrange("a p t d -> (a p) t d"), xn[u][:, :, :]
                                         ).then_inc(stored, 16)
                            sp.wait_ge(stored, 16 * n + 16)
                            sp.sem_inc(c["xn_free"].sem, 1)


def route(net, name, layer, choices, tiles, cols, rw, pre_sh, mixed, weight, row_of, back_of, tile_expert):
    nc = net.nc
    two = layer == 0
    G = 8
    with ExitStack() as ctx:
        sb = lambda n, s, d=F32: net.sbuf(f"{name}_{n}", s, d, ctx)
        sem = lambda n: net.sem(f"{name}_{n}", ctx)
        before = sb("before", [P, P])
        ones = sb("ones", [P, P])
        preference = sb("preference", [P, E])
        column = sb("column", [P, P])
        token_id = sb("token_id", [P, cols])
        not_first = sb("not_first", [P, E, NT])
        big = sb("big", [P, NT, E])
        prob = sb("prob", [P, NT, E])
        pick = [sb(f"pick{c}", [P, NT, E]) for c in range(2)]
        chosen = sb("chosen", [P, NT, E])
        best = [sb(f"best{c}", [P, NT]) for c in range(2)]
        row = sb("row", [P, NT])
        by_expert = sb("by_expert", [P, E, NT])
        so_far = sb("so_far", [P, E, NT])
        rank = sb("rank", [P, NT, E])
        counts = sb("counts", [P, 4, E])
        counts_i = sb("counts_i", [P, E], I32)
        slot = sb("slot", [P, choices, NT])
        slot_i = sb("slot_i", [P, 2, cols], I32)
        hi_lo = sb("hi_lo", [P, 2, cols])
        lo_hot = [sb(f"lo_hot{u}", [P, G, P]) for u in range(2)]
        hi_hot = [sb(f"hi_hot{u}", [P, G, tiles]) for u in range(2)]
        ends = sb("ends", [P, tiles, E])
        table = sb("table", [P, 4, tiles])
        cnt_ps = net.psum(f"{name}_cnt_ps", [P, 2, NT * E], ctx)
        tab_ps = net.psum(f"{name}_tab_ps", [P, 512], ctx)
        made, step, exps_ready, logits_ready = sem("r_made"), sem("r_step"), sem("r_exps"), sem("r_logits")
        shared_ready = sem("r_shared")
        chosen_ready, counted, hots_ready, hots_used = sem("r_chosen"), sem("r_counted"), sem("r_hots"), sem("r_used")

        with nc.Block() as block:
            @block.gpsimd
            def _(pool):
                link = Chain(pool, made)
                link(pool.memset(ones[:, :], 1.0))
                link(pool.memset(not_first[:, :, :], 1.0))
                link(pool.memset(not_first[:, :, 0:1], 0.0))
                link(pool.affine_select(out=before[:, :], in_=ones[:, :], compare_op=ALU.is_gt, fill=0.0,
                                        base=0, pattern=[[1, P]], channel_multiplier=-1))
                link(pool.iota(column[:, :], [[1, P]], base=0, channel_multiplier=0,
                               allow_small_or_imprecise_dtypes=True))
                link(pool.iota(preference[:, :], [[-1, E]], base=E, channel_multiplier=0,
                               allow_small_or_imprecise_dtypes=True))
                link(pool.iota(token_id[:, :], [[P, cols]], base=1, channel_multiplier=1,
                               allow_small_or_imprecise_dtypes=True))

            @block.scalar
            def _(act):
                act.wait_ge(logits_ready, 1)
                act.activation(prob[:, :, :], prob[:, :, :], ACT.Exp).then_inc(exps_ready, 1)
                if two:
                    for t in range(0, NT, 8):
                        last = act.activation(mixed[:, t:t + 8, :], pre_sh[:, t:t + 8, 0:D], ACT.Gelu)
                    last.then_inc(shared_ready, 1)
                    act.wait_ge(shared_ready, 1)
                    for t in range(0, NT, 8):
                        act.activation(mixed[:, t:t + 8, :], mixed[:, t:t + 8, :], ACT.Copy, scale=0.5
                                       ).then_inc(shared_ready, 1)

            @block.tensor
            def _(pe):
                pe.wait_ge(made, 7)
                pe.wait_ge(chosen_ready, 1)
                hits = chosen[:, :, :].rearrange("p t e -> p (t e)")
                pe.matmul(cnt_ps[:, 0, :], before[:, :], hits, start=True, stop=True)
                pe.matmul(cnt_ps[:, 1, :], ones[:, :], hits, start=True, stop=True,
                          skip_group_check=True).then_inc(counted, 1)
                for r in range(cols // G):
                    pe.wait_ge(hots_ready, r + 1)
                    for g in range(G):
                        last = pe.matmul(tab_ps[:, 0:tiles], lo_hot[r % 2][:, g, :], hi_hot[r % 2][:, g, :],
                                         start=r == 0 and g == 0, stop=r == cols // G - 1 and g == G - 1)
                    last.then_inc(hots_used, 1)

            @block.vector
            def _(dve):
                link = Chain(dve, step)
                dve.wait_ge(made, 7)
                logits = pre_sh[:, :, rw - E:rw]
                over_e = lambda a: a.unsqueeze(2).broadcast_to([P, NT, E])
                link(dve.tensor_reduce(row[:, :], logits, AX.X, ALU.max))
                dve.tensor_tensor(prob[:, :, :], logits, over_e(row[:, :]), ALU.subtract).then_inc(logits_ready, 1)
                dve.wait_ge(exps_ready, 1)
                link(dve.tensor_reduce(row[:, :], prob[:, :, :], AX.X, ALU.add))
                link(dve.reciprocal(row[:, :], row[:, :]))
                link(dve.tensor_tensor(prob[:, :, :], prob[:, :, :], over_e(row[:, :]), ALU.mult))
                prefer = preference[:, :].unsqueeze(1).broadcast_to([P, NT, E])
                for c in range(choices):
                    link(dve.tensor_reduce(best[c][:, :], prob[:, :, :], AX.X, ALU.max))
                    link(dve.tensor_tensor(big[:, :, :], prob[:, :, :], over_e(best[c][:, :]), ALU.is_equal))
                    link(dve.tensor_tensor(big[:, :, :], big[:, :, :], prefer, ALU.mult))
                    link(dve.tensor_reduce(row[:, :], big[:, :, :], AX.X, ALU.max))
                    link(dve.tensor_tensor(pick[c][:, :, :], big[:, :, :], over_e(row[:, :]), ALU.is_equal))
                    if c + 1 < choices:
                        link(dve.scalar_tensor_tensor(out=prob[:, :, :], in0=pick[c][:, :, :], scalar=-2.0,
                                                      in1=prob[:, :, :], op0=ALU.mult, op1=ALU.add))
                if two:
                    link(dve.tensor_tensor(chosen[:, :, :], pick[0][:, :, :], pick[1][:, :, :], ALU.add))
                else:
                    link(dve.tensor_copy(chosen[:, :, :], pick[0][:, :, :]))
                dve.sem_inc(chosen_ready, 1)
                if two:
                    link(dve.tensor_tensor(row[:, :], best[0][:, :], best[1][:, :], ALU.add))
                    link(dve.reciprocal(row[:, :], row[:, :]))
                    for c in range(2):
                        link(dve.tensor_tensor(weight[:, c, :], best[c][:, :], row[:, :], ALU.mult))
                dve.wait_ge(counted, 1)
                totals = cnt_ps[:, 1, :].rearrange("p (t e) -> p e t", e=E)
                link(dve.tensor_copy(by_expert[:, :, :], totals))
                link(dve.tensor_tensor_scan(so_far[:, :, :].rearrange("p e t -> p (e t)"),
                                            not_first[:, :, :].rearrange("p e t -> p (e t)"),
                                            by_expert[:, :, :].rearrange("p e t -> p (e t)"), 0.0,
                                            ALU.mult, ALU.add))
                link(dve.tensor_copy(counts[:, 0, :], so_far[:, :, NT - 1]))
                link(dve.tensor_tensor(so_far[:, :, :], so_far[:, :, :], by_expert[:, :, :], ALU.subtract))
                link(dve.tensor_tensor(rank[:, :, :], cnt_ps[:, 0, :].rearrange("p (t e) -> p t e", e=E),
                                       so_far[:, :, :].rearrange("p e t -> p t e"), ALU.add))
                if not two:
                    link(dve.tensor_scalar(counts[:, 0, :], counts[:, 0, :], float(CAPACITY), None, ALU.min))
                link(dve.tensor_scalar(counts_i[:, :], counts[:, 0, :], float(P - 1), None, ALU.add))
                link(dve.tensor_scalar(counts_i[:, :], counts_i[:, :], 7, None, ALU.arith_shift_right))
                link(dve.tensor_copy(counts[:, 1, :], counts_i[:, :]))
                link(dve.tensor_tensor_scan(counts[:, 2, :], ones[:, 0:E], counts[:, 1, :], 0.0, ALU.mult, ALU.add))
                link(dve.tensor_tensor(counts[:, 3, :], counts[:, 2, :], counts[:, 1, :], ALU.subtract))
                link(dve.tensor_scalar(counts[:, 3, :], counts[:, 3, :], float(P), None, ALU.mult))
                if not two:
                    link(dve.tensor_tensor(big[:, :, :], rank[:, :, :], pick[0][:, :, :], ALU.mult))
                    link(dve.tensor_reduce(row[:, :], big[:, :, :], AX.X, ALU.add))
                    link(dve.tensor_scalar(weight[:, 1, :], row[:, :], float(CAPACITY), None, ALU.is_lt))
                    link(dve.tensor_tensor(weight[:, 0, :], weight[:, 1, :], best[0][:, :], ALU.mult))
                    link(dve.tensor_scalar(weight[:, 0, :], weight[:, 0, :], 0.5, None, ALU.mult))
                    link(dve.tensor_scalar(weight[:, 1, :], weight[:, 1, :], -FAR_AWAY, FAR_AWAY, ALU.mult, ALU.add))
                link(dve.tensor_tensor(rank[:, :, :], rank[:, :, :],
                                       counts[:, 3, :].unsqueeze(1).broadcast_to([P, NT, E]), ALU.add))
                for c in range(choices):
                    link(dve.tensor_tensor(big[:, :, :], rank[:, :, :], pick[c][:, :, :], ALU.mult))
                    link(dve.tensor_reduce(slot[:, c, :], big[:, :, :], AX.X, ALU.add))
                if not two:
                    link(dve.tensor_tensor(slot[:, 0, :], slot[:, 0, :], weight[:, 1, :], ALU.add))
                flat_slot = slot[:, :, :].rearrange("p c t -> p (c t)")
                link(dve.tensor_copy(slot_i[:, 0, :], flat_slot))
                link(dve.tensor_scalar(slot_i[:, 1, :], slot_i[:, 0, :], P - 1, None, ALU.bitwise_and))
                link(dve.tensor_scalar(slot_i[:, 0, :], slot_i[:, 0, :], 7, None, ALU.arith_shift_right))
                link(dve.tensor_copy(hi_lo[:, :, :], slot_i[:, :, :]))
                for r in range(cols // G):
                    if r >= 2:
                        dve.wait_ge(hots_used, r - 1)
                    for g in range(G):
                        col = r * G + g
                        dve.tensor_scalar(lo_hot[r % 2][:, g, :], column[:, :], hi_lo[:, 1, col:col + 1], None,
                                          ALU.is_equal)
                        last = dve.tensor_scalar(hi_hot[r % 2][:, g, :], column[:, 0:tiles], hi_lo[:, 0, col:col + 1],
                                                 token_id[:, col:col + 1], ALU.is_equal, ALU.mult)
                    last.then_inc(hots_ready, 1)
                link(dve.tensor_tensor(ends[:, :, :], column[:, 0:tiles].unsqueeze(2).broadcast_to([P, tiles, E]),
                                       counts[:, 2, :].unsqueeze(1).broadcast_to([P, tiles, E]), ALU.is_ge))
                link(dve.tensor_reduce(table[:, 0, :], ends[:, :, :], AX.X, ALU.add))
                link(dve.tensor_scalar(tile_expert[:, :], table[0:1, 0, :], float(E - 1), None, ALU.min))
                dve.wait_ge(hots_used, cols // G)
                full = table[:, 1, :]
                link(dve.tensor_scalar(full, tab_ps[:, 0:tiles], 1.0, None, ALU.subtract))
                link(dve.tensor_scalar(table[:, 2, :], full, 0.0, 1.0e6, ALU.is_lt, ALU.mult))
                link(dve.tensor_tensor(back_of[:, :], full, table[:, 2, :], ALU.add))
                link(dve.tensor_scalar(table[:, 2, :], full, float(N), float(-N), ALU.is_ge, ALU.mult))
                link(dve.tensor_tensor(table[:, 3, :], full, table[:, 2, :], ALU.add))
                link(dve.tensor_scalar(row_of[:, :], table[:, 3, :], 0.0, None, ALU.max))


def expert_tiles(net, name, tiles, experts, row_of, back_of, tile_expert):
    nc = net.nc
    R = RING
    trips = tiles // R
    with ExitStack() as ctx:
        sb = lambda n, s, d=F32: net.sbuf(f"{name}_{n}", s, d, ctx)
        xg = [sb(f"xg{u}", [P, D]) for u in range(R)]
        xg_t = [sb(f"xg_t{u}", [P, P]) for u in range(2)]
        wb = [sb(f"wb{u}", [P, EXPERT_W]) for u in range(R)]
        hid = [sb(f"hid{u}", [P, HC, P]) for u in range(2)]
        ys = [sb(f"ys{u}", [P, D]) for u in range(R)]
        row_ix = [sb(f"row_ix{u}", [P, 1], I32) for u in range(R)]
        back_ix = [sb(f"back_ix{u}", [P, 1], I32) for u in range(R)]
        t_ps = [net.psum(f"{name}_gt_ps{u}", [P, 512], ctx) for u in range(2)]
        h_ps = [net.psum(f"{name}_h_ps{u}", [P, HC, P], ctx) for u in range(2)]
        y_ps = [net.psum(f"{name}_y_ps{u}", [P, 512], ctx) for u in range(2)]
        gathered, scattered = net.gathered, net.scattered
        gathered_before, scattered_before = 16 * net.laps, 16 * (net.laps + 1)
        net.laps += trips
        passed = net.sem(f"{name}_passed", ctx)
        c = net.counters("row_ix_ready back_ix_ready turned xt_ready w_ready h_ready act_ready y_ready y_kept",
                         f"{name}_e", ctx)
        with nc.Block() as block:
            @block.gpsimd
            def _(pool):
                def gather(u):
                    pool.indirect_dma_start(xg[u][:, :], None, net.xn_rows,
                                            bass.IndirectOffsetOnAxis(ap=row_ix[u][:, :], axis=0)
                                            ).then_inc(gathered[u], 16)

                def scatter(u):
                    pool.indirect_dma_start(net.y_rows, bass.IndirectOffsetOnAxis(ap=back_ix[u][:, :], axis=0),
                                            ys[u][:, :], None, bounds_check=TOP_K * N - 1, oob_is_err=False
                                            ).then_inc(scattered[u], 16)

                def until(counter, count):
                    counter.wait(pool, count)
                    pool.sem_inc(passed, 1)

                def until_scattered(lap, u):
                    pool.wait_ge(scattered[u], 16 * lap + scattered_before)
                    pool.sem_inc(passed, 1)

                for u in range(R):
                    c["row_ix_ready"].by(pool.tensor_copy(row_ix[u][:, :], row_of[:, u:u + 1]))
                for u in range(R):
                    c["row_ix_ready"].wait(pool, u + 1)
                    gather(u)
                with pool.Fori(0, trips - 1) as k:
                    for u in range(R):
                        j = k * R + u
                        until(c["turned"], j + 1)
                        c["row_ix_ready"].by(pool.tensor_copy(row_ix[u][:, :], row_of[:, bass.ds(j + R, 1)]))
                        until_scattered(k, u)
                        c["back_ix_ready"].by(pool.tensor_copy(back_ix[u][:, :], back_of[:, bass.ds(j, 1)]))
                        until(c["row_ix_ready"], j + (R + 1))
                        gather(u)
                        until(c["back_ix_ready"], j + 1)
                        until(c["y_kept"], j + 1)
                        scatter(u)
                for u in range(R):
                    j = tiles - R + u
                    until_scattered(trips - 1, u)
                    c["back_ix_ready"].by(pool.tensor_copy(back_ix[u][:, :], back_of[:, j:j + 1]))
                    until(c["back_ix_ready"], j + 1)
                    until(c["y_kept"], j + 1)
                    scatter(u)
                for u in range(R):
                    pool.wait_ge(scattered[u], 16 * trips + scattered_before)

            @block.vector
            def _(dve):
                def weights(j, r):
                    e = dve.value_load(tile_expert[0:1, bass.ds(j, 1)], min_val=0, max_val=E - 1)
                    c["w_ready"].by(dve.tensor_copy(wb[r][:, :], flat(experts[:, bass.ds(e, 1), :])))

                def keep(lap, j, r):
                    c["y_ready"].wait(dve, j + 1)
                    dve.wait_ge(scattered[r], 16 * lap + scattered_before)
                    c["y_kept"].by(dve.tensor_tensor(ys[r][:, :], y_ps[r % 2][:, 0:D], wb[r][:, B2_AT:B2_AT + D],
                                                     ALU.add))

                for r in range(R - 1):
                    weights(r, r)
                with dve.Fori(0, trips - 1) as k:
                    for r in range(R):
                        j = k * R + r
                        c["y_kept"].wait(dve, j)
                        weights(j + (R - 1), (r + R - 1) % R)
                        keep(k, j, r)
                for j in range(tiles - R, tiles):
                    if j + R - 1 < tiles:
                        c["y_kept"].wait(dve, j)
                        weights(j + R - 1, (j + R - 1) % R)
                    keep(trips - 1, j, j % R)

            @block.scalar
            def _(act):
                def turn_copy(j, u):
                    c["turned"].wait(act, j + 1)
                    c["h_ready"].wait(act, j - 1)
                    c["xt_ready"].by(act.activation(xg_t[u][:, :], t_ps[u][:, 0:P], ACT.Copy))

                def gelu(j, r):
                    c["h_ready"].wait(act, j + 1)
                    c["y_ready"].wait(act, j - 1)
                    for k in range(HC):
                        last = act.activation(hid[r % 2][:, k, :], h_ps[r % 2][:, k, :], ACT.Gelu,
                                              bias=wb[r][:, B1_AT + k:B1_AT + k + 1])
                    c["act_ready"].by(last)

                turn_copy(0, 0)
                turn_copy(1, 1)
                gelu(0, 0)
                with act.Fori(0, trips - 1) as t:
                    for r in range(R):
                        j = t * R + r
                        turn_copy(j + 2, r % 2)
                        gelu(j + 1, (r + 1) % R)
                for j in range(tiles - R, tiles - 1):
                    if j + 2 < tiles:
                        turn_copy(j + 2, j % 2)
                    gelu(j + 1, (j + 1) % R)

            @block.tensor
            def _(pe):
                def turn(lap, j, r):
                    pe.wait_ge(gathered[r], 16 * lap + (16 + gathered_before))
                    c["xt_ready"].wait(pe, j - 1)
                    c["turned"].by(pe.transpose(t_ps[r % 2][:, 0:P], xg[r][:, :], net.ident[:, :]))

                def hidden(j, r):
                    c["xt_ready"].wait(pe, j + 1)
                    c["w_ready"].wait(pe, j + 1)
                    c["act_ready"].wait(pe, j - 1)
                    for k in range(HC):
                        last = pe.matmul(h_ps[r % 2][:, k, :], wb[r][:, k * P:(k + 1) * P], xg_t[r % 2][:, :],
                                         start=True, stop=True, skip_group_check=True)
                    c["h_ready"].by(last)

                def output(j, r):
                    c["act_ready"].wait(pe, j + 1)
                    c["y_kept"].wait(pe, j - 1)
                    for k in range(HC):
                        last = pe.matmul(y_ps[r % 2][:, 0:D], hid[r % 2][:, k, :],
                                         wb[r][:, W2_AT + k * D:W2_AT + (k + 1) * D], start=k == 0, stop=k == HC - 1)
                    c["y_ready"].by(last)

                turn(0, 0, 0)
                turn(0, 1, 1)
                hidden(0, 0)
                with pe.Fori(0, trips - 1) as t:
                    for r in range(R):
                        j = t * R + r
                        turn(t + (r + 2) // R, j + 2, (r + 2) % R)
                        hidden(j + 1, (r + 1) % R)
                        output(j, r)
                for j in range(tiles - R, tiles):
                    if j + 2 < tiles:
                        turn((j + 2) // R, j + 2, (j + 2) % R)
                    if j + 1 < tiles:
                        hidden(j + 1, (j + 1) % R)
                    output(j, j % R)


def combine(net, name, layer, choices, mixed, weight):
    nc, dram = net.nc, net.dram
    two = layer == 0
    steps, rings = NT // TB, 4
    with ExitStack() as ctx:
        sb = lambda n, s, d=F32: net.sbuf(f"{name}_{n}", s, d, ctx)
        yl = [sb(f"yl{u}", [P, choices, TB, D]) for u in range(rings)]
        norm_w = sb("norm_w", [P, 2, D])
        loaded = [net.sem(f"{name}_y_loaded{u}", ctx) for u in range(rings)]
        w_loaded, halved = net.sem(f"{name}_norm_w_loaded", ctx), net.sem(f"{name}_w_halved", ctx)
        c = net.counters("first_added used beta_added measured", f"{name}_c", ctx)
        rows = net.y_rows.rearrange("(c n t p) d -> n c p t d", c=TOP_K, t=TB, p=P)
        with nc.Block() as block:
            @block.sync
            def _(sp):
                if two:
                    sp.dma_start(norm_w[:, :, :], dram["l0_norm_w"]).then_inc(w_loaded, 16)
                for n in range(steps):
                    u = n % rings
                    c["used"].wait(sp, n + 1 - rings)
                    for k in range(choices):
                        sp.dma_start(yl[u][:, k, :, :], rows[n, k]).then_inc(loaded[u], 16)

            if two:
                @block.gpsimd
                def _(pool):
                    pool.wait_ge(w_loaded, 16)
                    pool.tensor_scalar(norm_w[:, :, :], norm_w[:, :, :], 0.5, None, ALU.mult).then_inc(halved, 1)
                    pool.wait_ge(halved, 1)
                    c["beta_added"].by(pool.tensor_tensor(net.x[:, :, :], net.x[:, :, :], norm_w[:, 1, :].unsqueeze(1)
                                                          .broadcast_to([P, NT, D]), ALU.add))

            @block.vector
            def _(dve):
                for n in range(steps):
                    u = n % rings
                    dve.wait_ge(loaded[u], 16 * choices * (n // rings + 1))
                    tiles = range(n * TB, (n + 1) * TB)
                    if not two:
                        for t in tiles:
                            last = dve.scalar_tensor_tensor(
                                out=net.x[:, t, :], in0=yl[u][:, 0, t % TB, :], scalar=weight[:, 0, t:t + 1],
                                in1=net.x[:, t, :], op0=ALU.mult, op1=ALU.add)
                        c["used"].by(last)
                        continue
                    for t in tiles:
                        last = dve.scalar_tensor_tensor(
                            out=mixed[:, t, :], in0=yl[u][:, 0, t % TB, :], scalar=weight[:, 0, t:t + 1],
                            in1=mixed[:, t, :], op0=ALU.mult, op1=ALU.add)
                    c["first_added"].by(last)
                    c["first_added"].wait(dve, n + 1)
                    for t in tiles:
                        last = dve.scalar_tensor_tensor(
                            out=mixed[:, t, :], in0=yl[u][:, 1, t % TB, :], scalar=weight[:, 1, t:t + 1],
                            in1=mixed[:, t, :], op0=ALU.mult, op1=ALU.add)
                    c["used"].by(last)
                    c["used"].wait(dve, n + 1)
                    for t in tiles:
                        last = dve.bn_stats(net.stats[:, t, :], mixed[:, t, :])
                    c["measured"].by(last)
                c["used"].wait(dve, steps)
                if two:
                    c["measured"].wait(dve, steps)
                    c["beta_added"].wait(dve, 1)
        if two:
            add_normalised(net, name, mixed, norm_w)


def add_normalised(net, name, mixed, norm_w):
    nc = net.nc
    layer_norm_stats(net, f"{name}_out")
    with ExitStack() as ctx:
        centred, added = (net.sem(f"{name}_{n}", ctx) for n in ("centred", "added"))
        with nc.Block() as block:
            @block.vector
            def _(dve):
                def centre(n):
                    for t in range(n * TB, (n + 1) * TB):
                        last = dve.scalar_tensor_tensor(
                            out=mixed[:, t, :], in0=mixed[:, t, :], scalar=net.mean[:, t:t + 1], in1=norm_w[:, 0, :],
                            op0=ALU.subtract, op1=ALU.mult)
                    last.then_inc(centred, 1)

                def add(n):
                    dve.wait_ge(centred, n + 1)
                    for t in range(n * TB, (n + 1) * TB):
                        last = dve.scalar_tensor_tensor(
                            out=net.x[:, t, :], in0=mixed[:, t, :], scalar=net.rstd[:, t:t + 1], in1=net.x[:, t, :],
                            op0=ALU.mult, op1=ALU.add)
                    last.then_inc(added, 1)

                centre(0)
                for n in range(NT // TB):
                    if n + 1 < NT // TB:
                        centre(n + 1)
                    add(n)


def mamba(net):
    nc, dram = net.nc, net.dram
    layer_norm_stats(net, "mb", net.x)
    with ExitStack() as ctx:
        sb = lambda n, s, d=F32: net.sbuf(f"mb_{n}", s, d, ctx)
        sem = lambda n: net.sem(f"mb_{n}", ctx)
        w_in = sb("w_in", [P, 2 * DI])
        w_out = sb("w_out", [P, IC, D])
        w_b = sb("w_b", [P, IC, DS])
        w_c = sb("w_c", [DS, DI])
        conv_w = sb("conv_w", [P, IC, DC])
        conv_b = sb("conv_b", [P, IC])
        keep = sb("keep", [DS, S])
        xn = [sb(f"xn{u}", [P, TB, D]) for u in range(2)]
        xt = [sb(f"xt{u}", [P, S]) for u in range(2)]
        xp = [sb(f"xp{u}", [P, IC, S + DC - 1]) for u in range(2)]
        conv = [sb(f"conv{u}", [P, IC, S]) for u in range(2)]
        xc = [sb(f"xc{u}", [P, IC, S]) for u in range(2)]
        gate = [sb(f"gate{u}", [P, IC, S]) for u in range(2)]
        taken = [sb(f"taken{u}", [DS, S]) for u in range(2)]
        state = [sb(f"state{u}", [DS, S]) for u in range(2)]
        gated = [sb(f"gated{u}", [P, IC, S]) for u in range(2)]
        t_ps = net.psum("mb_t_ps", [P, S], ctx)
        z_ps = net.psum("mb_z_ps", [P, 2 * IC, S], ctx)
        u_ps = net.psum("mb_u_ps", [P, S], ctx)
        y_ps = net.psum("mb_y_ps", [P, IC, S], ctx)
        w_loaded, padded, xn_ready, turned, xt_ready = (sem(n) for n in ("w_loaded", "padded", "xn_ready", "turned", "xt_ready"))
        xz_ready, xp_ready, conv_step, conv_ready, xc_ready = (sem(n) for n in ("xz_ready", "xp_ready", "conv_step", "conv_ready", "xc_ready"))
        gate_ready, u_ready, taken_ready, state_ready = (sem(n) for n in ("gate_ready", "u_ready", "taken_ready", "state_ready"))
        y_ready, gated_ready, o_ready, added = (sem(n) for n in ("y_ready", "gated_ready", "o_ready", "added"))
        loads = [(w_in, "w_in"), (w_out, "w_out"), (w_b, "w_b"), (w_c, "w_c"), (conv_w, "conv_w"), (conv_b, "conv_b")]
        with nc.Block() as block:
            @block.sync
            def _(sp):
                for dst, src in loads:
                    sp.dma_start(dst[:], dram[src]).then_inc(w_loaded, 16)

            @block.gpsimd
            def _(pool):
                for u in range(2):
                    pool.memset(xp[u][:, :, 0:DC - 1], 0.0).then_inc(padded, 1)
                pool.memset(keep[:, :], KEEP).then_inc(padded, 1)

            @block.vector
            def _(dve):
                dve.wait_ge(w_loaded, 16 * len(loads))
                dve.wait_ge(padded, 3)
                with dve.Fori(0, B // 2) as k:
                    for u in range(2):
                        b = k * 2 + u
                        dve.wait_ge(turned, b)
                        for t in range(TB):
                            at = b * TB + t
                            dve.tensor_scalar(xn[u][:, t, :], flat(net.x[:, bass.ds(at, 1), :]),
                                              net.mean[:, bass.ds(at, 1)], net.rstd[:, bass.ds(at, 1)],
                                              ALU.subtract, ALU.mult).then_inc(xn_ready, 1)
                        dve.wait_ge(xp_ready, b + 1)
                        for c in range(IC):
                            for j in range(DC):
                                if j == 0:
                                    ins = dve.tensor_scalar(conv[u][:, c, :], xp[u][:, c, 0:S], conv_w[:, c, 0:1],
                                                            None, ALU.mult)
                                else:
                                    ins = dve.scalar_tensor_tensor(
                                        out=conv[u][:, c, :], in0=xp[u][:, c, j:j + S], scalar=conv_w[:, c, j:j + 1],
                                        in1=conv[u][:, c, :], op0=ALU.mult, op1=ALU.add)
                                if j < DC - 1:
                                    ins.then_inc(conv_step, 1)
                                    dve.wait_ge(conv_step, b * (IC * (DC - 1)) + (c * (DC - 1) + j + 1))
                            ins.then_inc(conv_ready, 1)
                        dve.wait_ge(taken_ready, b + 1)
                        dve.tensor_tensor_scan(state[u][:, :], keep[:, :], taken[u][:, :], 0.0,
                                               ALU.mult, ALU.add).then_inc(state_ready, 1)
                        dve.wait_ge(gate_ready, b + 1)
                        dve.wait_ge(y_ready, b + 1)
                        dve.tensor_tensor(gated[u][:, :, :], y_ps[:, :, :], gate[u][:, :, :],
                                          ALU.mult).then_inc(gated_ready, 1)
                        dve.wait_ge(o_ready, b + 1)
                        rows = net.x[:, bass.ds(b * TB, TB), :]
                        dve.tensor_tensor(rows, rows, y_ps[:, 0, :].rearrange("p (t d) -> p t d", t=TB),
                                          ALU.add).then_inc(added, 1)

            @block.scalar
            def _(act):
                with act.Fori(0, B // 2) as k:
                    for u in range(2):
                        b = k * 2 + u
                        act.wait_ge(turned, b + 1)
                        act.activation(xt[u][:, :], t_ps[:, :], ACT.Copy).then_inc(xt_ready, 1)
                        act.wait_ge(xz_ready, b + 1)
                        act.activation(xp[u][:, :, DC - 1:], z_ps[:, 0:IC, :], ACT.Copy).then_inc(xp_ready, 1)
                        act.activation(gate[u][:, :, :], z_ps[:, IC:, :], ACT.Silu).then_inc(gate_ready, 1)
                        for c in range(IC):
                            act.wait_ge(conv_ready, b * IC + (c + 1))
                            act.activation(xc[u][:, c, :], conv[u][:, c, :], ACT.Silu,
                                           bias=conv_b[:, c:c + 1]).then_inc(xc_ready, 1)
                        act.wait_ge(u_ready, b + 1)
                        act.activation(taken[u][:, :], u_ps[0:DS, :], ACT.Copy, scale=TAKE).then_inc(taken_ready, 1)

            @block.tensor
            def _(pe):
                pe.wait_ge(w_loaded, 16 * len(loads))
                with pe.Fori(0, B // 2) as k:
                    for u in range(2):
                        b = k * 2 + u
                        pe.wait_ge(xt_ready, b)
                        for t in range(TB):
                            pe.wait_ge(xn_ready, b * TB + (t + 1))
                            last = pe.transpose(t_ps[:, t * P:(t + 1) * P], xn[u][:, t, :], net.ident[:, :])
                        last.then_inc(turned, 1)
                        pe.wait_ge(xt_ready, b + 1)
                        pe.wait_ge(gate_ready, b)
                        for c in range(2 * IC):
                            last = pe.matmul(z_ps[:, c, :], w_in[:, c * P:(c + 1) * P], xt[u][:, :],
                                             start=True, stop=True)
                        last.then_inc(xz_ready, 1)
                        for c in range(IC):
                            pe.wait_ge(xc_ready, b * IC + (c + 1))
                            last = pe.matmul(u_ps[0:DS, :], w_b[:, c, :], xc[u][:, c, :],
                                             start=c == 0, stop=c == IC - 1)
                        last.then_inc(u_ready, 1)
                        pe.wait_ge(state_ready, b + 1)
                        pe.wait_ge(added, b)
                        for c in range(IC):
                            last = pe.matmul(y_ps[:, c, :], w_c[:, c * P:(c + 1) * P], state[u][:, :],
                                             start=True, stop=True)
                        last.then_inc(y_ready, 1)
                        pe.wait_ge(gated_ready, b + 1)
                        for t in range(TB):
                            for c in range(IC):
                                last = pe.matmul(y_ps[:, 0, t * P:(t + 1) * P], gated[u][:, c, t * P:(t + 1) * P],
                                                 w_out[:, c, :], start=c == 0, stop=c == IC - 1,
                                                 skip_group_check=True)
                        last.then_inc(o_ready, 1)


def power_attention(net):
    nc, dram = net.nc, net.dram
    layer_norm_stats(net, "pa", net.x)
    with ExitStack() as ctx:
        sb = lambda n, s, d=F32: net.sbuf(f"pa_{n}", s, d, ctx)
        sem = lambda n: net.sem(f"pa_{n}", ctx)
        w_g = sb("w_group", [P, KV, GROUP_W])
        w_gate = sb("w_gate", [P, KV])
        w_proj = sb("w_proj", [P, KV, D])
        ln_w = sb("ln_w", [P, 1])
        v_mean = sb("v_mean", [P, KV])
        rope_c = sb("rope_c", [P, TB, ROPE_W])
        rope_s = sb("rope_s", [P, TB, ROPE_W])
        select = sb("select", [KV, KV, P])
        ident_b = sb("ident_b", [P, P], BF16)
        mask_b = sb("mask_b", [P, P], BF16)
        one = sb("one", [P, S])
        score_min = sb("score_min", [P, 1])
        head_eps = sb("head_eps", [P, 1])
        xn = sb("xn", [P, TB, D])
        xt = sb("xt", [P, S])
        gate_x = sb("gate_x", [KV, S])
        gate_e = sb("gate_e", [KV, S])
        gate_sum = sb("gate_sum", [KV, S])
        neg_gate = sb("neg_gate", [P, TB, KV])
        rope_a = sb("rope_a", [P, TB, ROPE_W])
        rope_b = sb("rope_b", [P, TB, ROPE_W])
        qk = [sb(f"qk{u}", [P, TB, QW + 2 * KW]) for u in range(2)]
        q_t = [sb(f"q_t{u}", [P, S]) for u in range(2)]
        k_t = [sb(f"k_t{u}", [P, S]) for u in range(2)]
        v = [sb(f"v{u}", [P, TB, HD + 1]) for u in range(2)]
        decay = [sb(f"decay{u}", [P, SCORE_W]) for u in range(2)]
        a = [sb(f"a{u}", [P, SCORE_W]) for u in range(2)]
        top = sb("top", [P, S])
        top_row = sb("top_row", [P, TB])
        den = sb("den", [P, TB])
        y = [sb(f"y{u}", [P, TB, RATIO, HD]) for u in range(2)]
        y_sq = sb("y_sq", [P, TB, HD])
        sq_sum = sb("sq_sum", [P, TB, RATIO])
        y_rstd = [sb(f"y_rstd{u}", [P, TB, RATIO]) for u in range(2)]
        y_t = sb("y_t", [P, KV, S])
        s_ps = net.psum("pa_s_ps", [P, 3 * S], ctx)
        p_ps = net.psum("pa_p_ps", [P, TB, GROUP_W], ctx)
        o_ps = net.psum("pa_o_ps", [P, S], ctx)
        t_ps = net.psum("pa_t_ps", [P, S], ctx)
        g_ps = net.psum("pa_g_ps", [P, S], ctx)
        o_view = o_ps[:, 0:TB * (HD + 1)].rearrange("p (t d) -> p t d", t=TB)
        names = ("w_loaded made prepared setup xn_ready x_turned xt_ready gate_z gate_x gate_na gate_exp gate_ln gate_log "
                 "gate_sum gate_passed gate_turned neg_gate projected rope_ab roped v_ready q_turned q_ready k_turned k_ready "
                 "spread decay_off masked decay_ready scored squared weighed topped_step topped top_turned top_read "
                 "valued den_step den_ready y_raw y_squared sq_summed y_ln y_rstd y_ready y_turned y_copied out_ready added")
        m = {n: sem(n) for n in names.split()}
        loads = [(w_g, "w_group"), (w_gate, "w_gate"), (w_proj, "w_proj"), (ln_w, "ln_w"),
                 (rope_c, "rope_c"), (rope_s, "rope_s"), (select, "select")]

        with nc.Block() as block:
            @block.sync
            def _(sp):
                for dst, src in loads:
                    sp.dma_start(dst[:], dram[src]).then_inc(m["w_loaded"], 16)

            @block.gpsimd
            def _(pool):
                link = Chain(pool, m["made"])
                link(pool.memset(one[:, :], 1.0))
                link(pool.memset(score_min[:, :], SCORE_SCALE * SCORE_MIN))
                link(pool.memset(head_eps[:, :], HEAD_EPS))
                for u in range(2):
                    link(pool.memset(v[u][:, :, HD:], 1.0))
                link(pool.memset(mask_b[:, :], 0.0))
                link(pool.affine_select(out=mask_b[:, :], in_=mask_b[:, :], compare_op=ALU.is_ge, fill=MASKED,
                                        base=0, pattern=[[1, P]], channel_multiplier=-1))

            @block.vector
            def _(dve):
                link = Chain(dve, m["prepared"])
                link(dve.tensor_copy(ident_b[:, :], net.ident[:, :]))
                dve.wait_ge(m["w_loaded"], 16 * len(loads))
                values = w_g[:, :, ROPE_W:]
                link(dve.tensor_reduce(v_mean[:, :], values, AX.X, ALU.add))
                link(dve.tensor_scalar(v_mean[:, :], v_mean[:, :], 1.0 / HD, None, ALU.mult))
                link(dve.tensor_tensor(values, values, v_mean[:, :].unsqueeze(2).broadcast_to([P, KV, HD]), ALU.subtract))
                link(dve.tensor_scalar(w_proj[:, :, :], w_proj[:, :, :], ln_w[:, 0:1], None, ALU.mult))

        with nc.Block() as block:
            @block.vector
            def _(dve):
                with dve.Fori(0, B) as b:
                    def rope(g):
                        dve.wait_ge(m["projected"], b * KV + (g + 1))
                        dve.wait_ge(m["v_ready"], b * KV + (g + 1))
                        dve.wait_ge(m["roped"], b * KV + g)
                        pairs = lambda ap: ap.rearrange("p t (h two) -> p t h two", two=2)
                        dve.tensor_tensor(rope_a[:, :, :], p_ps[:, :, 0:ROPE_W], rope_c[:, :, :],
                                          ALU.mult).then_inc(m["rope_ab"], 1)
                        dve.tensor_tensor(pairs(rope_b[:, :, :]), pairs(p_ps[:, :, 0:ROPE_W])[:, :, :, ::-1],
                                          pairs(rope_s[:, :, :]), ALU.mult).then_inc(m["rope_ab"], 1)

                    def weigh(g, u):
                        n = b * (2 * KV) + (2 * g + u + 1)
                        dve.wait_ge(m["squared"], n)
                        dve.wait_ge(m["decay_ready"], b * KV + (g + 1))
                        dve.tensor_tensor(a[u][:, :], a[u][:, :], decay[g % 2][:, :], ALU.mult).then_inc(m["weighed"], 1)

                    def largest(g, u):
                        n = b * (2 * KV) + (2 * g + u)
                        dve.wait_ge(m["weighed"], n + 1)
                        dve.wait_ge(m["top_turned"], n)
                        at = lambda i: a[u][:, block_at(i, i):block_at(i, i) + (TB - i) * P]
                        dve.tensor_tensor(top[:, P:], a[u][:, P:S], at(1), ALU.max).then_inc(m["topped_step"], 1)
                        dve.wait_ge(m["topped_step"], 2 * n + 1)
                        dve.tensor_tensor(top[:, 2 * P:], top[:, 2 * P:], at(2), ALU.max).then_inc(m["topped_step"], 1)
                        dve.wait_ge(m["topped_step"], 2 * n + 2)
                        dve.tensor_tensor(top[:, 3 * P:], top[:, 3 * P:], at(3), ALU.max).then_inc(m["topped"], 1)

                    def divide(g, u):
                        n = b * (2 * KV) + (2 * g + u)
                        dve.wait_ge(m["top_turned"], n + 1)
                        dve.tensor_reduce(top_row[:, :], t_ps[:, :].rearrange("p (t s) -> p t s", t=TB), AX.X,
                                          ALU.max).then_inc(m["top_read"], 1)
                        dve.wait_ge(m["top_read"], n + 1)
                        dve.wait_ge(m["valued"], n + 1)
                        dve.scalar_tensor_tensor(out=den[:, :], in0=top_row[:, :], scalar=DEN_EPS, in1=o_view[:, :, HD],
                                                 op0=ALU.mult, op1=ALU.add).then_inc(m["den_step"], 1)
                        dve.wait_ge(m["den_step"], n + 1)
                        dve.reciprocal(den[:, :], den[:, :]).then_inc(m["den_ready"], 1)
                        dve.wait_ge(m["den_ready"], n + 1)
                        if u == 0:
                            dve.wait_ge(m["y_turned"], max(g - 1, 0) + b * KV)
                        dve.tensor_tensor(y[g % 2][:, :, u, :], o_view[:, :, 0:HD],
                                          den[:, :].unsqueeze(2).broadcast_to([P, TB, HD]), ALU.mult).then_inc(m["y_raw"], 1)

                    def sum_squares(g, u):
                        n = b * (2 * KV) + (2 * g + u)
                        dve.wait_ge(m["y_squared"], n + 1)
                        dve.wait_ge(m["y_ln"], b * KV + g)
                        dve.tensor_reduce(sq_sum[:, :, u], y_sq[:, :, :], AX.X, ALU.add).then_inc(m["sq_summed"], 1)

                    for t in range(TB):
                        at = b * TB + t
                        dve.wait_ge(m["x_turned"], b)
                        dve.tensor_scalar(xn[:, t, :], flat(net.x[:, bass.ds(at, 1), :]), net.mean[:, bass.ds(at, 1)],
                                          net.rstd[:, bass.ds(at, 1)], ALU.subtract, ALU.mult).then_inc(m["xn_ready"], 1)
                    dve.wait_ge(m["gate_z"], b + 1)
                    dve.tensor_scalar(gate_x[:, :], g_ps[0:KV, :], GATE_BIAS, None, ALU.add).then_inc(m["gate_x"], 1)
                    dve.wait_ge(m["gate_x"], b + 1)
                    dve.scalar_tensor_tensor(out=gate_e[:, :], in0=gate_x[:, :], scalar=-1.0, in1=gate_x[:, :],
                                             op0=ALU.mult, op1=ALU.min).then_inc(m["gate_na"], 1)
                    dve.wait_ge(m["gate_ln"], b + 1)
                    dve.scalar_tensor_tensor(out=gate_x[:, :], in0=gate_x[:, :], scalar=0.0, in1=gate_e[:, :],
                                             op0=ALU.min, op1=ALU.subtract).then_inc(m["gate_log"], 1)
                    dve.wait_ge(m["gate_log"], b + 1)
                    dve.tensor_tensor_scan(gate_sum[:, :], one[0:KV, :], gate_x[:, :], 0.0,
                                           ALU.mult, ALU.add).then_inc(m["gate_sum"], 1)
                    dve.wait_ge(m["gate_turned"], b + 1)
                    dve.tensor_scalar(neg_gate[:, :, :].rearrange("p t g -> p (t g)"), g_ps[:, 0:TB * KV], -1.0, None,
                                      ALU.mult).then_inc(m["neg_gate"], 1)
                    rope(0)
                    for g in range(KV):
                        weigh(g, 0)
                        if g + 1 < KV:
                            rope(g + 1)
                        largest(g, 0)
                        weigh(g, 1)
                        divide(g, 0)
                        largest(g, 1)
                        sum_squares(g, 0)
                        divide(g, 1)
                        sum_squares(g, 1)
                    dve.wait_ge(m["out_ready"], b + 1)
                    rows = net.x[:, bass.ds(b * TB, TB), :]
                    dve.tensor_tensor(rows, rows, g_ps[:, :].rearrange("p (t d) -> p t d", t=TB),
                                      ALU.add).then_inc(m["added"], 1)

            @block.gpsimd
            def _(pool):
                with pool.Fori(0, B) as b:
                    def add_up(g):
                        pool.wait_ge(m["rope_ab"], b * (2 * KV) + (2 * g + 2))
                        pool.wait_ge(m["k_turned"], b * KV + max(g - 1, 0))
                        pool.tensor_tensor(qk[g % 2][:, :, ROPE_W:], rope_a[:, :, QW:], rope_b[:, :, QW:],
                                           ALU.add)
                        pool.tensor_tensor(qk[g % 2][:, :, 0:ROPE_W], rope_a[:, :, :], rope_b[:, :, :],
                                           ALU.add).then_inc(m["roped"], 1)

                    def scale(g):
                        pool.wait_ge(m["y_rstd"], b * KV + (g + 1))
                        pool.tensor_tensor(y[g % 2][:, :, :, :].rearrange("p t u d -> p (t u) d"),
                                           y[g % 2][:, :, :, :].rearrange("p t u d -> p (t u) d"),
                                           y_rstd[g % 2][:, :, :].rearrange("p t u -> p (t u)").unsqueeze(2)
                                           .broadcast_to([P, TB * RATIO, HD]), ALU.mult).then_inc(m["y_ready"], 1)

                    add_up(0)
                    for g in range(KV):
                        if g >= 1:
                            scale(g - 1)
                        if g + 1 < KV:
                            add_up(g + 1)
                    scale(KV - 1)

            @block.scalar
            def _(act):
                with act.Fori(0, B) as b:
                    def square(g, u):
                        n = b * (2 * KV) + (2 * g + u)
                        act.wait_ge(m["scored"], n + 1)
                        act.wait_ge(m["top_turned"], b * (2 * KV) + max(2 * g + u - 1, 0))
                        act.wait_ge(m["valued"], b * (2 * KV) + max(2 * g + u - 1, 0))
                        act.activation(a[u][:, :], s_ps[:, 0:SCORE_W], ACT.Square, bias=score_min[:, 0:1],
                                       scale=SCORE_SCALE * HD ** -0.5).then_inc(m["squared"], 1)

                    def keep_v(g):
                        act.wait_ge(m["projected"], b * KV + (g + 1))
                        act.wait_ge(m["valued"], b * (2 * KV) + max(2 * g - 2, 0))
                        act.activation(v[g % 2][:, :, 0:HD], p_ps[:, :, ROPE_W:], ACT.Copy).then_inc(m["v_ready"], 1)

                    def decay_off(g):
                        act.wait_ge(m["spread"], b * KV + (g + 1))
                        act.wait_ge(m["neg_gate"], b + 1)
                        act.wait_ge(m["weighed"], b * (2 * KV) + max(2 * g - 2, 0))
                        for i in range(TB - 1):
                            at = block_at(i, i + 1)
                            last = act.activation(decay[g % 2][:, at:at + (TB - 1 - i) * P], g_ps[:, (i + 1) * P:],
                                                  ACT.Exp, bias=neg_gate[:, i, g:g + 1])
                        last.then_inc(m["decay_off"], 1)

                    def decay_diagonal(g):
                        act.wait_ge(m["masked"], b * KV + (g + 1))
                        for i in range(TB):
                            at = block_at(i, i)
                            last = act.activation(decay[g % 2][:, at:at + P], g_ps[:, i * P:(i + 1) * P],
                                                  ACT.Exp, bias=neg_gate[:, i, g:g + 1])
                        last.then_inc(m["decay_ready"], 1)

                    def copy_qk(g):
                        act.wait_ge(m["q_turned"], b * KV + (g + 1))
                        act.wait_ge(m["scored"], b * (2 * KV) + max(2 * g - 2, 0))
                        act.activation(q_t[g % 2][:, :], t_ps[:, :], ACT.Copy).then_inc(m["q_ready"], 1)
                        act.wait_ge(m["k_turned"], b * KV + (g + 1))
                        act.activation(k_t[g % 2][:, :], t_ps[:, :], ACT.Copy).then_inc(m["k_ready"], 1)

                    def square_y(g, u):
                        n = b * (2 * KV) + (2 * g + u)
                        act.wait_ge(m["y_raw"], n + 1)
                        act.wait_ge(m["sq_summed"], n)
                        act.activation(y_sq[:, :, :], y[g % 2][:, :, u, :], ACT.Square).then_inc(m["y_squared"], 1)

                    def inverse_root(g):
                        act.wait_ge(m["sq_summed"], b * (2 * KV) + (2 * g + 2))
                        act.wait_ge(m["y_ready"], b * KV + max(g - 1, 0))
                        act.activation(y_rstd[g % 2][:, :, :], sq_sum[:, :, :], ACT.Ln, bias=head_eps[:, 0:1],
                                       scale=1.0 / HD).then_inc(m["y_ln"], 1)
                        act.wait_ge(m["y_ln"], b * KV + (g + 1))
                        act.activation(y_rstd[g % 2][:, :, :], y_rstd[g % 2][:, :, :], ACT.Exp,
                                       scale=-0.5).then_inc(m["y_rstd"], 1)

                    def copy_y(g):
                        act.wait_ge(m["y_turned"], b * KV + (g + 1))
                        act.activation(y_t[:, g, :], t_ps[:, :], ACT.Copy).then_inc(m["y_copied"], 1)

                    act.wait_ge(m["x_turned"], b + 1)
                    act.activation(xt[:, :], g_ps[:, :], ACT.Copy).then_inc(m["xt_ready"], 1)
                    act.wait_ge(m["gate_na"], b + 1)
                    act.activation(gate_e[:, :], gate_e[:, :], ACT.Exp).then_inc(m["gate_exp"], 1)
                    act.wait_ge(m["gate_exp"], b + 1)
                    act.activation(gate_e[:, :], gate_e[:, :], ACT.Ln, bias=one[0:KV, 0:1]).then_inc(m["gate_ln"], 1)
                    keep_v(0)
                    decay_off(0)
                    decay_diagonal(0)
                    copy_qk(0)
                    for g in range(KV):
                        square(g, 0)
                        if g >= 1:
                            inverse_root(g - 1)
                        if g + 1 < KV:
                            keep_v(g + 1)
                        square(g, 1)
                        if g >= 1:
                            copy_y(g - 1)
                        if g + 1 < KV:
                            decay_off(g + 1)
                        square_y(g, 0)
                        if g + 1 < KV:
                            decay_diagonal(g + 1)
                            copy_qk(g + 1)
                        square_y(g, 1)
                    inverse_root(KV - 1)
                    copy_y(KV - 1)

            @block.tensor
            def _(pe):
                with pe.Fori(0, B) as b:
                    def t_ps_free(tops, qs, ys):
                        pe.wait_ge(m["top_read"], b * (2 * KV) + tops)
                        pe.wait_ge(m["k_ready"], b * KV + qs)
                        pe.wait_ge(m["y_copied"], b * KV + ys)

                    def project(g):
                        pe.wait_ge(m["rope_ab"], b * (2 * KV) + 2 * g)
                        pe.wait_ge(m["v_ready"], b * KV + g)
                        for t in range(TB):
                            last = pe.matmul(p_ps[:, t, :], xt[:, t * P:(t + 1) * P], w_g[:, g, :],
                                             start=True, stop=True, skip_group_check=True)
                        last.then_inc(m["projected"], 1)

                    def turn_qk(g, tops, ys):
                        pe.wait_ge(m["roped"], b * KV + (g + 1))
                        t_ps_free(tops, g, ys)
                        for t in range(TB):
                            last = pe.transpose(t_ps[:, t * P:(t + 1) * P], qk[g % 2][:, t, 0:QW], net.ident[:, :])
                        last.then_inc(m["q_turned"], 1)
                        pe.wait_ge(m["q_ready"], b * KV + (g + 1))
                        for t in range(TB):
                            last = pe.transpose(t_ps[:, t * P:(t + 1) * P], qk[g % 2][:, t, QW:], net.ident[:, :])
                        last.then_inc(m["k_turned"], 1)

                    def spread(g):
                        pe.wait_ge(m["decay_ready"], b * KV + g)
                        pe.matmul(g_ps[:, :], select[:, g, :], gate_sum[:, :], start=True, stop=False,
                                  skip_group_check=True).then_inc(m["spread"], 1)

                    def mask(g):
                        pe.wait_ge(m["decay_off"], b * KV + (g + 1))
                        pe.matmul(g_ps[:, :].rearrange("p (t s) -> p t s", t=TB), ident_b[:, :],
                                  mask_b[:, :].unsqueeze(1).broadcast_to([P, TB, P]), start=False, stop=True,
                                  skip_group_check=True).then_inc(m["masked"], 1)

                    def score(g, u):
                        n = b * (2 * KV) + (2 * g + u)
                        pe.wait_ge(m["k_ready"], b * KV + (g + 1))
                        pe.wait_ge(m["squared"], n)
                        rows = slice(u * HD, (u + 1) * HD)
                        for i in range(TB):
                            at = block_at(i, i)
                            last = pe.matmul(s_ps[:, at:at + (TB - i) * P], k_t[g % 2][rows, i * P:(i + 1) * P],
                                             q_t[g % 2][rows, i * P:], start=True, stop=True, skip_group_check=True)
                        last.then_inc(m["scored"], 1)

                    def value(g, u):
                        n = b * (2 * KV) + (2 * g + u)
                        pe.wait_ge(m["weighed"], n + 1)
                        pe.wait_ge(m["v_ready"], b * KV + (g + 1))
                        pe.wait_ge(m["y_raw"], n)
                        for j in range(TB):
                            for i in range(j + 1):
                                at = block_at(i, j)
                                last = pe.matmul(o_view[:, j, :], a[u][:, at:at + P], v[g % 2][:, i, :],
                                                 start=i == 0, stop=i == j, skip_group_check=True)
                        last.then_inc(m["valued"], 1)

                    def turn_top(g, u, qs, ys):
                        n = b * (2 * KV) + (2 * g + u)
                        pe.wait_ge(m["topped"], n + 1)
                        t_ps_free(2 * g + u, qs, ys)
                        for t in range(TB):
                            src = a[u] if t == 0 else top
                            last = pe.transpose(t_ps[:, t * P:(t + 1) * P], src[:, t * P:(t + 1) * P], net.ident[:, :])
                        last.then_inc(m["top_turned"], 1)

                    def turn_y(g, tops, qs):
                        pe.wait_ge(m["y_ready"], b * KV + (g + 1))
                        t_ps_free(tops, qs, g)
                        for t in range(TB):
                            last = pe.transpose(t_ps[:, t * P:(t + 1) * P],
                                                y[g % 2][:, t, :, :].rearrange("p u d -> p (u d)"), net.ident[:, :])
                        last.then_inc(m["y_turned"], 1)

                    pe.wait_ge(m["added"], b)
                    for t in range(TB):
                        pe.wait_ge(m["xn_ready"], b * TB + (t + 1))
                        last = pe.transpose(g_ps[:, t * P:(t + 1) * P], xn[:, t, :], net.ident[:, :])
                    last.then_inc(m["x_turned"], 1)
                    pe.wait_ge(m["xt_ready"], b + 1)
                    pe.matmul(g_ps[0:KV, :], w_gate[:, :], xt[:, :], start=True, stop=True,
                              skip_group_check=True).then_inc(m["gate_z"], 1)
                    project(0)
                    pe.wait_ge(m["gate_sum"], b + 1)
                    pe.sem_inc(m["gate_passed"], 1)
                    for t in range(TB):
                        last = pe.transpose(g_ps[:, t * KV:(t + 1) * KV], gate_sum[:, t * P:(t + 1) * P],
                                            net.ident[0:KV, 0:KV])
                    last.then_inc(m["gate_turned"], 1)
                    pe.wait_ge(m["neg_gate"], b + 1)
                    spread(0)
                    mask(0)
                    turn_qk(0, 0, 0)
                    for g in range(KV):
                        score(g, 0)
                        if g + 1 < KV:
                            project(g + 1)
                        score(g, 1)
                        if g >= 1:
                            turn_y(g - 1, 2 * g, g + 1)
                        value(g, 0)
                        turn_top(g, 0, g + 1, g)
                        if g + 1 < KV:
                            spread(g + 1)
                        value(g, 1)
                        if g + 1 < KV:
                            mask(g + 1)
                            turn_qk(g + 1, 2 * g + 1, g)
                        turn_top(g, 1, min(g + 2, KV), g)
                    turn_y(KV - 1, 2 * KV, KV)
                    pe.wait_ge(m["y_copied"], b * KV + KV)
                    for t in range(TB):
                        for g in range(KV):
                            last = pe.matmul(g_ps[:, t * P:(t + 1) * P], y_t[:, g, t * P:(t + 1) * P], w_proj[:, g, :],
                                             start=g == 0, stop=g == KV - 1, skip_group_check=True)
                    last.then_inc(m["out_ready"], 1)


def program(nc, dram, out, stages):
    with ExitStack() as ctx:
        net = Net(nc, ctx, dram)
        with ExitStack() as first:
            load_inputs(net, first)
        stages(net)
        stored = net.sem("out_stored", ctx)
        with nc.Block() as block:
            @block.sync
            def _(sp):
                sp.dma_start(out.rearrange("b (t p) d -> p (b t) d", p=P), net.x[:, :, :]).then_inc(stored, 16)
                sp.wait_ge(stored, 16)


def load_experts(net, name, source, ctx):
    experts = net.sbuf(name, [P, E, EXPERT_W], F32, ctx)
    loaded = net.sem(f"{name}_loaded", ctx)
    with net.nc.Block() as block:
        @block.sync
        def _(sp):
            sp.dma_start(experts[:, :, :], net.dram[source]).then_inc(loaded, 16)
            sp.wait_ge(loaded, 16)
    return experts


def whole_net(net):
    with ExitStack() as ctx:
        l0 = load_experts(net, "l0_experts", "l0_experts", ctx)
        mixture(net, "m0", 0, l0)
        mamba(net)
        mixture(net, "m1", 0, l0)
    with ExitStack() as ctx:
        l1 = load_experts(net, "l1_experts", "l1_experts", ctx)
        mixture(net, "m2", 1, l1)
        power_attention(net)
        mixture(net, "m3", 1, l1)


def rope_tables():
    div = (2.0 * np.pi / float(S) ** (np.arange(0, HD, 2, dtype=np.float32) / HD)).astype(np.float32)
    angle = (np.arange(S, dtype=np.float32)[:, None] * div[None, :]).astype(np.float64)
    cos = np.repeat(np.cos(angle), 2, 1)
    sin = np.repeat(np.sin(angle), 2, 1) * np.tile([-1.0, 1.0], HD // 2)
    place = lambda z: np.tile(z, (1, RATIO + 1)).reshape(TB, P, ROPE_W).transpose(1, 0, 2).astype(np.float32)
    return place(cos), place(sin)


def lay_out(i):
    i = {k: np.asarray(v) for k, v in i.items()}

    def experts(w1, b1, w2, b2):
        out = np.empty((P, E, EXPERT_W), np.float32)
        out[:, :, W1_AT:W2_AT] = w1.transpose(1, 0, 2)
        out[:, :, W2_AT:B2_AT] = w2.reshape(E, HC, P, D).transpose(2, 0, 1, 3).reshape(P, E, HC * D)
        out[:, :, B2_AT:B1_AT] = b2[None]
        out[:, :, B1_AT:] = b1.reshape(E, HC, P).transpose(2, 0, 1)
        return out

    def rows(v):
        return np.ascontiguousarray(np.broadcast_to(v, (P,) + v.shape))

    a = {"x": i["L0_attn_x"].reshape(N, D)}
    a["l0_experts"] = experts(i["L0_ffn_W1"], i["L0_ffn_b1"], i["L0_ffn_W2"], i["L0_ffn_b2"])
    a["l1_experts"] = experts(i["L1_ffn_w1"], i["L1_ffn_b1"], i["L1_ffn_w2"], i["L1_ffn_b2"])
    a["l0_shared_w"] = np.concatenate([i["L0_ffn_shared_W"], i["L0_ffn_gate_W"]], 1)
    a["l0_shared_b"] = rows(np.concatenate([i["L0_ffn_shared_b"], np.zeros(E, np.float32)]))
    a["l1_shared_w"] = np.ascontiguousarray(i["L1_ffn_router_w"].T)
    a["l1_shared_b"] = rows(np.zeros(E, np.float32))
    a["w_in"] = i["L0_attn_w_in"]
    a["w_out"] = i["L0_attn_w_out"].reshape(IC, P, D).transpose(1, 0, 2)
    a["w_b"] = i["L0_attn_w_B"].reshape(IC, P, DS).transpose(1, 0, 2)
    a["w_c"] = i["L0_attn_w_C"]
    a["conv_w"] = i["L0_attn_conv_w"].reshape(IC, P, DC).transpose(1, 0, 2)
    a["conv_b"] = i["L0_attn_conv_b"].reshape(IC, P).T
    w = i["L1_attn_w_attn"]
    q, k, v = np.split(w[:, :2048], [1024, 1536], 1)
    a["w_group"] = np.concatenate([q.reshape(D, KV, QW), k.reshape(D, KV, HD), v.reshape(D, KV, HD)], 2)
    a["w_gate"] = w[:, 2048:]
    a["w_proj"] = i["L1_attn_w_proj"].reshape(KV, P, D).transpose(1, 0, 2)
    a["ln_w"] = np.tile(i["L1_attn_ln_w"], RATIO)[:, None]
    a["rope_c"], a["rope_s"] = rope_tables()
    a["select"] = np.repeat(np.eye(KV, dtype=np.float32)[:, :, None], P, 2)
    a["l0_norm_w"] = rows(np.stack([i["L0_ffn_gamma"], i["L0_ffn_beta"]]))
    return a


def build(nc, arrays):
    dram = {n: nc.dram_tensor(f"in_{n}_dram", v.shape, F32, kind="ExternalInput").ap() for n, v in arrays.items()}
    out = nc.dram_tensor("out_dram", (B, S, D), F32, kind="ExternalOutput").ap()
    program(nc, dram, out, whole_net)


def kernel(**inputs):
    import concourse.bacc as _bacc
    from concourse.bass_utils import run_bass_kernel_spmd as _run

    nc = _bacc.Bacc("TRN2", target_bir_lowering=False, num_devices=1)
    arrays = {n: np.ascontiguousarray(v) for n, v in lay_out(inputs).items()}
    build(nc, arrays)
    r = _run(nc, [{f"in_{n}_dram": v for n, v in arrays.items()}], core_ids=[0])
    return r.results[0]["out_dram"]
```

```python
from contextlib import ExitStack

import concourse.bass as bass
from concourse import mybir
import numpy as np

F32 = mybir.dt.float32
BF16 = mybir.dt.bfloat16
I32 = mybir.dt.int32
F32R = mybir.dt.float32r
ALU = mybir.AluOpType
ACT = mybir.ActivationFunctionType
AX = mybir.AxisListType

P = 128
B, S, D = 8, 512, 128
N = B * S
NT = N // P
TB = S // P
E = 8
H = 512
HC = H // P
TOP_K = 2
CAPACITY = -(-3 * N // (2 * E))
LN_EPS = 1e-5

W1_AT, W2_AT, B2_AT, B1_AT = 0, H, H + HC * D, H + HC * D + D
EXPERT_W = B1_AT + HC

RING = 8
W_RING = 4


def ring_multiple(tiles):
    return -(-tiles // RING) * RING


SLOT_TILES_L0 = ring_multiple((TOP_K * N + E * (P - 1)) // P)
SLOT_TILES_L1 = ring_multiple((N + E * (P - 1)) // P)
FAR_AWAY = 1.0e6

DI, DS, DC = 256, 16, 4
IC = DI // P
KEEP, TAKE = 0.9, 0.1

KV, HD, RATIO = 8, 64, 2
QW, KW = RATIO * HD, HD
GROUP_W = QW + KW + HD
ROPE_W = QW + KW
GATE_BIAS = 6.906768
SCORE_SCALE = 2.0 ** 40
SCORE_MIN = 1e-30
DEN_EPS, HEAD_EPS = 1e-6, 1e-9
MASKED = -1.0e30
GATE_PARTS, GATE_PART = 3, 32
GATE_ROWS = GATE_PARTS * GATE_PART
SCORE_AT = {0: 0, 1: S, 3: S + 3 * P, 2: 2 * S}
SCORE_W = 2 * S + 2 * P


def block_at(i, j):
    return SCORE_AT[i] + (j - i) * P


class Counter:

    LEAD = 4

    def __init__(self, sem):
        self.sem = sem

    def wait(self, engine, count):
        engine.wait_ge(self.sem, count + self.LEAD)

    def by(self, instruction):
        instruction.then_inc(self.sem, 1)


class Chain:

    def __init__(self, engine, sem):
        self.engine, self.sem, self.n = engine, sem, 0

    def __call__(self, instruction):
        self.n += 1
        instruction.then_inc(self.sem, 1)
        self.engine.wait_ge(self.sem, self.n)


def flat(ap):
    return ap.rearrange("p a n -> p (a n)")


class Net:

    def __init__(self, nc, ctx, dram):
        self.nc, self.dram = nc, dram
        self.ctx = ctx
        self.counting = []
        sb = self.sbuf
        self.x = sb("stream", [P, NT, D])
        self.ident = sb("ident", [P, P])
        self.mean = sb("mean", [P, NT])
        self.rstd = sb("rstd", [P, NT])
        self.shift = sb("shift", [P, NT])
        self.stats = sb("stats", [P, NT, 6])
        self.ln_tmp = sb("ln_tmp", [P, 4, NT])
        self.eps = sb("eps", [P, 1])
        self.gathered = [self.sem(f"gathered{u}", ctx) for u in range(RING)]
        self.scattered = [self.sem(f"scattered{u}", ctx) for u in range(RING)]
        self.laps = 0
        self.xn_rows = nc.dram_tensor("xn_rows", (N, D), F32, kind="Internal").ap()
        self.y_rows = nc.dram_tensor("y_rows", (TOP_K * N, D), F32, kind="Internal").ap()

    def sbuf(self, name, shape, dtype=F32, ctx=None):
        return (ctx or self.ctx).enter_context(self.nc.sbuf_tensor(name, shape, dtype))

    def psum(self, name, shape, ctx):
        return ctx.enter_context(self.nc.psum_tensor(name, shape, F32))

    def sem(self, name, ctx):
        if not any(ctx is c for c, _ in self.counting):
            numbers = []
            self.counting.append((ctx, numbers))
            ctx.callback(self.zero, numbers)
        handle = ctx.enter_context(self.nc.semaphore(name))
        [numbers for c, numbers in self.counting if c is ctx][0].append(handle.num)
        return handle

    def counters(self, names, prefix, ctx):
        found = {n: Counter(self.sem(f"{prefix}_{n}", ctx)) for n in names.split()}
        with self.nc.Block() as block:
            @block.sync
            def _(sp):
                for c in found.values():
                    sp.sem_inc(c.sem, Counter.LEAD)
        return found

    def zero(self, numbers):
        self.counting.pop()
        with self.nc.Block() as block:
            @block.sync
            def _(sp):
                left = sorted(numbers)
                while left:
                    n = next((k for k in range(len(left)) if left[k] != left[0] + k), len(left))
                    sp.sem_clear(range(left[0], left[0] + n))
                    left = left[n:]


def load_inputs(net, ctx):
    nc = net.nc
    loaded, made = net.sem("x_loaded", ctx), net.sem("ident_made", ctx)
    with nc.Block() as block:
        @block.sync
        def _(sp):
            sp.dma_start(net.x[:, :, :], net.dram["x"].rearrange("(t p) d -> p t d", p=P)).then_inc(loaded, 16)
            sp.wait_ge(loaded, 16)

        @block.gpsimd
        def _(pool):
            pool.memset(net.eps[:, :], LN_EPS)
            pool.memset(net.ident[:, :], 0.0).then_inc(made, 1)
            pool.wait_ge(made, 1)
            pool.affine_select(out=net.ident[:, :], in_=net.ident[:, :], compare_op=ALU.not_equal, fill=1.0,
                               base=0, pattern=[[-1, P]], channel_multiplier=1).then_inc(made, 1)
            pool.wait_ge(made, 2)
            for u in range(RING):
                pool.dma_start(net.y_rows[u:u + 1, :], net.ident[u:u + 1, :]).then_inc(net.scattered[u], 16)


def start_loads(net, loads, loaded):
    with net.nc.Block() as block:
        @block.sync
        def _(sp):
            for dst, src in loads:
                sp.dma_start(dst[:], net.dram[src]).then_inc(loaded, 16)


def layer_norm_stats(net, name, src=None):
    nc = net.nc
    with ExitStack() as ctx:
        step = net.sem(f"{name}_ln_step", ctx)
        var_ready = net.sem(f"{name}_var_ready", ctx)
        std_ready = net.sem(f"{name}_std_ready", ctx)
        var, std, diff, half = (net.ln_tmp[:, k, :] for k in range(4))
        with nc.Block() as block:
            @block.vector
            def _(dve):
                link = Chain(dve, step)
                if src is not None:
                    for t in range(NT):
                        last = dve.bn_stats(net.stats[:, t, :], src[:, t, :])
                    link(last)
                even, odd = net.stats[:, :, 1], net.stats[:, :, 4]
                link(dve.tensor_tensor(half, even, odd, ALU.add))
                link(dve.tensor_scalar(net.mean[:, :], half, 0.5, None, ALU.mult))
                link(dve.tensor_tensor(diff, even, odd, ALU.subtract))
                link(dve.tensor_tensor(diff, diff, diff, ALU.mult))
                link(dve.tensor_tensor(var, net.stats[:, :, 2], net.stats[:, :, 5], ALU.add))
                link(dve.tensor_scalar(diff, diff, 0.25, None, ALU.mult))
                dve.scalar_tensor_tensor(out=var, in0=var, scalar=1.0 / D, in1=diff,
                                         op0=ALU.mult, op1=ALU.add).then_inc(var_ready, 1)
                dve.wait_ge(std_ready, 1)
                link(dve.reciprocal(net.rstd[:, :], std))
                link(dve.scalar_tensor_tensor(out=net.shift[:, :], in0=net.mean[:, :], scalar=-1.0, in1=net.rstd[:, :],
                                              op0=ALU.mult, op1=ALU.mult))

            @block.scalar
            def _(act):
                act.wait_ge(var_ready, 1)
                act.activation(std, var, ACT.Sqrt, bias=net.eps[:, 0:1]).then_inc(std_ready, 1)


def mixture(net, name, layer, experts):
    nc, dram = net.nc, net.dram
    two = layer == 0
    choices = TOP_K if two else 1
    tiles = SLOT_TILES_L0 if two else SLOT_TILES_L1
    cols = choices * NT
    rw = D + E if two else E
    pre = f"l{layer}"
    with ExitStack() as ctx:
        sb = lambda n, s, d=F32: net.sbuf(f"{name}_{n}", s, d, ctx)
        shared_w = sb("shared_w", [P, rw])
        shared_b = sb("shared_b", [P, rw])
        pre_sh = sb("pre_sh", [P, NT, rw])
        mixed = sb("mixed", [P, NT, D]) if two else None
        weight = sb("weight", [P, TOP_K, NT])
        row_of = sb("row_of", [P, tiles], I32)
        back_of = sb("back_of", [P, tiles], I32)
        tile_expert = sb("tile_expert", [1, tiles], I32)

        w_loaded = net.sem(f"{name}_w_loaded", ctx)
        start_loads(net, [(shared_w, f"{pre}_shared_w"), (shared_b, f"{pre}_shared_b")], w_loaded)
        layer_norm_stats(net, name, net.x)
        meet_tokens(net, name, rw, pre_sh, shared_w, shared_b, w_loaded, store=True)
        route(net, name, layer, choices, tiles, cols, rw, pre_sh, mixed, weight, row_of, back_of, tile_expert)
        expert_tiles(net, name, tiles, experts, row_of, back_of, tile_expert)
        combine(net, name, layer, choices, mixed, weight)


def pipelined(engine, ahead, behind, steps):
    ahead(0, 0, 0)
    with engine.Fori(0, steps // 2 - 1) as k:
        for u in range(2):
            ahead(k * 2 + (u + 1), 1 - u, k + u)
            behind(k * 2 + u, u, k)
    ahead(steps - 1, 1, steps // 2 - 1)
    behind(steps - 2, 0, steps // 2 - 1)
    behind(steps - 1, 1, steps // 2 - 1)


def meet_tokens(net, name, width, met, weights, bias, w_loaded, store=False, kept=None):
    nc, dram = net.nc, net.dram
    steps = NT // TB
    with ExitStack() as ctx:
        xn = [net.sbuf(f"{name}_xn{u}", [P, TB, D], F32, ctx) for u in range(2)]
        xt = [net.sbuf(f"{name}_xt{u}", [P, S], F32, ctx) for u in range(2)]
        t_ps = [net.psum(f"{name}_t_ps{u}", [P, S], ctx) for u in range(2)]
        m_ps = [net.psum(f"{name}_m_ps{u}", [P, 2, 512], ctx) for u in range(2)]
        stored = [net.sem(f"{name}_xn_stored{u}", ctx) for u in range(2)]
        c = net.counters("xn_ready xn_turned xt_ready met met_kept kept", name, ctx)
        with nc.Block() as block:
            @block.scalar
            def _(act):
                def normalise(n, u, lap):
                    if store:
                        act.wait_ge(stored[u], 16 * lap + 16)
                    c["xn_turned"].wait(act, n - 1)
                    for t in range(TB):
                        at = bass.ds(n * TB + t, 1)
                        last = act.activation(xn[u][:, t, :], flat(net.x[:, at, :]), ACT.Identity,
                                              bias=net.shift[:, at], scale=net.rstd[:, at])
                    c["xn_ready"].by(last)

                def keep_turned(n, u, lap):
                    c["xt_ready"].wait(act, n + 1)
                    act.activation(kept[:, bass.ds(n * S, S)], t_ps[u][:, :], ACT.Copy).then_inc(c["kept"].sem, 1)

                pipelined(act, normalise, (lambda n, u, lap: None) if kept is None else keep_turned, steps)

            @block.vector
            def _(dve):
                def copy(n, u, lap):
                    c["xn_turned"].wait(dve, n + 1)
                    c["met"].wait(dve, n - 1)
                    c["xt_ready"].by(dve.tensor_copy(xt[u][:, :], t_ps[u][:, :]))

                def keep(n, u, lap):
                    c["met"].wait(dve, n + 1)
                    for h in range(2):
                        out = met[:, bass.ds(n * TB + 2 * h, 2), :]
                        ps = m_ps[u][:, h, 0:2 * width].rearrange("p (t w) -> p t w", t=2)
                        last = (dve.tensor_tensor(out, ps, bias[:, :].unsqueeze(1).broadcast_to([P, 2, width]), ALU.add)
                                if bias is not None else dve.tensor_copy(out, ps))
                    c["met_kept"].by(last)

                dve.wait_ge(w_loaded, 32 if bias is not None else 16)
                pipelined(dve, copy, keep, steps)

            @block.tensor
            def _(pe):
                def turn(n, u, lap):
                    c["xn_ready"].wait(pe, n + 1)
                    c["xt_ready"].wait(pe, n - 1)
                    if kept is not None:
                        c["kept"].wait(pe, n - 1)
                    for t in range(TB):
                        last = pe.transpose(t_ps[u][:, t * P:(t + 1) * P], xn[u][:, t, :], net.ident[:, :])
                    c["xn_turned"].by(last)

                def meet(n, u, lap):
                    c["xt_ready"].wait(pe, n + 1)
                    c["met_kept"].wait(pe, n - 1)
                    for t in range(TB):
                        last = pe.matmul(m_ps[u][:, t // 2, (t % 2) * width:(t % 2 + 1) * width],
                                         xt[u][:, t * P:(t + 1) * P], weights[:, :],
                                         start=True, stop=True, skip_group_check=True)
                    c["met"].by(last)

                pe.wait_ge(w_loaded, 32 if bias is not None else 16)
                pipelined(pe, turn, meet, steps)

            if store:
                @block.sync
                def _(sp):
                    rows = net.xn_rows.rearrange("(n t p) d -> n p t d", t=TB, p=P)
                    for u in range(2):
                        sp.sem_inc(stored[u], 16)
                    with sp.Fori(0, steps // 2) as k:
                        for u in range(2):
                            n = k * 2 + u
                            c["xn_ready"].wait(sp, n + 1)
                            sp.dma_start(rows[bass.ds(n, 1)].rearrange("a p t d -> (a p) t d"), xn[u][:, :, :]
                                         ).then_inc(stored[u], 16)
                    for u in range(2):
                        sp.wait_ge(stored[u], 16 * (steps // 2) + 16)


def route(net, name, layer, choices, tiles, cols, rw, pre_sh, mixed, weight, row_of, back_of, tile_expert):
    nc = net.nc
    two = layer == 0
    G = 8
    with ExitStack() as ctx:
        sb = lambda n, s, d=F32: net.sbuf(f"{name}_{n}", s, d, ctx)
        sem = lambda n: net.sem(f"{name}_{n}", ctx)
        before = sb("before", [P, P])
        ones = sb("ones", [P, P])
        preference = sb("preference", [P, E])
        column = sb("column", [P, P])
        column_id = sb("column_id", [P, cols])
        place = sb("place", [P, 1])
        not_first = sb("not_first", [P, E, NT])
        big = sb("big", [P, NT, E])
        prob = sb("prob", [P, NT, E])
        pick = [sb(f"pick{c}", [P, NT, E]) for c in range(2)]
        chosen = sb("chosen", [P, NT, E])
        best = [sb(f"best{c}", [P, NT]) for c in range(2)]
        row = sb("row", [P, NT])
        by_expert = sb("by_expert", [P, E, NT])
        so_far = sb("so_far", [P, E, NT])
        rank = sb("rank", [P, NT, E])
        counts = sb("counts", [P, 4, E])
        counts_i = sb("counts_i", [P, E], I32)
        slot = sb("slot", [P, choices, NT])
        slot_i = sb("slot_i", [P, 2, cols], I32)
        hi_lo = sb("hi_lo", [P, 2, cols])
        column_b = sb("column_b", [P, P], BF16)
        lo_hot = [sb(f"lo_hot{u}", [P, G, P], BF16) for u in range(2)]
        hi_hot = [sb(f"hi_hot{u}", [P, G, tiles], BF16) for u in range(2)]
        hi_ids = [sb(f"hi_ids{u}", [P, G, 2, tiles], BF16) for u in range(2)]
        ends = sb("ends", [P, tiles, E])
        table = sb("table", [P, 4, tiles])
        cnt_ps = net.psum(f"{name}_cnt_ps", [P, 2, NT * E], ctx)
        tab_ps = net.psum(f"{name}_tab_ps", [P, 512], ctx)
        made, step, exps_ready, logits_ready = sem("r_made"), sem("r_step"), sem("r_exps"), sem("r_logits")
        shared_ready = sem("r_shared")
        chosen_ready, counted, hots_ready, hots_used = sem("r_chosen"), sem("r_counted"), sem("r_hots"), sem("r_used")

        with nc.Block() as block:
            @block.gpsimd
            def _(pool):
                link = Chain(pool, made)
                link(pool.memset(ones[:, :], 1.0))
                link(pool.memset(not_first[:, :, :], 1.0))
                link(pool.memset(not_first[:, :, 0:1], 0.0))
                link(pool.affine_select(out=before[:, :], in_=ones[:, :], compare_op=ALU.is_gt, fill=0.0,
                                        base=0, pattern=[[1, P]], channel_multiplier=-1))
                link(pool.iota(column[:, :], [[1, P]], base=0, channel_multiplier=0,
                               allow_small_or_imprecise_dtypes=True))
                link(pool.iota(preference[:, :], [[-1, E]], base=E, channel_multiplier=0,
                               allow_small_or_imprecise_dtypes=True))
                link(pool.iota(column_id[:, :], [[1, cols]], base=1, channel_multiplier=0,
                               allow_small_or_imprecise_dtypes=True))
                link(pool.iota(place[:, :], [[1, 1]], base=0, channel_multiplier=1,
                               allow_small_or_imprecise_dtypes=True))

            @block.scalar
            def _(act):
                act.wait_ge(logits_ready, 1)
                act.activation(prob[:, :, :], prob[:, :, :], ACT.Exp).then_inc(exps_ready, 1)
                if two:
                    for t in range(0, NT, 8):
                        last = act.activation(mixed[:, t:t + 8, :], pre_sh[:, t:t + 8, 0:D], ACT.Gelu)
                    last.then_inc(shared_ready, 1)
                    act.wait_ge(shared_ready, 1)
                    for t in range(0, NT, 8):
                        act.activation(mixed[:, t:t + 8, :], mixed[:, t:t + 8, :], ACT.Copy, scale=0.5
                                       ).then_inc(shared_ready, 1)

            @block.tensor
            def _(pe):
                pe.wait_ge(made, 8)
                pe.wait_ge(chosen_ready, 1)
                hits = chosen[:, :, :].rearrange("p t e -> p (t e)")
                pe.matmul(cnt_ps[:, 0, :], before[:, :], hits, start=True, stop=True)
                pe.matmul(cnt_ps[:, 1, :], ones[:, :], hits, start=True, stop=True,
                          skip_group_check=True).then_inc(counted, 1)
                for r in range(cols // G):
                    pe.wait_ge(hots_ready, r + 1)
                    for g in range(G):
                        last = pe.matmul(tab_ps[:, 0:2 * tiles], lo_hot[r % 2][:, g, :],
                                         hi_ids[r % 2][:, g, :, :].rearrange("p z s -> p (z s)"),
                                         start=r == 0 and g == 0, stop=r == cols // G - 1 and g == G - 1)
                    last.then_inc(hots_used, 1)

            @block.vector
            def _(dve):
                link = Chain(dve, step)
                dve.wait_ge(made, 8)
                logits = pre_sh[:, :, rw - E:rw]
                over_e = lambda a: a.unsqueeze(2).broadcast_to([P, NT, E])
                link(dve.tensor_reduce(row[:, :], logits, AX.X, ALU.max))
                dve.tensor_tensor(prob[:, :, :], logits, over_e(row[:, :]), ALU.subtract).then_inc(logits_ready, 1)
                dve.wait_ge(exps_ready, 1)
                link(dve.tensor_reduce(row[:, :], prob[:, :, :], AX.X, ALU.add))
                link(dve.reciprocal(row[:, :], row[:, :]))
                link(dve.tensor_tensor(prob[:, :, :], prob[:, :, :], over_e(row[:, :]), ALU.mult))
                prefer = preference[:, :].unsqueeze(1).broadcast_to([P, NT, E])
                for c in range(choices):
                    link(dve.tensor_reduce(best[c][:, :], prob[:, :, :], AX.X, ALU.max))
                    link(dve.tensor_tensor(big[:, :, :], prob[:, :, :], over_e(best[c][:, :]), ALU.is_equal))
                    link(dve.tensor_tensor(big[:, :, :], big[:, :, :], prefer, ALU.mult))
                    link(dve.tensor_reduce(row[:, :], big[:, :, :], AX.X, ALU.max))
                    link(dve.tensor_tensor(pick[c][:, :, :], big[:, :, :], over_e(row[:, :]), ALU.is_equal))
                    if c + 1 < choices:
                        link(dve.scalar_tensor_tensor(out=prob[:, :, :], in0=pick[c][:, :, :], scalar=-2.0,
                                                      in1=prob[:, :, :], op0=ALU.mult, op1=ALU.add))
                if two:
                    link(dve.tensor_tensor(chosen[:, :, :], pick[0][:, :, :], pick[1][:, :, :], ALU.add))
                else:
                    link(dve.tensor_copy(chosen[:, :, :], pick[0][:, :, :]))
                dve.sem_inc(chosen_ready, 1)
                if two:
                    link(dve.tensor_tensor(row[:, :], best[0][:, :], best[1][:, :], ALU.add))
                    link(dve.reciprocal(row[:, :], row[:, :]))
                    for c in range(2):
                        link(dve.tensor_tensor(weight[:, c, :], best[c][:, :], row[:, :], ALU.mult))
                dve.wait_ge(counted, 1)
                totals = cnt_ps[:, 1, :].rearrange("p (t e) -> p e t", e=E)
                link(dve.tensor_copy(by_expert[:, :, :], totals))
                link(dve.tensor_tensor_scan(so_far[:, :, :].rearrange("p e t -> p (e t)"),
                                            not_first[:, :, :].rearrange("p e t -> p (e t)"),
                                            by_expert[:, :, :].rearrange("p e t -> p (e t)"), 0.0,
                                            ALU.mult, ALU.add))
                link(dve.tensor_copy(counts[:, 0, :], so_far[:, :, NT - 1]))
                link(dve.tensor_tensor(so_far[:, :, :], so_far[:, :, :], by_expert[:, :, :], ALU.subtract))
                link(dve.tensor_tensor(rank[:, :, :], cnt_ps[:, 0, :].rearrange("p (t e) -> p t e", e=E),
                                       so_far[:, :, :].rearrange("p e t -> p t e"), ALU.add))
                if not two:
                    link(dve.tensor_scalar(counts[:, 0, :], counts[:, 0, :], float(CAPACITY), None, ALU.min))
                link(dve.tensor_scalar(counts_i[:, :], counts[:, 0, :], float(P - 1), None, ALU.add))
                link(dve.tensor_scalar(counts_i[:, :], counts_i[:, :], 7, None, ALU.arith_shift_right))
                link(dve.tensor_copy(counts[:, 1, :], counts_i[:, :]))
                link(dve.tensor_tensor_scan(counts[:, 2, :], ones[:, 0:E], counts[:, 1, :], 0.0, ALU.mult, ALU.add))
                link(dve.tensor_tensor(counts[:, 3, :], counts[:, 2, :], counts[:, 1, :], ALU.subtract))
                link(dve.tensor_scalar(counts[:, 3, :], counts[:, 3, :], float(P), None, ALU.mult))
                if not two:
                    link(dve.tensor_tensor(big[:, :, :], rank[:, :, :], pick[0][:, :, :], ALU.mult))
                    link(dve.tensor_reduce(row[:, :], big[:, :, :], AX.X, ALU.add))
                    link(dve.tensor_scalar(weight[:, 1, :], row[:, :], float(CAPACITY), None, ALU.is_lt))
                    link(dve.tensor_tensor(weight[:, 0, :], weight[:, 1, :], best[0][:, :], ALU.mult))
                    link(dve.tensor_scalar(weight[:, 0, :], weight[:, 0, :], 0.5, None, ALU.mult))
                    link(dve.tensor_scalar(weight[:, 1, :], weight[:, 1, :], -FAR_AWAY, FAR_AWAY, ALU.mult, ALU.add))
                link(dve.tensor_tensor(rank[:, :, :], rank[:, :, :],
                                       counts[:, 3, :].unsqueeze(1).broadcast_to([P, NT, E]), ALU.add))
                for c in range(choices):
                    link(dve.tensor_tensor(big[:, :, :], rank[:, :, :], pick[c][:, :, :], ALU.mult))
                    link(dve.tensor_reduce(slot[:, c, :], big[:, :, :], AX.X, ALU.add))
                if not two:
                    link(dve.tensor_tensor(slot[:, 0, :], slot[:, 0, :], weight[:, 1, :], ALU.add))
                flat_slot = slot[:, :, :].rearrange("p c t -> p (c t)")
                link(dve.tensor_copy(slot_i[:, 0, :], flat_slot))
                link(dve.tensor_scalar(slot_i[:, 1, :], slot_i[:, 0, :], P - 1, None, ALU.bitwise_and))
                link(dve.tensor_scalar(slot_i[:, 0, :], slot_i[:, 0, :], 7, None, ALU.arith_shift_right))
                link(dve.tensor_copy(hi_lo[:, :, :], slot_i[:, :, :]))
                link(dve.tensor_copy(column_b[:, :], column[:, :]))
                for r in range(cols // G):
                    if r >= 2:
                        dve.wait_ge(hots_used, r - 1)
                    at = slice(r * G, (r + 1) * G)
                    link(dve.tensor_tensor(hi_hot[r % 2][:, :, :],
                                           column_b[:, 0:tiles].unsqueeze(1).broadcast_to([P, G, tiles]),
                                           hi_lo[:, 0, at].unsqueeze(2).broadcast_to([P, G, tiles]), ALU.is_equal))
                    for g in range(G):
                        dve.tensor_scalar(lo_hot[r % 2][:, g, :], column_b[:, :],
                                          hi_lo[:, 1, r * G + g:r * G + g + 1], None, ALU.is_equal)
                    dve.tensor_tensor(hi_ids[r % 2][:, :, 0, :], hi_hot[r % 2][:, :, :],
                                      column_id[:, at].unsqueeze(2).broadcast_to([P, G, tiles]), ALU.mult)
                    last = dve.tensor_scalar(hi_ids[r % 2][:, :, 1, :], hi_hot[r % 2][:, :, :], place[:, 0:1], None,
                                             ALU.mult)
                    last.then_inc(hots_ready, 1)
                link(dve.tensor_tensor(ends[:, :, :], column[:, 0:tiles].unsqueeze(2).broadcast_to([P, tiles, E]),
                                       counts[:, 2, :].unsqueeze(1).broadcast_to([P, tiles, E]), ALU.is_ge))
                link(dve.tensor_reduce(table[:, 0, :], ends[:, :, :], AX.X, ALU.add))
                link(dve.tensor_scalar(tile_expert[:, :], table[0:1, 0, :], float(E - 1), None, ALU.min))
                dve.wait_ge(hots_used, cols // G)
                full = table[:, 1, :]
                link(dve.tensor_scalar(table[:, 3, :], tab_ps[:, 0:tiles], float(P), float(-P), ALU.mult, ALU.add))
                link(dve.tensor_tensor(full, table[:, 3, :], tab_ps[:, tiles:2 * tiles], ALU.add))
                link(dve.tensor_scalar(table[:, 2, :], full, 0.0, 1.0e6, ALU.is_lt, ALU.mult))
                link(dve.tensor_tensor(back_of[:, :], full, table[:, 2, :], ALU.add))
                link(dve.tensor_scalar(table[:, 2, :], full, float(N), float(-N), ALU.is_ge, ALU.mult))
                link(dve.tensor_tensor(table[:, 3, :], full, table[:, 2, :], ALU.add))
                link(dve.tensor_scalar(row_of[:, :], table[:, 3, :], 0.0, None, ALU.max))


def expert_tiles(net, name, tiles, experts, row_of, back_of, tile_expert):
    nc = net.nc
    R = RING
    trips = tiles // R
    with ExitStack() as ctx:
        sb = lambda n, s, d=F32: net.sbuf(f"{name}_{n}", s, d, ctx)
        xg = [sb(f"xg{u}", [P, D]) for u in range(R)]
        xg_t = [sb(f"xg_t{u}", [P, P]) for u in range(2)]
        wb = [sb(f"wb{u}", [P, EXPERT_W]) for u in range(W_RING)]
        hid = [sb(f"hid{u}", [P, HC, P]) for u in range(2)]
        ys = [sb(f"ys{u}", [P, D]) for u in range(R)]
        row_ix = [sb(f"row_ix{u}", [P, 1], I32) for u in range(R)]
        back_ix = [sb(f"back_ix{u}", [P, 1], I32) for u in range(R)]
        t_ps = [net.psum(f"{name}_gt_ps{u}", [P, 512], ctx) for u in range(2)]
        h_ps = [net.psum(f"{name}_h_ps{u}", [P, HC, P], ctx) for u in range(2)]
        y_ps = [net.psum(f"{name}_y_ps{u}", [P, 512], ctx) for u in range(2)]
        gathered, scattered = net.gathered, net.scattered
        gathered_before, scattered_before = 16 * net.laps, 16 * (net.laps + 1)
        net.laps += trips
        passed = net.sem(f"{name}_passed", ctx)
        c = net.counters("row_ix_ready turned xt_ready w_ready h_ready act_ready y_ready y_kept",
                         f"{name}_e", ctx)
        with nc.Block() as block:
            @block.gpsimd
            def _(pool):
                def gather(u):
                    pool.indirect_dma_start(xg[u][:, :], None, net.xn_rows,
                                            bass.IndirectOffsetOnAxis(ap=row_ix[u][:, :], axis=0)
                                            ).then_inc(gathered[u], 16)

                def scatter(u):
                    pool.indirect_dma_start(net.y_rows, bass.IndirectOffsetOnAxis(ap=back_ix[u][:, :], axis=0),
                                            ys[u][:, :], None, bounds_check=TOP_K * N - 1, oob_is_err=False
                                            ).then_inc(scattered[u], 16)

                def until(counter, count):
                    counter.wait(pool, count)
                    pool.sem_inc(passed, 1)

                for u in range(R):
                    pool.wait_ge(scattered[u], scattered_before)
                for u in range(R):
                    c["row_ix_ready"].wait(pool, u + 1)
                    gather(u)
                with pool.Fori(0, trips - 1) as k:
                    for u in range(R):
                        j = k * R + u
                        until(c["row_ix_ready"], j + (R + 1))
                        gather(u)
                        until(c["y_kept"], j + 1)
                        scatter(u)
                for u in range(R):
                    j = tiles - R + u
                    until(c["y_kept"], j + 1)
                    scatter(u)
                for u in range(R):
                    pool.wait_ge(scattered[u], 16 * trips + scattered_before)

            @block.vector
            def _(dve):
                def weights(j, r):
                    e = dve.value_load(tile_expert[0:1, bass.ds(j, 1)], min_val=0, max_val=E - 1)
                    c["w_ready"].by(dve.tensor_copy(wb[r][:, :], flat(experts.weights[:, bass.ds(e, 1), :])))

                def next_rows(j, r):
                    c["turned"].wait(dve, j + 1)
                    c["row_ix_ready"].by(dve.tensor_copy(row_ix[r][:, :], row_of[:, bass.ds(j + R, 1)]))

                def keep(lap, j, r):
                    dve.wait_ge(scattered[r], 16 * lap + scattered_before)
                    dve.tensor_copy(back_ix[r][:, :], back_of[:, bass.ds(j, 1)])
                    c["y_ready"].wait(dve, j + 1)
                    c["y_kept"].by(dve.tensor_tensor(ys[r][:, :], y_ps[r % 2][:, 0:D], wb[r % W_RING][:, B2_AT:B2_AT + D],
                                                     ALU.add))

                for r in range(R):
                    c["row_ix_ready"].by(dve.tensor_copy(row_ix[r][:, :], row_of[:, r:r + 1]))
                dve.wait_ge(experts.loaded, 16)
                for r in range(W_RING - 1):
                    weights(r, r)
                with dve.Fori(0, trips - 1) as k:
                    for r in range(R):
                        j = k * R + r
                        c["y_kept"].wait(dve, j)
                        weights(j + (W_RING - 1), (r + W_RING - 1) % W_RING)
                        next_rows(j, r)
                        keep(k, j, r)
                for j in range(tiles - R, tiles):
                    if j + W_RING - 1 < tiles:
                        c["y_kept"].wait(dve, j)
                        weights(j + W_RING - 1, (j + W_RING - 1) % W_RING)
                    keep(trips - 1, j, j % R)

            @block.scalar
            def _(act):
                def turn_copy(j, u):
                    c["turned"].wait(act, j + 1)
                    c["h_ready"].wait(act, j - 1)
                    c["xt_ready"].by(act.activation(xg_t[u][:, :], t_ps[u][:, 0:P], ACT.Copy))

                def gelu(j, r):
                    c["h_ready"].wait(act, j + 1)
                    c["y_ready"].wait(act, j - 1)
                    for k in range(HC):
                        last = act.activation(hid[r % 2][:, k, :], h_ps[r % 2][:, k, :], ACT.Gelu,
                                              bias=wb[r % W_RING][:, B1_AT + k:B1_AT + k + 1])
                    c["act_ready"].by(last)

                turn_copy(0, 0)
                turn_copy(1, 1)
                gelu(0, 0)
                with act.Fori(0, trips - 1) as t:
                    for r in range(R):
                        j = t * R + r
                        turn_copy(j + 2, r % 2)
                        gelu(j + 1, (r + 1) % R)
                for j in range(tiles - R, tiles - 1):
                    if j + 2 < tiles:
                        turn_copy(j + 2, j % 2)
                    gelu(j + 1, (j + 1) % R)

            @block.tensor
            def _(pe):
                def turn(lap, j, r):
                    pe.wait_ge(gathered[r], 16 * lap + (16 + gathered_before))
                    c["xt_ready"].wait(pe, j - 1)
                    c["turned"].by(pe.transpose(t_ps[r % 2][:, 0:P], xg[r][:, :], net.ident[:, :]))

                def hidden(j, r):
                    c["xt_ready"].wait(pe, j + 1)
                    c["w_ready"].wait(pe, j + 1)
                    c["act_ready"].wait(pe, j - 1)
                    for k in range(HC):
                        last = pe.matmul(h_ps[r % 2][:, k, :], wb[r % W_RING][:, k * P:(k + 1) * P], xg_t[r % 2][:, :],
                                         start=True, stop=True, skip_group_check=True)
                    c["h_ready"].by(last)

                def output(j, r):
                    c["act_ready"].wait(pe, j + 1)
                    c["y_kept"].wait(pe, j - 1)
                    for k in range(HC):
                        last = pe.matmul(y_ps[r % 2][:, 0:D], hid[r % 2][:, k, :],
                                         wb[r % W_RING][:, W2_AT + k * D:W2_AT + (k + 1) * D], start=k == 0, stop=k == HC - 1)
                    c["y_ready"].by(last)

                turn(0, 0, 0)
                turn(0, 1, 1)
                hidden(0, 0)
                with pe.Fori(0, trips - 1) as t:
                    for r in range(R):
                        j = t * R + r
                        turn(t + (r + 2) // R, j + 2, (r + 2) % R)
                        hidden(j + 1, (r + 1) % R)
                        output(j, r)
                for j in range(tiles - R, tiles):
                    if j + 2 < tiles:
                        turn((j + 2) // R, j + 2, (j + 2) % R)
                    if j + 1 < tiles:
                        hidden(j + 1, (j + 1) % R)
                    output(j, j % R)


def combine(net, name, layer, choices, mixed, weight):
    nc, dram = net.nc, net.dram
    two = layer == 0
    steps, rings = NT // TB, 4
    with ExitStack() as ctx:
        sb = lambda n, s, d=F32: net.sbuf(f"{name}_{n}", s, d, ctx)
        yl = [sb(f"yl{u}", [P, choices, TB, D]) for u in range(rings)]
        norm_w = sb("norm_w", [P, 2, D])
        loaded = [net.sem(f"{name}_y_loaded{u}", ctx) for u in range(rings)]
        w_loaded, halved = net.sem(f"{name}_norm_w_loaded", ctx), net.sem(f"{name}_w_halved", ctx)
        c = net.counters("first_added used beta_added measured", f"{name}_c", ctx)
        rows = net.y_rows.rearrange("(c n t p) d -> n c p t d", c=TOP_K, t=TB, p=P)
        with nc.Block() as block:
            @block.sync
            def _(sp):
                if two:
                    sp.dma_start(norm_w[:, :, :], dram["l0_norm_w"]).then_inc(w_loaded, 16)
                for n in range(steps):
                    u = n % rings
                    c["used"].wait(sp, n + 1 - rings)
                    for k in range(choices):
                        sp.dma_start(yl[u][:, k, :, :], rows[n, k]).then_inc(loaded[u], 16)

            if two:
                @block.gpsimd
                def _(pool):
                    pool.wait_ge(w_loaded, 16)
                    pool.tensor_scalar(norm_w[:, :, :], norm_w[:, :, :], 0.5, None, ALU.mult).then_inc(halved, 1)
                    pool.wait_ge(halved, 1)
                    c["beta_added"].by(pool.tensor_tensor(net.x[:, :, :], net.x[:, :, :], norm_w[:, 1, :].unsqueeze(1)
                                                          .broadcast_to([P, NT, D]), ALU.add))

            @block.vector
            def _(dve):
                for n in range(steps):
                    u = n % rings
                    dve.wait_ge(loaded[u], 16 * choices * (n // rings + 1))
                    tiles = range(n * TB, (n + 1) * TB)
                    if not two:
                        for t in tiles:
                            last = dve.scalar_tensor_tensor(
                                out=net.x[:, t, :], in0=yl[u][:, 0, t % TB, :], scalar=weight[:, 0, t:t + 1],
                                in1=net.x[:, t, :], op0=ALU.mult, op1=ALU.add)
                        c["used"].by(last)
                        continue
                    for t in tiles:
                        last = dve.scalar_tensor_tensor(
                            out=mixed[:, t, :], in0=yl[u][:, 0, t % TB, :], scalar=weight[:, 0, t:t + 1],
                            in1=mixed[:, t, :], op0=ALU.mult, op1=ALU.add)
                    c["first_added"].by(last)
                    c["first_added"].wait(dve, n + 1)
                    for t in tiles:
                        last = dve.scalar_tensor_tensor(
                            out=mixed[:, t, :], in0=yl[u][:, 1, t % TB, :], scalar=weight[:, 1, t:t + 1],
                            in1=mixed[:, t, :], op0=ALU.mult, op1=ALU.add)
                    c["used"].by(last)
                    c["used"].wait(dve, n + 1)
                    for t in tiles:
                        last = dve.bn_stats(net.stats[:, t, :], mixed[:, t, :])
                    c["measured"].by(last)
                c["used"].wait(dve, steps)
                if two:
                    c["measured"].wait(dve, steps)
                    c["beta_added"].wait(dve, 1)
        if two:
            add_normalised(net, name, mixed, norm_w)


def add_normalised(net, name, mixed, norm_w):
    nc = net.nc
    layer_norm_stats(net, f"{name}_out")
    with ExitStack() as ctx:
        normed, scaled, added = (net.sem(f"{name}_{n}", ctx) for n in ("normed", "scaled", "added"))
        with nc.Block() as block:
            @block.scalar
            def _(act):
                for n in range(NT // TB):
                    for t in range(n * TB, (n + 1) * TB):
                        last = act.activation(mixed[:, t, :], mixed[:, t, :], ACT.Identity,
                                              bias=net.shift[:, t:t + 1], scale=net.rstd[:, t:t + 1])
                    last.then_inc(normed, 1)

            @block.vector
            def _(dve):
                gamma = norm_w[:, 0, :].unsqueeze(1).broadcast_to([P, TB, D])

                def scale(n):
                    rows = mixed[:, n * TB:(n + 1) * TB, :]
                    dve.wait_ge(normed, n + 1)
                    dve.tensor_tensor(rows, rows, gamma, ALU.mult).then_inc(scaled, 1)

                def add(n):
                    rows = net.x[:, n * TB:(n + 1) * TB, :]
                    dve.wait_ge(scaled, n + 1)
                    dve.tensor_tensor(rows, rows, mixed[:, n * TB:(n + 1) * TB, :], ALU.add).then_inc(added, 1)

                scale(0)
                for n in range(NT // TB):
                    if n + 1 < NT // TB:
                        scale(n + 1)
                    add(n)


def mamba(net):
    nc, dram = net.nc, net.dram
    with ExitStack() as ctx:
        sb = lambda n, s, d=F32: net.sbuf(f"mb_{n}", s, d, ctx)
        w_in = sb("w_in", [P, 2 * DI])
        w_out = sb("w_out", [P, IC, D])
        w_b = sb("w_b", [P, IC, DS])
        w_c = sb("w_c", [DS, DI])
        conv_w = sb("conv_w", [P, IC, DC])
        conv_b = sb("conv_b", [P, IC])
        keep = sb("keep", [DS, S])
        xn = [sb(f"xn{u}", [P, TB, D]) for u in range(2)]
        xt = [sb(f"xt{u}", [P, S]) for u in range(2)]
        xp = [sb(f"xp{u}", [P, IC, S + DC - 1]) for u in range(2)]
        conv = [sb(f"conv{u}", [P, IC, S]) for u in range(2)]
        xc = [sb(f"xc{u}", [P, IC, S]) for u in range(2)]
        gate = [sb(f"gate{u}", [P, IC, S]) for u in range(2)]
        taken = [sb(f"taken{u}", [DS, S]) for u in range(2)]
        state = [sb(f"state{u}", [DS, S]) for u in range(2)]
        gated = [sb(f"gated{u}", [P, IC, S]) for u in range(2)]
        t_ps = net.psum("mb_t_ps", [P, S], ctx)
        z_ps = net.psum("mb_z_ps", [P, 2 * IC, S], ctx)
        u_ps = net.psum("mb_u_ps", [P, S], ctx)
        y_ps = net.psum("mb_y_ps", [P, IC, S], ctx)
        loads = [(w_in, "w_in"), (w_out, "w_out"), (w_b, "w_b"), (w_c, "w_c"), (conv_w, "conv_w"), (conv_b, "conv_b")]
        w_loaded, padded = net.sem("mb_w_loaded", ctx), net.sem("mb_padded", ctx)
        start_loads(net, loads, w_loaded)
        layer_norm_stats(net, "mb", net.x)
        c = net.counters("xn_ready turned xt_ready xz_ready xp_ready gate_ready conv_step conv_ready xc_ready u_ready "
                         "taken_ready state_ready y_ready gated_ready o_ready added", "mb", ctx)

        def steps_of(engine, step):
            step(-2, 0)
            step(-1, 1)
            with engine.Fori(0, B // 2 - 1) as k:
                for u in range(2):
                    step(k * 2 + u, u)
            step(B - 2, 0)
            step(B - 1, 1)

        def there(s):
            return not isinstance(s, int) or 0 <= s < B

        with nc.Block() as block:
            @block.gpsimd
            def _(pool):
                for u in range(2):
                    pool.memset(xp[u][:, :, 0:DC - 1], 0.0).then_inc(padded, 1)
                pool.memset(keep[:, :], KEEP).then_inc(padded, 1)

            @block.vector
            def _(dve):
                def normalise(b, u):
                    c["turned"].wait(dve, b - 1)
                    for t in range(TB):
                        at = b * TB + t
                        last = dve.tensor_scalar(xn[u][:, t, :], flat(net.x[:, bass.ds(at, 1), :]),
                                                 net.mean[:, bass.ds(at, 1)], net.rstd[:, bass.ds(at, 1)],
                                                 ALU.subtract, ALU.mult)
                    c["xn_ready"].by(last)

                def convolve(b, u, ch):
                    c["xp_ready"].wait(dve, b + 1)
                    c["xc_ready"].wait(dve, b * IC + (ch + 1 - 2 * IC))
                    for j in range(DC):
                        if j == 0:
                            ins = dve.tensor_scalar(conv[u][:, ch, :], xp[u][:, ch, 0:S], conv_w[:, ch, 0:1],
                                                    None, ALU.mult)
                        else:
                            ins = dve.scalar_tensor_tensor(
                                out=conv[u][:, ch, :], in0=xp[u][:, ch, j:j + S], scalar=conv_w[:, ch, j:j + 1],
                                in1=conv[u][:, ch, :], op0=ALU.mult, op1=ALU.add)
                        if j < DC - 1:
                            c["conv_step"].by(ins)
                            c["conv_step"].wait(dve, b * (IC * (DC - 1)) + (ch * (DC - 1) + j + 1))
                    c["conv_ready"].by(ins)

                def scan(b, u):
                    c["taken_ready"].wait(dve, b + 1)
                    c["y_ready"].wait(dve, b - 1)
                    c["state_ready"].by(dve.tensor_tensor_scan(state[u][:, :], keep[:, :], taken[u][:, :], 0.0,
                                                               ALU.mult, ALU.add))

                def gate_y(b, u):
                    c["gate_ready"].wait(dve, b + 1)
                    c["y_ready"].wait(dve, b + 1)
                    c["o_ready"].wait(dve, b - 1)
                    c["gated_ready"].by(dve.tensor_tensor(gated[u][:, :, :], y_ps[:, :, :], gate[u][:, :, :], ALU.mult))

                def add(b):
                    c["o_ready"].wait(dve, b + 1)
                    rows = net.x[:, bass.ds(b * TB, TB), :]
                    c["added"].by(dve.tensor_tensor(rows, rows, y_ps[:, 0, :].rearrange("p (t d) -> p t d", t=TB),
                                                    ALU.add))

                def step(s, u):
                    if there(s + 2):
                        normalise(s + 2, u)
                    if there(s):
                        scan(s, u)
                    if there(s + 1):
                        convolve(s + 1, 1 - u, 0)
                    if there(s):
                        gate_y(s, u)
                    if there(s + 1):
                        convolve(s + 1, 1 - u, 1)
                    if there(s):
                        add(s)

                dve.wait_ge(w_loaded, 16 * len(loads))
                dve.wait_ge(padded, 3)
                steps_of(dve, step)

            @block.scalar
            def _(act):
                def copy_xt(b, u):
                    c["turned"].wait(act, b + 1)
                    c["xz_ready"].wait(act, b - 1)
                    c["xt_ready"].by(act.activation(xt[u][:, :], t_ps[:, :], ACT.Copy))

                def copy_xp(b, u):
                    c["xz_ready"].wait(act, b + 1)
                    c["conv_ready"].wait(act, b * IC - IC)
                    c["xp_ready"].by(act.activation(xp[u][:, :, DC - 1:], z_ps[:, 0:IC, :], ACT.Copy))

                def silu_z(b, u):
                    c["xz_ready"].wait(act, b + 1)
                    c["gated_ready"].wait(act, b - 1)
                    c["gate_ready"].by(act.activation(gate[u][:, :, :], z_ps[:, IC:, :], ACT.Silu))

                def silu_conv(b, u, ch):
                    c["conv_ready"].wait(act, b * IC + (ch + 1))
                    c["u_ready"].wait(act, b - 1)
                    c["xc_ready"].by(act.activation(xc[u][:, ch, :], conv[u][:, ch, :], ACT.Silu,
                                                    bias=conv_b[:, ch:ch + 1]))

                def take(b, u):
                    c["u_ready"].wait(act, b + 1)
                    c["state_ready"].wait(act, b - 1)
                    c["taken_ready"].by(act.activation(taken[u][:, :], u_ps[0:DS, :], ACT.Copy, scale=TAKE))

                def step(s, u):
                    if there(s + 2):
                        copy_xt(s + 2, u)
                    if there(s + 1):
                        silu_conv(s + 1, 1 - u, 0)
                    if there(s + 2):
                        copy_xp(s + 2, u)
                    if there(s + 1):
                        silu_conv(s + 1, 1 - u, 1)
                    if there(s + 2):
                        silu_z(s + 2, u)
                    if there(s + 1):
                        take(s + 1, 1 - u)

                steps_of(act, step)

            @block.tensor
            def _(pe):
                def turn(b, u):
                    c["xn_ready"].wait(pe, b + 1)
                    c["xt_ready"].wait(pe, b)
                    for t in range(TB):
                        last = pe.transpose(t_ps[:, t * P:(t + 1) * P], xn[u][:, t, :], net.ident[:, :])
                    c["turned"].by(last)

                def project(b, u):
                    c["xt_ready"].wait(pe, b + 1)
                    c["xp_ready"].wait(pe, b)
                    c["gate_ready"].wait(pe, b)
                    for ch in range(2 * IC):
                        last = pe.matmul(z_ps[:, ch, :], w_in[:, ch * P:(ch + 1) * P], xt[u][:, :],
                                         start=True, stop=True)
                    c["xz_ready"].by(last)

                def input_states(b, u):
                    c["taken_ready"].wait(pe, b)
                    for ch in range(IC):
                        c["xc_ready"].wait(pe, b * IC + (ch + 1))
                        last = pe.matmul(u_ps[0:DS, :], w_b[:, ch, :], xc[u][:, ch, :],
                                         start=ch == 0, stop=ch == IC - 1)
                    c["u_ready"].by(last)

                def read_states(b, u):
                    c["state_ready"].wait(pe, b + 1)
                    c["added"].wait(pe, b)
                    for ch in range(IC):
                        last = pe.matmul(y_ps[:, ch, :], w_c[:, ch * P:(ch + 1) * P], state[u][:, :],
                                         start=True, stop=True)
                    c["y_ready"].by(last)

                def output(b, u):
                    c["gated_ready"].wait(pe, b + 1)
                    for t in range(TB):
                        for ch in range(IC):
                            last = pe.matmul(y_ps[:, 0, t * P:(t + 1) * P], gated[u][:, ch, t * P:(t + 1) * P],
                                             w_out[:, ch, :], start=ch == 0, stop=ch == IC - 1,
                                             skip_group_check=True)
                    c["o_ready"].by(last)

                def step(s, u):
                    if there(s + 2):
                        turn(s + 2, u)
                    if there(s):
                        read_states(s, u)
                    if there(s + 2):
                        project(s + 2, u)
                    if there(s):
                        output(s, u)
                    if there(s + 1):
                        input_states(s + 1, 1 - u)

                pe.wait_ge(w_loaded, 16 * len(loads))
                steps_of(pe, step)


def power_attention(net):
    with ExitStack() as ctx:
        held = AttentionWeights(net, ctx)
        layer_norm_stats(net, "pa", net.x)
        xt_all = net.sbuf("pa_xt_all", [P, (B + 1) * S], F32, ctx)
        neg_gate_all = net.sbuf("pa_neg_gate_all", [P, NT + TB, KV], F32, ctx)
        gate_all = net.sbuf("pa_gate_all", [GATE_ROWS, (B + 1) * S], BF16, ctx)
        gate_sums(net, held, xt_all, neg_gate_all, gate_all)
        attend(net, held, xt_all, neg_gate_all, gate_all)


class AttentionWeights:

    def __init__(self, net, ctx):
        sb = lambda n, s: net.sbuf(f"pa_{n}", s, F32, ctx)
        self.w_gate = sb("w_gate", [P, KV])
        self.w_g = sb("w_group", [P, KV, GROUP_W])
        self.w_proj = sb("w_proj", [P, KV, D])
        self.ln_w = sb("ln_w", [P, 1])
        self.rope_c = sb("rope_c", [P, TB, ROPE_W])
        self.rope_s = sb("rope_s", [P, TB, ROPE_W])
        self.select = sb("select", [GATE_ROWS, KV, P])
        self.gate_loaded, self.loaded = net.sem("pa_gate_w_loaded", ctx), net.sem("pa_w_loaded", ctx)
        start_loads(net, [(self.w_gate, "w_gate")], self.gate_loaded)
        loads = [(self.w_g, "w_group"), (self.w_proj, "w_proj"), (self.ln_w, "ln_w"),
                 (self.rope_c, "rope_c"), (self.rope_s, "rope_s"), (self.select, "select")]
        self.to_load = 16 * len(loads)
        start_loads(net, loads, self.loaded)


def gate_sums(net, held, xt_all, neg_gate_all, gate_all):
    nc = net.nc
    with ExitStack() as ctx:
        sb = lambda n, s, d=F32: net.sbuf(f"pg_{n}", s, d, ctx)
        gate = sb("gate", [P, NT, KV])
        meet_tokens(net, "pg", KV, gate, held.w_gate, None, held.gate_loaded, kept=xt_all)
        e = sb("e", [P, NT, KV])
        up_to = sb("up_to", [P, P])
        ones = sb("ones", [P, P])
        carry = sb("carry", [P, B, TB, KV])
        total = sb("total", [P, B, TB, KV])
        sums = sb("sums", [P, NT, KV])
        sum_ps = net.psum("pg_sum_ps", [P, 2, NT * KV], ctx)
        parts = sb("parts", [P, NT, GATE_ROWS])
        rest = sb("rest", [P, NT, KV])
        part_b = sb("part_b", [P, NT, KV], BF16)
        row_ps = [net.psum(f"pg_row_ps{u}", [GATE_ROWS, S], ctx) for u in range(2)]
        made, step, exp_in, exp_done, ln_done, log_ready = (net.sem(f"pg_{n}", ctx) for n in
                                                            ("made", "step", "exp_in", "exp_done", "ln_done", "log_ready"))
        summed, sums_ready, row_turned, row_kept = (net.sem(f"pg_{n}", ctx) for n in
                                                    ("summed", "sums_ready", "row_turned", "row_kept"))
        with nc.Block() as block:
            @block.gpsimd
            def _(pool):
                link = Chain(pool, made)
                link(pool.memset(ones[:, :], 1.0))
                link(pool.affine_select(out=up_to[:, :], in_=ones[:, :], compare_op=ALU.is_ge, fill=0.0,
                                        base=0, pattern=[[1, P]], channel_multiplier=-1))
                link(pool.memset(carry[:, :, 0, :], 0.0))
                link(pool.memset(xt_all[:, B * S:], 0.0))
                link(pool.memset(neg_gate_all[:, NT:, :], 0.0))
                link(pool.memset(gate_all[:, B * S:], 0.0))
                link(pool.memset(parts[:, :, :], 0.0))

            @block.scalar
            def _(act):
                act.wait_ge(exp_in, 1)
                act.activation(e[:, :, :], e[:, :, :], ACT.Exp).then_inc(exp_done, 1)
                act.wait_ge(exp_done, 1)
                act.activation(e[:, :, :], e[:, :, :], ACT.Ln, bias=ones[:, 0:1]).then_inc(ln_done, 1)
                for b in range(B):
                    act.wait_ge(row_turned, b + 1)
                    act.activation(gate_all[:, b * S:(b + 1) * S], row_ps[b % 2][:, :], ACT.Copy).then_inc(row_kept, 1)

            @block.vector
            def _(dve):
                link = Chain(dve, step)
                dve.wait_ge(made, 7)
                link(dve.tensor_scalar(gate[:, :, :], gate[:, :, :], GATE_BIAS, None, ALU.add))
                dve.scalar_tensor_tensor(out=e[:, :, :], in0=gate[:, :, :], scalar=-1.0, in1=gate[:, :, :],
                                         op0=ALU.mult, op1=ALU.min).then_inc(exp_in, 1)
                dve.wait_ge(ln_done, 1)
                dve.scalar_tensor_tensor(out=gate[:, :, :], in0=gate[:, :, :], scalar=0.0, in1=e[:, :, :],
                                         op0=ALU.min, op1=ALU.subtract).then_inc(log_ready, 1)
                dve.wait_ge(summed, 1)
                link(dve.tensor_copy(total[:, :, :, :].rearrange("p b t h -> p (b t h)"), sum_ps[:, 1, :]))
                for t in range(1, TB):
                    link(dve.tensor_tensor(carry[:, :, t, :], carry[:, :, t - 1, :], total[:, :, t - 1, :], ALU.add))
                flat_sums = sums[:, :, :].rearrange("p t h -> p (t h)")
                link(dve.tensor_tensor(flat_sums, carry[:, :, :, :].rearrange("p b t h -> p (b t h)"),
                                       sum_ps[:, 0, :], ALU.add))
                link(dve.tensor_copy(rest[:, :, :], sums[:, :, :]))
                for z in range(GATE_PARTS):
                    part = parts[:, :, z * GATE_PART:z * GATE_PART + KV]
                    link(dve.tensor_copy(part_b[:, :, :], rest[:, :, :]))
                    link(dve.tensor_copy(part, part_b[:, :, :]))
                    link(dve.tensor_tensor(rest[:, :, :], rest[:, :, :], part, ALU.subtract))
                dve.sem_inc(sums_ready, 1)
                link(dve.tensor_scalar(neg_gate_all[:, 0:NT, :], sums[:, :, :], -1.0, None, ALU.mult))

            @block.tensor
            def _(pe):
                pe.wait_ge(made, 7)
                pe.wait_ge(log_ready, 1)
                logs = gate[:, :, :].rearrange("p t h -> p (t h)")
                pe.matmul(sum_ps[:, 0, :], up_to[:, :], logs, start=True, stop=True)
                pe.matmul(sum_ps[:, 1, :], ones[:, :], logs, start=True, stop=True,
                          skip_group_check=True).then_inc(summed, 1)
                pe.wait_ge(sums_ready, 1)
                for b in range(B):
                    if b >= 2:
                        pe.wait_ge(row_kept, b - 1)
                    for t in range(TB):
                        last = pe.transpose(row_ps[b % 2][:, t * P:(t + 1) * P], parts[:, b * TB + t, :], net.ident[:, :])
                    last.then_inc(row_turned, 1)


def attend(net, held, xt_all, neg_gate_all, gate_all):
    nc, dram = net.nc, net.dram
    with ExitStack() as ctx:
        sb = lambda n, s, d=F32: net.sbuf(f"pa_{n}", s, d, ctx)
        v_mean = sb("v_mean", [P, KV])
        select_b = sb("select_b", [GATE_ROWS, KV, P], BF16)
        ident_b = sb("ident_b", [P, P], BF16)
        mask_b = sb("mask_b", [P, P], BF16)
        score_min = sb("score_min", [P, 1])
        xt = sb("xt", [P, S])
        gate_row = sb("gate_row", [GATE_ROWS, S], BF16)
        neg_gate = sb("neg_gate", [P, TB, KV])
        rope_a = sb("rope_a", [P, TB, QW])
        rope_b = sb("rope_b", [P, TB, QW])
        k_a, k_b = sb("k_a", [P, TB, KW]), sb("k_b", [P, TB, KW])
        qk = [sb(f"qk{u}", [P, TB, QW + 2 * KW]) for u in range(2)]
        q_t = [sb(f"q_t{u}", [P, RATIO, S], F32R) for u in range(2)]
        k_t = [sb(f"k_t{u}", [P, 2, S], F32R) for u in range(2)]
        kv = [sb(f"kv{u}", [P, TB, KW + HD + 1]) for u in range(2)]
        v = [both[:, :, KW:] for both in kv]
        decay = [sb(f"decay{u}", [P, SCORE_W]) for u in range(2)]
        a = [sb(f"a{u}", [P, SCORE_W]) for u in range(2)]
        top = sb("top", [P, S])
        top_row = sb("top_row", [P, TB])
        den = sb("den", [P, TB])
        y = [sb(f"y{u}", [P, TB, RATIO, HD]) for u in range(2)]
        y_sq = sb("y_sq", [P, TB, HD])
        sq_sum = [sb(f"sq_sum{u}", [P, TB, RATIO]) for u in range(2)]
        y_rstd = [sb(f"y_rstd{u}", [P, TB, RATIO]) for u in range(2)]
        y_t = sb("y_t", [P, KV, S])
        minus_half = sb("minus_half", [P, TB, RATIO])
        head_eps = sb("head_eps", [P, TB, RATIO])
        s_ps = net.psum("pa_s_ps", [P, 3 * S], ctx)
        p_ps = net.psum("pa_p_ps", [P, TB, GROUP_W], ctx)
        o_ps = net.psum("pa_o_ps", [P, S], ctx)
        t_ps = net.psum("pa_t_ps", [P, S], ctx)
        g_ps = net.psum("pa_g_ps", [P, S], ctx)
        o_view = o_ps[:, 0:TB * (HD + 1)].rearrange("p (t d) -> p t d", t=TB)
        turned_ps = p_ps[:, :, :].rearrange("p (z t) w -> p z (t w)", z=2)
        w_g, w_proj, ln_w = held.w_g, held.w_proj, held.ln_w
        rope_c, rope_s, select = held.rope_c, held.rope_s, held.select
        made, prepared = (net.sem(f"pa_{n}", ctx) for n in ("made", "prepared"))

        with nc.Block() as block:
            @block.gpsimd
            def _(pool):
                link = Chain(pool, made)
                link(pool.memset(score_min[:, :], SCORE_SCALE * SCORE_MIN))
                for u in range(2):
                    link(pool.memset(v[u][:, :, HD:], 1.0))
                link(pool.memset(minus_half[:, :, :], -0.5))
                link(pool.memset(head_eps[:, :, :], HD * HEAD_EPS))
                link(pool.memset(mask_b[:, :], 0.0))
                link(pool.affine_select(out=mask_b[:, :], in_=mask_b[:, :], compare_op=ALU.is_ge, fill=MASKED,
                                        base=0, pattern=[[1, P]], channel_multiplier=-1))

            @block.vector
            def _(dve):
                link = Chain(dve, prepared)
                link(dve.tensor_copy(ident_b[:, :], net.ident[:, :]))
                dve.wait_ge(held.loaded, held.to_load)
                values = w_g[:, :, ROPE_W:]
                link(dve.tensor_reduce(v_mean[:, :], values, AX.X, ALU.add))
                link(dve.tensor_scalar(v_mean[:, :], v_mean[:, :], 1.0 / HD, None, ALU.mult))
                link(dve.tensor_tensor(values, values, v_mean[:, :].unsqueeze(2).broadcast_to([P, KV, HD]), ALU.subtract))
                link(dve.tensor_copy(select_b[:, :, :], select[:, :, :]))
                link(dve.tensor_scalar(w_proj[:, :, :], w_proj[:, :, :], ln_w[:, 0:1], HD ** 0.5, ALU.mult, ALU.mult))

        by_sequence = "xt_set gates_set out_ready added "
        by_head = ("projected rope_ab roped k_products k_rotated kv_ready q_turned q_rounded k_turned k_rounded k_ready spread decay_off masked "
                   "decay_ready eps_added rstd_ready y_ready y_turned y_copied ")
        by_query = "scored_first scored squared_first squared weighed topped_step topped top_turned top_read valued den_step den_ready y_raw y_squared sq_summed"
        c = net.counters(by_sequence + by_head + by_query, "pa", ctx)

        def heads(b, g):
            return b * KV + g

        def queries(b, g, u=0):
            return b * (KV * RATIO) + (g * RATIO + u)

        with nc.Block() as block:
            @block.vector
            def _(dve):
                def next_tokens(b):
                    c["projected"].wait(dve, heads(b, 0))
                    c["xt_set"].by(dve.tensor_copy(xt[:, :], xt_all[:, bass.ds(b * S, S)]))

                def next_gates(b):
                    c["decay_ready"].wait(dve, heads(b, 0))
                    dve.tensor_copy(neg_gate[:, :, :], neg_gate_all[:, bass.ds(b * TB, TB), :])
                    c["gates_set"].by(dve.tensor_copy(gate_row[:, :], gate_all[:, bass.ds(b * S, S)]))

                def rope(b, g):
                    c["projected"].wait(dve, heads(b, g) + 1)
                    c["kv_ready"].wait(dve, heads(b, g) + 1)
                    c["roped"].wait(dve, heads(b, g))
                    pairs = lambda ap: ap.rearrange("p t (h two) -> p t h two", two=2)
                    dve.tensor_tensor(rope_a[:, :, :], p_ps[:, :, 0:QW], rope_c[:, :, 0:QW], ALU.mult)
                    c["rope_ab"].by(dve.tensor_tensor(pairs(rope_b[:, :, :]), pairs(p_ps[:, :, 0:QW])[:, :, :, ::-1],
                                                      pairs(rope_s[:, :, 0:QW]), ALU.mult))

                def rest_of_qk(b, g):
                    c["q_rounded"].wait(dve, heads(b, g) + 1)
                    for u in range(RATIO):
                        rows, others = slice(u * HD, (u + 1) * HD), slice((1 - u) * HD, (2 - u) * HD)
                        dve.tensor_tensor(q_t[g % 2][others, u, :], turned_ps[rows, 0, :], q_t[g % 2][rows, u, :],
                                          ALU.subtract)
                    c["k_rounded"].wait(dve, heads(b, g) + 1)
                    c["k_ready"].by(dve.tensor_tensor(k_t[g % 2][:, 1, :], turned_ps[:, 1, :], k_t[g % 2][:, 0, :],
                                                      ALU.subtract))

                def weigh(b, g, u):
                    c["squared_first"].wait(dve, queries(b, g, u) + 1)
                    c["decay_ready"].wait(dve, heads(b, g) + 1)
                    dve.tensor_tensor(a[u][:, 0:S], a[u][:, 0:S], decay[g % 2][:, 0:S], ALU.mult)
                    c["squared"].wait(dve, queries(b, g, u) + 1)
                    c["weighed"].by(dve.tensor_tensor(a[u][:, S:], a[u][:, S:], decay[g % 2][:, S:], ALU.mult))

                def largest(b, g, u):
                    w = queries(b, g, u)
                    c["weighed"].wait(dve, w + 1)
                    c["top_turned"].wait(dve, w)
                    at = lambda i: a[u][:, block_at(i, i):block_at(i, i) + (TB - i) * P]
                    c["topped_step"].by(dve.tensor_tensor(top[:, P:], a[u][:, P:S], at(1), ALU.max))
                    steps = b * (2 * KV * RATIO) + 2 * (g * RATIO + u)
                    c["topped_step"].wait(dve, steps + 1)
                    c["topped_step"].by(dve.tensor_tensor(top[:, 2 * P:], top[:, 2 * P:], at(2), ALU.max))
                    c["topped_step"].wait(dve, steps + 2)
                    c["topped"].by(dve.tensor_tensor(top[:, 3 * P:], top[:, 3 * P:], at(3), ALU.max))

                def divide(b, g, u):
                    w = queries(b, g, u)
                    c["top_turned"].wait(dve, w + 1)
                    c["top_read"].by(dve.tensor_reduce(top_row[:, :], t_ps[:, :].rearrange("p (t s) -> p t s", t=TB),
                                                       AX.X, ALU.max))
                    c["top_read"].wait(dve, w + 1)
                    c["valued"].wait(dve, w + 1)
                    c["den_step"].by(dve.scalar_tensor_tensor(out=den[:, :], in0=top_row[:, :], scalar=DEN_EPS,
                                                              in1=o_view[:, :, HD], op0=ALU.mult, op1=ALU.add))
                    c["den_step"].wait(dve, w + 1)
                    c["den_ready"].by(dve.reciprocal(den[:, :], den[:, :]))
                    c["den_ready"].wait(dve, w + 1)
                    c["y_turned"].wait(dve, heads(b, g) - 1)
                    c["y_raw"].by(dve.tensor_tensor(y[g % 2][:, :, u, :], o_view[:, :, 0:HD],
                                                    den[:, :].unsqueeze(2).broadcast_to([P, TB, HD]), ALU.mult))

                def sum_squares(b, g, u):
                    c["y_squared"].wait(dve, queries(b, g, u) + 1)
                    c["rstd_ready"].wait(dve, heads(b, g) - 1)
                    c["sq_summed"].by(dve.tensor_reduce(sq_sum[g % 2][:, :, u], y_sq[:, :, :], AX.X, ALU.add))

                next_tokens(0)
                next_gates(0)
                rope(0, 0)
                rest_of_qk(0, 0)
                with dve.Fori(0, B) as b:
                    for g in range(KV):
                        weigh(b, g, 0)
                        if g >= 1:
                            sum_squares(b, g - 1, 1)
                        rope(b, g + 1)
                        if g == KV - 2:
                            next_tokens(b + 1)
                        if g == KV - 1:
                            next_gates(b + 1)
                        largest(b, g, 0)
                        weigh(b, g, 1)
                        divide(b, g, 0)
                        largest(b, g, 1)
                        rest_of_qk(b, g + 1)
                        sum_squares(b, g, 0)
                        divide(b, g, 1)
                    sum_squares(b, KV - 1, 1)
                    c["out_ready"].wait(dve, b + 1)
                    rows = net.x[:, bass.ds(b * TB, TB), :]
                    c["added"].by(dve.tensor_tensor(rows, rows, g_ps[:, :].rearrange("p (t d) -> p t d", t=TB), ALU.add))

            @block.gpsimd
            def _(pool):
                def rotate_k(b, g):
                    c["kv_ready"].wait(pool, heads(b, g) + 1)
                    c["k_rotated"].wait(pool, heads(b, g))
                    c["k_turned"].wait(pool, heads(b, g) - 1)
                    pairs = lambda ap: ap.rearrange("p t (h two) -> p t h two", two=2)
                    k = kv[g % 2][:, :, 0:KW]
                    pool.tensor_tensor(k_a[:, :, :], k, rope_c[:, :, QW:], ALU.mult)
                    c["k_products"].by(pool.tensor_tensor(pairs(k_b[:, :, :]), pairs(k)[:, :, :, ::-1],
                                                          pairs(rope_s[:, :, QW:]), ALU.mult))
                    c["k_products"].wait(pool, heads(b, g) + 1)
                    for twice in range(2):
                        at = QW + twice * KW
                        last = pool.tensor_tensor(qk[g % 2][:, :, at:at + KW], k_a[:, :, :], k_b[:, :, :], ALU.add)
                    c["k_rotated"].by(last)

                def add_up_q(b, g):
                    c["rope_ab"].wait(pool, heads(b, g) + 1)
                    c["roped"].by(pool.tensor_tensor(qk[g % 2][:, :, 0:QW], rope_a[:, :, :], rope_b[:, :, :], ALU.add))

                def normalise(b, g):
                    c["sq_summed"].wait(pool, queries(b, g + 1))
                    c["y_ready"].wait(pool, heads(b, g) - 1)
                    c["eps_added"].by(pool.tensor_tensor(y_rstd[g % 2][:, :, :], sq_sum[g % 2][:, :, :],
                                                         head_eps[:, :, :], ALU.add))
                    c["eps_added"].wait(pool, heads(b, g) + 1)
                    c["rstd_ready"].by(pool.tensor_tensor(y_rstd[g % 2][:, :, :], y_rstd[g % 2][:, :, :],
                                                          minus_half[:, :, :], ALU.pow))
                    c["rstd_ready"].wait(pool, heads(b, g) + 1)
                    both = y[g % 2][:, :, :, :].rearrange("p t u d -> p (t u) d")
                    c["y_ready"].by(pool.tensor_tensor(both, both, y_rstd[g % 2][:, :, :].rearrange("p t u -> p (t u)")
                                                       .unsqueeze(2).broadcast_to([P, TB * RATIO, HD]), ALU.mult))

                rotate_k(0, 0)
                add_up_q(0, 0)
                with pool.Fori(0, B) as b:
                    for g in range(KV):
                        rotate_k(b, g + 1)
                        add_up_q(b, g + 1)
                        if g >= 1:
                            normalise(b, g - 1)
                    normalise(b, KV - 1)

            @block.scalar
            def _(act):
                def square(b, g, u):
                    w = queries(b, g, u)
                    c["scored_first"].wait(act, w + 1)
                    c["top_turned"].wait(act, w - 1)
                    c["valued"].wait(act, w - 1)
                    for part, cols in (("squared_first", slice(0, S)), ("squared", slice(S, SCORE_W))):
                        if part == "squared":
                            c["scored"].wait(act, w + 1)
                        c[part].by(act.activation(a[u][:, cols], s_ps[:, cols], ACT.Square, bias=score_min[:, 0:1],
                                                  scale=SCORE_SCALE * HD ** -0.5))

                def keep_kv(b, g):
                    c["projected"].wait(act, heads(b, g) + 1)
                    c["valued"].wait(act, queries(b, g - 1))
                    c["k_products"].wait(act, heads(b, g) - 1)
                    c["kv_ready"].by(act.activation(kv[g % 2][:, :, 0:KW + HD], p_ps[:, :, QW:], ACT.Copy))

                def decay_off(b, g):
                    c["spread"].wait(act, heads(b, g) + 1)
                    c["weighed"].wait(act, queries(b, g - 1))
                    for i in range(TB - 1):
                        at = block_at(i, i + 1)
                        last = act.activation(decay[g % 2][:, at:at + (TB - 1 - i) * P], g_ps[:, (i + 1) * P:],
                                              ACT.Exp, bias=neg_gate[:, i, g % KV:g % KV + 1])
                    c["decay_off"].by(last)

                def decay_diagonal(b, g):
                    c["masked"].wait(act, heads(b, g) + 1)
                    for i in range(TB):
                        at = block_at(i, i)
                        last = act.activation(decay[g % 2][:, at:at + P], g_ps[:, i * P:(i + 1) * P],
                                              ACT.Exp, bias=neg_gate[:, i, g % KV:g % KV + 1])
                    c["decay_ready"].by(last)

                def round_qk(b, g):
                    c["q_turned"].wait(act, heads(b, g) + 1)
                    c["scored"].wait(act, queries(b, g - 1))
                    for u in range(RATIO):
                        rows = slice(u * HD, (u + 1) * HD)
                        last = act.activation(q_t[g % 2][rows, u, :], turned_ps[rows, 0, :], ACT.Copy)
                    c["q_rounded"].by(last)
                    c["k_turned"].wait(act, heads(b, g) + 1)
                    c["k_rounded"].by(act.activation(k_t[g % 2][:, 0, :], turned_ps[:, 1, :], ACT.Copy))

                def square_y(b, g, u):
                    w = queries(b, g, u)
                    c["y_raw"].wait(act, w + 1)
                    c["sq_summed"].wait(act, w)
                    c["y_squared"].by(act.activation(y_sq[:, :, :], y[g % 2][:, :, u, :], ACT.Square))

                def copy_y(b, g, bank):
                    c["y_turned"].wait(act, heads(b, g) + 1)
                    c["out_ready"].wait(act, b)
                    c["y_copied"].by(act.activation(y_t[:, g, :], bank[:, :], ACT.Copy))

                keep_kv(0, 0)
                decay_off(0, 0)
                decay_diagonal(0, 0)
                round_qk(0, 0)
                with act.Fori(0, B) as b:
                    for g in range(KV):
                        square(b, g, 0)
                        if g >= 1:
                            square_y(b, g - 1, 1)
                        keep_kv(b, g + 1)
                        square(b, g, 1)
                        decay_off(b, g + 1)
                        decay_diagonal(b, g + 1)
                        round_qk(b, g + 1)
                        square_y(b, g, 0)
                        if g >= 1:
                            copy_y(b, g - 1, g_ps)
                    square_y(b, KV - 1, 1)
                    copy_y(b, KV - 1, t_ps)

            @block.tensor
            def _(pe):
                def project(b, g):
                    c["k_ready"].wait(pe, heads(b, g))
                    if g % KV == 0:
                        c["xt_set"].wait(pe, b + (g // KV + 1))
                    for t in range(TB):
                        last = pe.matmul(p_ps[:, t, :], xt[:, t * P:(t + 1) * P], w_g[:, g % KV, :],
                                         start=True, stop=True, skip_group_check=True)
                    c["projected"].by(last)

                def turn_qk(b, g):
                    c["roped"].wait(pe, heads(b, g) + 1)
                    for z, (kind, at) in enumerate((("q_turned", 0), ("k_turned", QW))):
                        for t in range(TB):
                            last = pe.transpose(turned_ps[:, z, t * P:(t + 1) * P], qk[g % 2][:, t, at:at + P],
                                                net.ident[:, :])
                        c[kind].by(last)

                def spread(b, g):
                    c["decay_ready"].wait(pe, heads(b, g))
                    c["y_copied"].wait(pe, heads(b, max(g - 2, 0)))
                    if g % KV == 0:
                        c["gates_set"].wait(pe, b + (g // KV + 1))
                    if g == 1:
                        c["added"].wait(pe, b)
                    pe_spread = pe.matmul(g_ps[:, :], select_b[:, g % KV, :], gate_row[:, :], start=True, stop=False,
                                          skip_group_check=True)
                    c["spread"].by(pe_spread)

                def mask(b, g):
                    c["decay_off"].wait(pe, heads(b, g) + 1)
                    c["masked"].by(pe.matmul(g_ps[:, :].rearrange("p (t s) -> p t s", t=TB), ident_b[:, :],
                                             mask_b[:, :].unsqueeze(1).broadcast_to([P, TB, P]), start=False, stop=True,
                                             skip_group_check=True))

                def score(b, g, u):
                    c["k_ready"].wait(pe, heads(b, g) + 1)
                    c["squared"].wait(pe, queries(b, g, u))
                    for i in range(TB):
                        at = block_at(i, i)
                        for z in range(2):
                            last = pe.matmul(s_ps[:, at:at + (TB - i) * P], k_t[g % 2][:, z, i * P:(i + 1) * P],
                                             q_t[g % 2][:, u, i * P:], start=z == 0, stop=z == 1,
                                             skip_group_check=True)
                        if i == 0:
                            c["scored_first"].by(last)
                    c["scored"].by(last)

                def value(b, g, u):
                    w = queries(b, g, u)
                    c["weighed"].wait(pe, w + 1)
                    c["kv_ready"].wait(pe, heads(b, g) + 1)
                    c["y_raw"].wait(pe, w)
                    for j in range(TB):
                        for i in range(j + 1):
                            at = block_at(i, j)
                            last = pe.matmul(o_view[:, j, :], a[u][:, at:at + P], v[g % 2][:, i, :],
                                             start=i == 0, stop=i == j, skip_group_check=True)
                    c["valued"].by(last)

                def turn_top(b, g, u):
                    w = queries(b, g, u)
                    c["topped"].wait(pe, w + 1)
                    c["top_read"].wait(pe, w)
                    c["y_copied"].wait(pe, heads(b, 0))
                    for t in range(TB):
                        src = a[u] if t == 0 else top
                        last = pe.transpose(t_ps[:, t * P:(t + 1) * P], src[:, t * P:(t + 1) * P], net.ident[:, :])
                    c["top_turned"].by(last)

                def turn_y(b, g, bank):
                    c["y_ready"].wait(pe, heads(b, g) + 1)
                    if bank is g_ps:
                        c["decay_ready"].wait(pe, heads(b, g + 2) + 1)
                    else:
                        c["top_read"].wait(pe, queries(b, g + 1))
                    for t in range(TB):
                        last = pe.transpose(bank[:, t * P:(t + 1) * P],
                                            y[g % 2][:, t, :, :].rearrange("p u d -> p (u d)"), net.ident[:, :])
                    c["y_turned"].by(last)

                def output(b, some):
                    c["y_copied"].wait(pe, heads(b, some[-1]) + 1)
                    for g in some:
                        for t in range(TB):
                            last = pe.matmul(g_ps[:, t * P:(t + 1) * P], y_t[:, g, t * P:(t + 1) * P], w_proj[:, g, :],
                                             start=g == 0 and t == 0, stop=g == KV - 1,
                                             skip_group_check=True)
                    return last

                project(0, 0)
                spread(0, 0)
                turn_qk(0, 0)
                mask(0, 0)
                score(0, 0, 0)
                with pe.Fori(0, B) as b:
                    for g in range(KV):
                        project(b, g + 1)
                        score(b, g, 1)
                        spread(b, g + 1)
                        value(b, g, 0)
                        turn_top(b, g, 0)
                        mask(b, g + 1)
                        turn_qk(b, g + 1)
                        value(b, g, 1)
                        if g >= 1:
                            turn_y(b, g - 1, g_ps)
                        turn_top(b, g, 1)
                        score(b, g + 1, 0)
                    c["decay_ready"].wait(pe, heads(b, KV) + 1)
                    output(b, range(KV - 1))
                    turn_y(b, KV - 1, t_ps)
                    c["out_ready"].by(output(b, [KV - 1]))


def program(nc, dram, out, stages):
    with ExitStack() as ctx:
        net = Net(nc, ctx, dram)
        with ExitStack() as first:
            load_inputs(net, first)
        stages(net)
        stored = net.sem("out_stored", ctx)
        with nc.Block() as block:
            @block.sync
            def _(sp):
                sp.dma_start(out.rearrange("b (t p) d -> p (b t) d", p=P), net.x[:, :, :]).then_inc(stored, 16)
                sp.wait_ge(stored, 16)


class Experts:

    def __init__(self, net, name, ctx):
        self.weights = net.sbuf(name, [P, E, EXPERT_W], F32, ctx)
        self.name, self.loaded = name, net.sem(f"{name}_loaded", ctx)

    def load(self, net):
        with net.nc.Block() as block:
            @block.scalar
            def _(act):
                act.dma_start(self.weights[:, :, :], net.dram[self.name]).then_inc(self.loaded, 16)


def whole_net(net):
    with ExitStack() as both:
        l1 = Experts(net, "l1_experts", both)
        with ExitStack() as ctx:
            l0 = Experts(net, "l0_experts", ctx)
            l0.load(net)
            mixture(net, "m0", 0, l0)
            l1.load(net)
            mamba(net)
            mixture(net, "m1", 0, l0)
        mixture(net, "m2", 1, l1)
        power_attention(net)
        mixture(net, "m3", 1, l1)


def rope_tables():
    div = (2.0 * np.pi / float(S) ** (np.arange(0, HD, 2, dtype=np.float32) / HD)).astype(np.float32)
    angle = (np.arange(S, dtype=np.float32)[:, None] * div[None, :]).astype(np.float64)
    cos = np.repeat(np.cos(angle), 2, 1)
    sin = np.repeat(np.sin(angle), 2, 1) * np.tile([-1.0, 1.0], HD // 2)
    place = lambda z: np.tile(z, (1, RATIO + 1)).reshape(TB, P, ROPE_W).transpose(1, 0, 2).astype(np.float32)
    return place(cos), place(sin)


def lay_out(i):
    i = {k: np.asarray(v) for k, v in i.items()}

    def experts(w1, b1, w2, b2):
        out = np.empty((P, E, EXPERT_W), np.float32)
        out[:, :, W1_AT:W2_AT] = w1.transpose(1, 0, 2)
        out[:, :, W2_AT:B2_AT] = w2.reshape(E, HC, P, D).transpose(2, 0, 1, 3).reshape(P, E, HC * D)
        out[:, :, B2_AT:B1_AT] = b2[None]
        out[:, :, B1_AT:] = b1.reshape(E, HC, P).transpose(2, 0, 1)
        return out

    def rows(v):
        return np.ascontiguousarray(np.broadcast_to(v, (P,) + v.shape))

    a = {"x": i["L0_attn_x"].reshape(N, D)}
    a["l0_experts"] = experts(i["L0_ffn_W1"], i["L0_ffn_b1"], i["L0_ffn_W2"], i["L0_ffn_b2"])
    a["l1_experts"] = experts(i["L1_ffn_w1"], i["L1_ffn_b1"], i["L1_ffn_w2"], i["L1_ffn_b2"])
    a["l0_shared_w"] = np.concatenate([i["L0_ffn_shared_W"], i["L0_ffn_gate_W"]], 1)
    a["l0_shared_b"] = rows(np.concatenate([i["L0_ffn_shared_b"], np.zeros(E, np.float32)]))
    a["l1_shared_w"] = np.ascontiguousarray(i["L1_ffn_router_w"].T)
    a["l1_shared_b"] = rows(np.zeros(E, np.float32))
    a["w_in"] = i["L0_attn_w_in"]
    a["w_out"] = i["L0_attn_w_out"].reshape(IC, P, D).transpose(1, 0, 2)
    a["w_b"] = i["L0_attn_w_B"].reshape(IC, P, DS).transpose(1, 0, 2)
    a["w_c"] = i["L0_attn_w_C"]
    a["conv_w"] = i["L0_attn_conv_w"].reshape(IC, P, DC).transpose(1, 0, 2)
    a["conv_b"] = i["L0_attn_conv_b"].reshape(IC, P).T
    w = i["L1_attn_w_attn"]
    q, k, v = np.split(w[:, :2048], [1024, 1536], 1)
    a["w_group"] = np.concatenate([q.reshape(D, KV, QW), k.reshape(D, KV, HD), v.reshape(D, KV, HD)], 2)
    a["w_gate"] = w[:, 2048:]
    a["w_proj"] = i["L1_attn_w_proj"].reshape(KV, P, D).transpose(1, 0, 2)
    a["ln_w"] = np.tile(i["L1_attn_ln_w"], RATIO)[:, None]
    a["rope_c"], a["rope_s"] = rope_tables()
    select = np.zeros((GATE_PARTS, GATE_PART, KV, P), np.float32)
    select[:, :KV] = np.eye(KV, dtype=np.float32)[None, :, :, None]
    a["select"] = select.reshape(GATE_ROWS, KV, P)
    a["l0_norm_w"] = rows(np.stack([i["L0_ffn_gamma"], i["L0_ffn_beta"]]))
    return a


def build(nc, arrays):
    dram = {n: nc.dram_tensor(f"in_{n}_dram", v.shape, F32, kind="ExternalInput").ap() for n, v in arrays.items()}
    out = nc.dram_tensor("out_dram", (B, S, D), F32, kind="ExternalOutput").ap()
    program(nc, dram, out, whole_net)


def kernel(**inputs):
    import concourse.bacc as _bacc
    from concourse.bass_utils import run_bass_kernel_spmd as _run

    nc = _bacc.Bacc("TRN2", target_bir_lowering=False, num_devices=1)
    arrays = {n: np.ascontiguousarray(v) for n, v in lay_out(inputs).items()}
    build(nc, arrays)
    r = _run(nc, [{f"in_{n}_dram": v for n, v in arrays.items()}], core_ids=[0])
    return r.results[0]["out_dram"]
```
